# Optimizing a Trainium2 kernel written in Bass

```python
import numpy as np
import jax
import jax.numpy as jnp

def _softmax(x, axis=-1):
    return jax.nn.softmax(x, axis=axis)

def _gelu(x):
    return jax.nn.gelu(x, approximate=True)

def _silu(x):
    return jax.nn.silu(x)

def _sigmoid(x):
    return jax.nn.sigmoid(x)

def _layernorm(x, axis=-1, eps=1e-05):
    m = jnp.mean(x, axis=axis, keepdims=True)
    v = jnp.var(x, axis=axis, keepdims=True)
    return (x - m) / jnp.sqrt(v + eps)

def _scatter_add(tgt, idx, src, axis=0):
    return tgt.at[idx].add(src)

def _segment_sum(src, seg, n):
    return jax.ops.segment_sum(src, seg, n)
kernel_name = 'mk_recurrent_d1_jaxref_r4_1a93d0'

def setup_inputs(seed: int=0):
    np.random.seed(seed)
    _w = jnp.asarray

    def _L0_attn_setup():
        import jax, jax.numpy as jnp
        import numpy as np
        B, S, D = (2, 512, 256)
        H, DH = (16, 64)
        DQL, DKVL = (128, 128)
        DR = 64
        TOPK = 64
        LN_EPS = 1e-05
        ROPE_BASE = 10000.0

        def _rope_tables(seq_len, dim):
            inv_freq = 1.0 / ROPE_BASE ** (np.arange(0, dim, 2, dtype=np.float32) / dim)
            t = np.arange(seq_len, dtype=np.float32)
            freqs = np.outer(t, inv_freq)
            cos = np.concatenate([np.cos(freqs), np.cos(freqs)], -1)[:, ::2]
            sin = np.concatenate([np.sin(freqs), np.sin(freqs)], -1)[:, ::2]
            return (jnp.asarray(cos), jnp.asarray(sin))

        def _apply_rope_subspace(x, d_rope):
            s = x.shape[-2]
            cos, sin = _rope_tables(s, d_rope)
            xr, xp = (x[..., :d_rope], x[..., d_rope:])
            e, o = (xr[..., 0::2], xr[..., 1::2])
            rot = jnp.stack([e * cos - o * sin, e * sin + o * cos], axis=-1).reshape(xr.shape)
            return jnp.concatenate([rot, xp], axis=-1)

        def _reference_tuple_inner(x, w_down_q, w_down_kv, w_up_q, w_up_k, w_up_v, w_out, ln_scale, ln_bias):
            b, s, d = x.shape
            residual = x
            mu = jnp.mean(x, axis=-1, keepdims=True)
            var = jnp.mean((x - mu) ** 2, axis=-1, keepdims=True)
            h = (x - mu) * jax.lax.rsqrt(var + LN_EPS) * ln_scale + ln_bias
            c_q = h @ w_down_q.T
            c_kv = h @ w_down_kv.T
            q = (c_q @ w_up_q.T).reshape(b, s, H, DH).transpose(0, 2, 1, 3)
            k = (c_kv @ w_up_k.T).reshape(b, s, H, DH).transpose(0, 2, 1, 3)
            v = (c_kv @ w_up_v.T).reshape(b, s, H, DH).transpose(0, 2, 1, 3)
            q = _apply_rope_subspace(q, DR)
            k = _apply_rope_subspace(k, DR)
            scale = 1.0 / np.sqrt(DH).astype(np.float32)
            scores = jnp.einsum('bhqd,bhkd->bhqk', q, k) * scale
            _, indices = jax.lax.top_k(scores, min(TOPK, s))
            attn = jax.nn.softmax(scores, axis=-1)
            out = jnp.einsum('bhqk,bhkd->bhqd', attn, v)
            out = out.transpose(0, 2, 1, 3).reshape(b, s, H * DH)
            out = out @ w_out.T + residual
            return (out, indices.astype(jnp.int64))
        key = jax.random.key(seed)
        ks = jax.random.split(key, 7)
        init = lambda k, shape: jax.random.normal(k, shape, jnp.float32) * 0.02
        return {'x': jax.random.normal(ks[0], (B, S, D), jnp.float32), 'w_down_q': init(ks[1], (DQL, D)), 'w_down_kv': init(ks[2], (DKVL, D)), 'w_up_q': init(ks[3], (H * DH, DQL)), 'w_up_k': init(ks[4], (H * DH, DKVL)), 'w_up_v': init(ks[5], (H * DH, DKVL)), 'w_out': init(ks[6], (D, H * DH)), 'ln_scale': jnp.ones((D,), jnp.float32), 'ln_bias': jnp.zeros((D,), jnp.float32)}
    _L0_attn_in = _L0_attn_setup()

    def _L0_ffn_setup():
        import jax, jax.numpy as jnp
        import numpy as np
        NUM_EXPERTS = 8
        TOP_K = 2
        CAP_RATIO = 1.25
        INIT_STD = 0.02
        key = jax.random.key(seed)
        k1, k2, k3, k4 = jax.random.split(key, 4)
        B, T, H, F = (4, 512, 256, 1024)
        x = jax.random.normal(k1, (B, T, H), jnp.float32)
        router_w = jax.random.normal(k2, (NUM_EXPERTS, H), jnp.float32) * INIT_STD
        w1 = jax.random.normal(k3, (NUM_EXPERTS, H, F), jnp.float32) * INIT_STD
        w2 = jax.random.normal(k4, (NUM_EXPERTS, F, H), jnp.float32) * INIT_STD
        return {'x': x, 'router_w': router_w, 'w1': w1, 'w2': w2}
    _L0_ffn_in = _L0_ffn_setup()
    _d = {'L0_attn_x': _L0_attn_in['x'], 'L0_attn_w_down_q': _L0_attn_in['w_down_q'], 'L0_attn_w_down_kv': _L0_attn_in['w_down_kv'], 'L0_attn_w_up_q': _L0_attn_in['w_up_q'], 'L0_attn_w_up_k': _L0_attn_in['w_up_k'], 'L0_attn_w_up_v': _L0_attn_in['w_up_v'], 'L0_attn_w_out': _L0_attn_in['w_out'], 'L0_attn_ln_scale': _L0_attn_in['ln_scale'], 'L0_attn_ln_bias': _L0_attn_in['ln_bias'], 'L0_ffn_router_w': _L0_ffn_in['router_w'], 'L0_ffn_w1': _L0_ffn_in['w1'], 'L0_ffn_w2': _L0_ffn_in['w2']}
    _x0 = _d['L0_attn_x']
    _d['L0_attn_x'] = jax.random.normal(jax.random.fold_in(jax.random.key(seed), 1), (8, 1024, 256), dtype=_x0.dtype)
    del _x0
    return _d

def reference(L0_attn_x, L0_attn_w_down_q, L0_attn_w_down_kv, L0_attn_w_up_q, L0_attn_w_up_k, L0_attn_w_up_v, L0_attn_w_out, L0_attn_ln_scale, L0_attn_ln_bias, L0_ffn_router_w, L0_ffn_w1, L0_ffn_w2):

    def _L0_attn_ref(x, w_down_q, w_down_kv, w_up_q, w_up_k, w_up_v, w_out, ln_scale, ln_bias):
        import jax, jax.numpy as jnp
        import numpy as np
        B, S, D = (2, 512, 256)
        H, DH = (16, 64)
        DQL, DKVL = (128, 128)
        DR = 64
        TOPK = 64
        LN_EPS = 1e-05
        ROPE_BASE = 10000.0

        def _rope_tables(seq_len, dim):
            inv_freq = 1.0 / ROPE_BASE ** (np.arange(0, dim, 2, dtype=np.float32) / dim)
            t = np.arange(seq_len, dtype=np.float32)
            freqs = np.outer(t, inv_freq)
            cos = np.concatenate([np.cos(freqs), np.cos(freqs)], -1)[:, ::2]
            sin = np.concatenate([np.sin(freqs), np.sin(freqs)], -1)[:, ::2]
            return (jnp.asarray(cos), jnp.asarray(sin))

        def _apply_rope_subspace(x, d_rope):
            s = x.shape[-2]
            cos, sin = _rope_tables(s, d_rope)
            xr, xp = (x[..., :d_rope], x[..., d_rope:])
            e, o = (xr[..., 0::2], xr[..., 1::2])
            rot = jnp.stack([e * cos - o * sin, e * sin + o * cos], axis=-1).reshape(xr.shape)
            return jnp.concatenate([rot, xp], axis=-1)

        def _reference_tuple_inner(x, w_down_q, w_down_kv, w_up_q, w_up_k, w_up_v, w_out, ln_scale, ln_bias):
            b, s, d = x.shape
            residual = x
            mu = jnp.mean(x, axis=-1, keepdims=True)
            var = jnp.mean((x - mu) ** 2, axis=-1, keepdims=True)
            h = (x - mu) * jax.lax.rsqrt(var + LN_EPS) * ln_scale + ln_bias
            c_q = h @ w_down_q.T
            c_kv = h @ w_down_kv.T
            q = (c_q @ w_up_q.T).reshape(b, s, H, DH).transpose(0, 2, 1, 3)
            k = (c_kv @ w_up_k.T).reshape(b, s, H, DH).transpose(0, 2, 1, 3)
            v = (c_kv @ w_up_v.T).reshape(b, s, H, DH).transpose(0, 2, 1, 3)
            q = _apply_rope_subspace(q, DR)
            k = _apply_rope_subspace(k, DR)
            scale = 1.0 / np.sqrt(DH).astype(np.float32)
            scores = jnp.einsum('bhqd,bhkd->bhqk', q, k) * scale
            _, indices = jax.lax.top_k(scores, min(TOPK, s))
            attn = jax.nn.softmax(scores, axis=-1)
            out = jnp.einsum('bhqk,bhkd->bhqd', attn, v)
            out = out.transpose(0, 2, 1, 3).reshape(b, s, H * DH)
            out = out @ w_out.T + residual
            return (out, indices.astype(jnp.int64))
        return _reference_tuple_inner(x, w_down_q, w_down_kv, w_up_q, w_up_k, w_up_v, w_out, ln_scale, ln_bias)[0]

    def _L0_ffn_ref(x, router_w, w1, w2):
        import jax, jax.numpy as jnp
        import numpy as np
        NUM_EXPERTS = 8
        TOP_K = 2
        CAP_RATIO = 1.25
        INIT_STD = 0.02
        B, T, H = x.shape
        E, K = (NUM_EXPERTS, TOP_K)
        xf = x.reshape(-1, H)
        N = xf.shape[0]
        P = N * K
        capacity = int(CAP_RATio * N * K / E) + 1 if False else int(CAP_RATIO * N * K / E) + 1
        logits = xf @ router_w.T
        probs = jax.nn.softmax(logits, axis=-1)
        k_probs, k_idx = jax.lax.top_k(probs, K)
        k_probs = k_probs / jnp.sum(k_probs, axis=-1, keepdims=True)
        flat_e = k_idx.reshape(-1)
        onehot = jax.nn.one_hot(flat_e, E, dtype=jnp.int32)
        rank = jnp.take_along_axis(jnp.cumsum(onehot, axis=0) - 1, flat_e[:, None], axis=1)[:, 0]
        keep = rank < capacity
        slot = jnp.minimum(rank, capacity - 1)
        token_id = jnp.arange(P) // K
        dispatched = jnp.where(keep[:, None], xf[token_id], 0.0)
        buf = jnp.zeros((E, capacity, H), x.dtype).at[flat_e, slot].add(dispatched)
        h = jax.nn.silu(jnp.einsum('ech,ehf->ecf', buf, w1))
        out_buf = jnp.einsum('ecf,efh->ech', h, w2)
        pair_out = out_buf[flat_e, slot] * keep[:, None].astype(x.dtype)
        combined = jnp.sum(pair_out.reshape(N, K, H) * k_probs[..., None], axis=1)
        return combined.reshape(B, T, H) + x
    x = L0_attn_x
    xn = _layernorm(x, axis=-1)
    s = _L0_attn_ref(xn, L0_attn_w_down_q, L0_attn_w_down_kv, L0_attn_w_up_q, L0_attn_w_up_k, L0_attn_w_up_v, L0_attn_w_out, L0_attn_ln_scale, L0_attn_ln_bias)
    g = _silu(_L0_ffn_ref(xn, L0_ffn_router_w, L0_ffn_w1, L0_ffn_w2))
    x = x + s * g
    return x

_drawn_inputs = setup_inputs


def setup_inputs(seed=0):
    import zlib

    import numpy as np

    out = dict(_drawn_inputs(seed))
    spreads = {'L0_attn_ln_scale': (1.0, 0.6), 'L0_attn_ln_bias': (0.0, 0.8)}
    factors = {'L0_attn_w_down_q': 8.0,
     'L0_attn_w_down_kv': 8.0,
     'L0_attn_w_up_q': 8.0,
     'L0_attn_w_up_k': 8.0,
     'L0_attn_w_up_v': 8.0,
     'L0_attn_w_out': 8.0}
    for name, (base, spread) in spreads.items():
        noise = np.random.default_rng([zlib.crc32(name.encode()), seed]).standard_normal(out[name].shape)
        drawn = base * np.exp(spread * noise) if base else spread * noise
        out[name] = jnp.asarray(drawn.astype(out[name].dtype))
    for name, factor in factors.items():
        out[name] = (out[name] * factor).astype(out[name].dtype)
    return out
```

```python
from contextlib import ExitStack

import numpy as np
import concourse.bass as bass
from concourse import mybir

F32, F32R, I32 = mybir.dt.float32, mybir.dt.float32r, mybir.dt.int32
ALU, ACT, AX = mybir.AluOpType, mybir.ActivationFunctionType, mybir.AxisListType

P = 128
NBATCH, S, D = 8, 1024, 256
H, DH, DL = 16, 64, 128
NE, FF = 8, 1024
NTOK = NBATCH * S
NT = NTOK // P
TB = S // P
KD = D // P
HALF = 512
NH2 = S // HALF
HP = H // 2
NPAIR = NBATCH * HP
KT = S // P
CAP = int(1.25 * NTOK * 2 / NE) + 1
SLOT_P = 122
SLOT_T = 21
CAPP = SLOT_P * SLOT_T
PART_T = 3
PARTS = SLOT_T // PART_T
PW = PART_T * SLOT_P
NF = FF // P
NSLOT = NE * CAPP
EPS = 1e-5
FAR = float(1 << 20)
SCALE = 1.0 / 8.0


class At:

    def __init__(self, base, off):
        self.base, self.off, self.u = base, off, off % 2

    def n(self, k=1, add=0):
        return self.base * (2 * k) + (self.off * k + add)

    def same(self, k, add=0):
        return self.base * k + ((self.off // 2) * k + add)

    def next(self, d):
        return At(self.base, self.off + d)


def wait(eng, sem, value):
    if not (isinstance(value, int) and value <= 0):
        eng.wait_ge(sem, value)


def wait_apart(eng, sem, value, own):
    wait(eng, sem, value)
    eng.sem_inc(own, 1)


class Phase:

    def __init__(self, nc, ctx, tag):
        self.nc, self.ctx, self.tag = nc, ctx, tag

    def sb(self, name, shape, dt=F32):
        return self.ctx.enter_context(self.nc.sbuf_tensor(f"{self.tag}_{name}", shape, dt))

    def ps(self, name, shape):
        return self.ctx.enter_context(self.nc.psum_tensor(f"{self.tag}_{name}", shape, F32))

    def sem(self, name):
        return self.ctx.enter_context(self.nc.semaphore(f"{self.tag}_{name}"))

    def block(self):
        return self.ctx.enter_context(self.nc.Block())


def project_phase(nc, io, scr, keep):
    with ExitStack() as ctx:
        ph = Phase(nc, ctx, "pj")
        sb, ps, sem = ph.sb, ph.ps, ph.sem
        xin = [sb(f"xin{u}", [P, TB, D]) for u in range(2)]
        xn = [sb(f"xn{u}", [P, TB, D]) for u in range(2)]
        h = sb("h", [P, TB, D])
        stats = sb("stats", [P, TB, 6])
        mv = sb("mv", [P, TB, 2])
        rstd, veps, minus_half = (sb(n, [P, TB]) for n in ("rstd", "veps", "minus_half"))
        xnT = sb("xnT", [P, KD, S])
        hT = sb("hT", [P, KD, S])
        csb = [sb(f"c{u}", [P, 2, S]) for u in range(2)]
        vsb = [sb(f"v{k}", [P, H * DH]) for k in range(4)]
        wd = sb("wd", [P, 2, KD, DL])
        wv = sb("wv", [DL, H * DH])
        rw = sb("rw", [P, KD, NE])
        lnp = sb("lnp", [P, KD, 2])
        pa = [ps(f"pa{k}", [P, S]) for k in range(2)]
        lg = ps("lg", [P, TB, NE])
        s_const, s_ln, s_pa, s_lgf, s_lgd = (sem(n) for n in ("const", "ln", "pa", "lgf", "lgd"))
        s_eps, s_apart, s_apart_v = sem("eps"), sem("apart"), sem("apart_v")
        s_x = [sem(f"x{u}") for u in range(2)]
        s_xs = [sem(f"xs{u}") for u in range(2)]
        s_cs = [sem(f"cs{u}") for u in range(2)]
        s_vs = [sem(f"vs{k}") for k in range(4)]
        s_act, s_dve = sem("act"), sem("dve")
        blk = ph.block()
        NCONST = 16 * 6
        ITEMS = 6 + TB

        @blk.sync
        def _(e):
            e.dma_start(keep["ident"][:, :], io["ident"]).then_inc(s_const, 16)
            e.dma_start(rw[:, :, :], io["rwT"].rearrange("(k p) e -> p k e", p=P)).then_inc(s_const, 16)
            e.dma_start(wd[:, 0, :, :], io["wdqT"].rearrange("(k p) m -> p k m", p=P)).then_inc(s_const, 16)
            e.dma_start(wd[:, 1, :, :], io["wdkvT"].rearrange("(k p) m -> p k m", p=P)).then_inc(s_const, 16)
            e.dma_start(wv[:, :], io["wvT"]).then_inc(s_const, 16)
            e.dma_start(lnp[:, :, :], io["lnp"]).then_inc(s_const, 16)
            for s in s_xs:
                e.sem_inc(s, 16)
            for s in s_cs:
                e.sem_inc(s, 32)
            for s in s_vs:
                e.sem_inc(s, 16)
            with e.Fori(0, NBATCH // 2) as it:
                for u in range(2):
                    a = At(it, u)
                    e.wait_ge(s_ln, a.n(8, 4))
                    e.dma_start(scr["xn"][a.n(), :, :].rearrange("(t p) d -> p t d", p=P), xn[u][:, :, :]).then_inc(s_xs[u], 16)
                    e.wait_ge(s_act, a.n(7, 4))
                    e.dma_start(scr["c"][a.n(), 0, :, :], csb[u][:, 0, :]).then_inc(s_cs[u], 16)
                    e.wait_ge(s_dve, a.n(7, 4))
                    e.dma_start(scr["c"][a.n(), 1, :, :], csb[u][:, 1, :]).then_inc(s_cs[u], 16)
                    for t in range(TB):
                        e.wait_ge((s_act, s_dve)[t % 2], a.n(7, 5 + t // 2))
                        e.dma_start(scr["v"][a.n(), :, :, t, :].rearrange("r p m -> p r m"),
                                    vsb[t % 4][:, :].rearrange("p (r m) -> p r m", r=HP)).then_inc(s_vs[t % 4], 16)
            for s in s_xs:
                e.wait_ge(s, 16 * (NBATCH // 2 + 1))
            for s in s_cs:
                e.wait_ge(s, 32 * (NBATCH // 2 + 1))
            for s in s_vs:
                e.wait_ge(s, 16 * (2 * NBATCH + 1))

        @blk.gpsimd
        def _(e):
            def load(a):
                e.dma_start(xin[a.u][:, :, :], io["x"][a.n(), :, :].rearrange("(t p) d -> p t d", p=P)).then_inc(s_x[a.u], 16)

            def deviations(a):
                for k in (0, 4):
                    wait_apart(e, s_ln, a.n(8, k + 2), s_apart)
                    e.tensor_scalar(veps[:, :], mv[:, :, 1], EPS, None, ALU.add).then_inc(s_eps, 1)
                    wait_apart(e, s_eps, a.n(2, k // 4 + 2), s_apart)
                    e.tensor_tensor(out=rstd[:, :], in0=veps[:, :], in1=minus_half[:, :], op=ALU.pow).then_inc(s_ln, 1)

            e.memset(minus_half[:, :], -0.5).then_inc(s_eps, 1)
            for u in range(2):
                load(At(0, u))
            for u in range(2):
                deviations(At(0, u))
            with e.Fori(1, NBATCH // 2) as it:
                for u in range(2):
                    a = At(it, u)
                    wait_apart(e, s_ln, a.n(8, -12), s_apart)
                    load(a)
                    deviations(a)

        @blk.vector
        def _(e):
            def norm_stats(src):
                for t in range(TB):
                    last = e.bn_stats(stats[:, t, :], src[:, t, :])
                last.then_inc(s_ln, 1)

            def norm_apply(a, k, src, dst):
                wait_apart(e, s_ln, a.n(8, k + 1), s_apart_v)
                for t in range(TB):
                    last = e.bn_aggr(mv[:, t, :], stats[:, t, :])
                last.then_inc(s_ln, 1)
                e.wait_ge(s_ln, a.n(8, k + 3))
                for t in range(TB):
                    last = e.tensor_scalar(dst[:, t, :], src[:, t, :], mv[:, t, 0:1], rstd[:, t:t + 1], ALU.subtract, ALU.mult)
                last.then_inc(s_ln, 1)

            def norms(a):
                u = a.u
                e.wait_ge(s_x[u], a.same(16, 16))
                norm_stats(xin[u])
                yield
                e.wait_ge(s_xs[u], a.same(16, 16))
                norm_apply(a, 0, xin[u], xn[u])
                yield
                e.wait_ge(s_ln, a.n(8, 4))
                norm_stats(xn[u])
                yield
                norm_apply(a, 4, xn[u], h)
                yield

            def evacuate(a, following):
                u = a.u
                e.wait_ge(s_pa, a.n(ITEMS, 2))
                e.tensor_copy(xnT[:, 1, :], pa[1][:, :]).then_inc(s_dve, 1)
                e.wait_ge(s_pa, a.n(ITEMS, 4))
                e.tensor_scalar(hT[:, 1, :], pa[1][:, :], lnp[:, 1, 0:1], lnp[:, 1, 1:2], ALU.mult, ALU.add).then_inc(s_dve, 1)
                e.wait_ge(s_lgf, a.n(1, 1))
                e.tensor_copy(keep["logits"][:, bass.ds(a.n(TB * NE), TB * NE)], lg[:, :, :].rearrange("p t e -> p (t e)")).then_inc(s_lgd, 1)
                e.wait_ge(s_pa, a.n(ITEMS, 6))
                e.wait_ge(s_cs[u], a.same(32, 32))
                e.tensor_copy(csb[u][:, 1, :], pa[1][:, :]).then_inc(s_dve, 1)
                for t in range(1, TB, 2):
                    if following:
                        next(following)
                    e.wait_ge(s_pa, a.n(ITEMS, 7 + t))
                    e.wait_ge(s_vs[t % 4], a.n(32, 16 + 16 * (t // 4)))
                    e.tensor_copy(vsb[t % 4][:, :], pa[1][:, :]).then_inc(s_dve, 1)

            e.sem_inc(s_dve, 1)
            e.sem_inc(s_lgd, 1)
            e.wait_ge(s_const, NCONST)
            for _ in norms(At(0, 0)):
                pass
            with e.Fori(0, NBATCH // 2 - 1) as it:
                for u in range(2):
                    evacuate(At(it, u), norms(At(it, u + 1)))
            evacuate(At(0, NBATCH - 2), norms(At(0, NBATCH - 1)))
            evacuate(At(0, NBATCH - 1), None)

        @blk.scalar
        def _(e):
            e.sem_inc(s_act, 1)
            e.wait_ge(s_const, NCONST)
            with e.Fori(0, NBATCH // 2) as it:
                for u in range(2):
                    a = At(it, u)
                    e.wait_ge(s_pa, a.n(ITEMS, 1))
                    e.activation(xnT[:, 0, :], pa[0][:, :], ACT.Copy).then_inc(s_act, 1)
                    e.wait_ge(s_pa, a.n(ITEMS, 3))
                    e.activation(hT[:, 0, :], pa[0][:, :], ACT.Identity, scale=lnp[:, 0, 0:1], bias=lnp[:, 0, 1:2]).then_inc(s_act, 1)
                    e.wait_ge(s_pa, a.n(ITEMS, 5))
                    e.wait_ge(s_cs[u], a.same(32, 32))
                    e.activation(csb[u][:, 0, :], pa[0][:, :], ACT.Copy).then_inc(s_act, 1)
                    for t in range(0, TB, 2):
                        e.wait_ge(s_pa, a.n(ITEMS, 7 + t))
                        e.wait_ge(s_vs[t % 4], a.n(32, 16 + 16 * (t // 4)))
                        e.activation(vsb[t % 4][:, :], pa[0][:, :], ACT.Copy).then_inc(s_act, 1)

        @blk.tensor
        def _(e):
            e.wait_ge(s_const, NCONST)
            with e.Fori(0, NBATCH // 2) as it:
                for u in range(2):
                    a = At(it, u)

                    def fill(k):
                        e.wait_ge((s_act, s_dve)[k % 2], a.n(7, 1 + k // 2))
                        return pa[k % 2]

                    for src, k0, ready in ((xn[u], 0, 4), (h, 2, 8)):
                        e.wait_ge(s_ln, a.n(8, ready))
                        for k in range(KD):
                            out = fill(k0 + k)
                            for t in range(TB):
                                mm = e.transpose(out[:, t * P:(t + 1) * P], src[:, t, k * P:(k + 1) * P], keep["ident"][:, :])
                            mm.then_inc(s_pa, 1)
                    e.wait_ge(s_act, a.n(7, 2))
                    e.wait_ge(s_dve, a.n(7, 2))
                    e.wait_ge(s_lgd, a.n(1, 1))
                    for t in range(TB):
                        for k in range(KD):
                            mm = e.matmul(lg[:, t, :], xnT[:, k, t * P:(t + 1) * P], rw[:, k, :], start=(k == 0), stop=(k == KD - 1))
                    mm.then_inc(s_lgf, 1)
                    e.wait_ge(s_act, a.n(7, 3))
                    e.wait_ge(s_dve, a.n(7, 3))
                    for j in range(2):
                        out = fill(4 + j)
                        for k in range(KD):
                            for n in range(NH2):
                                cols = slice(n * HALF, (n + 1) * HALF)
                                mm = e.matmul(out[:, cols], wd[:, j, k, :], hT[:, k, cols], start=(k == 0), stop=(k == KD - 1))
                        mm.then_inc(s_pa, 1)
                    e.wait_ge(s_dve, a.n(7, 4))
                    for t in range(TB):
                        out = fill(6 + t)
                        for n in range(NH2):
                            cols = slice(n * HALF, (n + 1) * HALF)
                            mm = e.matmul(out[:, cols], csb[u][:, 1, t * P:(t + 1) * P], wv[:, cols], start=True, stop=True)
                        mm.then_inc(s_pa, 1)


def route_phase(nc, io, scr, keep):
    with ExitStack() as ctx:
        ph = Phase(nc, ctx, "rt")
        sb, ps, sem = ph.sb, ph.ps, ph.sem
        C = NT * NE
        lg3 = keep["logits"][:, :].rearrange("p (t e) -> p t e", e=NE)
        rev, ebase, newe = sb("rev", [P, C]), sb("ebase", [P, C]), sb("newe", [P, C])
        tri, ones = sb("tri", [P, P]), sb("ones", [P, P])
        rev3, ebase3 = (x[:, :].rearrange("p (t e) -> p t e", e=NE) for x in (rev, ebase))

        def cube(name):
            return sb(name, [P, C])[:, :].rearrange("p (t e) -> p t e", e=NE)

        w, pick, second, both, rank, tmp = (cube(n) for n in ("w", "pick", "second", "both", "rank", "tmp"))
        oh = [cube("oh0"), cube("oh1")]
        tot, cum = sb("tot", [P, NE, NT]), sb("cum", [P, NE, NT])
        m = [sb(f"m{k}", [P, NT]) for k in range(2)]
        idx = sb("idx", [P, NT])
        dif, p2, den = (sb(n, [P, NT]) for n in ("dif", "p2", "den"))
        rk, pos, over, kept = (sb(n, [P, NT]) for n in ("rk", "pos", "over", "kept"))
        zero = sb("zero", [SLOT_P, NSLOT // SLOT_P], I32)
        pp, pt = ps("prefix", [P, C]), ps("total", [P, C])
        s_const, s_v, s_oh, s_mm, s_dif, s_exp, s_zero = (sem(n) for n in ("const", "v", "oh", "mm", "dif", "exp", "zero"))
        blk = ph.block()

        @blk.sync
        def _(e):
            e.dma_start(rev[:, :], io["rev"]).then_inc(s_const, 16)
            e.dma_start(ebase[:, :], io["ebase"]).then_inc(s_const, 16)
            e.dma_start(newe[:, :], io["newe"]).then_inc(s_const, 16)
            e.dma_start(tri[:, :], io["tri"]).then_inc(s_const, 16)
            e.dma_start(keep["tok"][:, :], io["tok"]).then_inc(s_const, 16)
            e.wait_ge(s_zero, 1)
            e.dma_start(scr["table"].rearrange("(p n) o -> p (n o)", p=SLOT_P), zero[:, :]).then_inc(s_const, 16)
            e.wait_ge(s_const, 96)

        @blk.gpsimd
        def _(e):
            e.memset(zero[:, :], 0).then_inc(s_zero, 1)

        @blk.scalar
        def _(e):
            e.wait_ge(s_dif, 1)
            e.activation(p2[:, :], dif[:, :], ACT.Exp).then_inc(s_exp, 1)

        @blk.tensor
        def _(e):
            e.wait_ge(s_const, 96)
            e.wait_ge(s_oh, 1)
            e.matmul(pp[:, :], tri[:, :], both.rearrange("p t e -> p (t e)"), start=True, stop=True)
            e.matmul(pt[:, :], ones[:, :], both.rearrange("p t e -> p (t e)"), start=True, stop=True).then_inc(s_mm, 1)

        @blk.vector
        def _(e):
            done = [0]

            def then(ins):
                done[0] += 1
                ins.then_inc(s_v, 1)
                e.wait_ge(s_v, done[0])

            def bc(x):
                return x[:, :].unsqueeze(2).broadcast_to((P, NT, NE))

            e.memset(ones[:, :], 1.0)
            e.wait_ge(s_const, 96)
            src = lg3
            for k in range(2):
                then(e.tensor_reduce(out=m[k][:, :], in_=src, axis=AX.X, op=ALU.max))
                then(e.tensor_tensor(out=pick, in0=src, in1=bc(m[k]), op=ALU.is_ge))
                then(e.tensor_tensor(out=w, in0=pick, in1=rev3, op=ALU.mult))
                then(e.tensor_reduce(out=idx[:, :], in_=w, axis=AX.X, op=ALU.max))
                then(e.tensor_tensor(out=oh[k], in0=rev3, in1=bc(idx), op=ALU.is_equal))
                if k == 0:
                    then(e.scalar_tensor_tensor(out=second, in0=oh[0], scalar=-3e38, in1=lg3, op0=ALU.mult, op1=ALU.add))
                    src = second
            e.tensor_tensor(out=both, in0=oh[0], in1=oh[1], op=ALU.add).then_inc(s_oh, 1)
            e.tensor_tensor(out=dif[:, :], in0=m[1][:, :], in1=m[0][:, :], op=ALU.subtract).then_inc(s_dif, 1)
            e.wait_ge(s_exp, 1)
            then(e.tensor_scalar(den[:, :], p2[:, :], 1.0, None, ALU.add))
            then(e.reciprocal(keep["gate"][:, :, 0], den[:, :]))
            then(e.tensor_tensor(out=keep["gate"][:, :, 1], in0=p2[:, :], in1=keep["gate"][:, :, 0], op=ALU.mult))
            e.wait_ge(s_mm, 1)
            then(e.tensor_copy(tot[:, :, :], pt[:, :].rearrange("p (t e) -> p e t", e=NE)))
            then(e.tensor_tensor_scan(cum[:, :, :].rearrange("p e t -> p (e t)"), newe[:, :], tot[:, :, :].rearrange("p e t -> p (e t)"), 0.0, ALU.mult, ALU.add))
            then(e.tensor_tensor(out=cum[:, :, :], in0=cum[:, :, :], in1=tot[:, :, :], op=ALU.subtract))
            then(e.tensor_tensor(out=rank, in0=pp[:, :].rearrange("p (t e) -> p t e", e=NE), in1=cum[:, :, :].rearrange("p e t -> p t e"), op=ALU.add))
            for k in range(2):
                then(e.tensor_tensor(out=tmp, in0=oh[k], in1=rank, op=ALU.mult))
                then(e.tensor_reduce(out=rk[:, :], in_=tmp, axis=AX.X, op=ALU.add))
                then(e.tensor_tensor(out=tmp, in0=oh[k], in1=ebase3, op=ALU.mult))
                then(e.tensor_reduce(out=pos[:, :], in_=tmp, axis=AX.X, op=ALU.add))
                then(e.tensor_scalar(over[:, :], rk[:, :], float(CAP), FAR, ALU.is_ge, ALU.mult))
                then(e.tensor_tensor(out=over[:, :], in0=over[:, :], in1=rk[:, :], op=ALU.add))
                then(e.tensor_tensor(out=keep["fill"][:, :, k], in0=over[:, :], in1=pos[:, :], op=ALU.add))
                then(e.tensor_scalar(kept[:, :], rk[:, :], float(CAP), None, ALU.is_lt))
                then(e.tensor_tensor(out=keep["gate"][:, :, k], in0=keep["gate"][:, :, k], in1=kept[:, :], op=ALU.mult))
                then(e.tensor_scalar(rk[:, :], rk[:, :], float(CAP - 1), None, ALU.min))
                then(e.tensor_tensor(out=keep["read"][:, :, k], in0=rk[:, :], in1=pos[:, :], op=ALU.add))


def attend_phase(nc, io, scr, keep):
    with ExitStack() as ctx:
        ph = Phase(nc, ctx, "at")
        sb, ps, sem = ph.sb, ph.ps, ph.sem
        NP = 8
        MAXES = 2 * KT
        FRONT = 4 + MAXES + 1
        TILES = 2 * KT
        LO, HI = slice(0, DH), slice(DH, P)
        rows = [LO, HI]
        other = [HI, LO]
        wqk = [sb(f"wqk{u}", [DL, 4, P]) for u in range(2)]
        c = [sb(f"c{u}", [DL, 2, S]) for u in range(2)]
        v = [sb(f"v{u}", [P, KT, P]) for u in range(2)]
        t1, t2 = sb("t1", [P, S]), sb("t2", [P, S])
        rot = [sb("rotq", [P, S]), sb("rotk", [P, S])]
        qa = [[sb(f"qa{u}{h}", [P, S], F32R) for h in range(2)] for u in range(2)]
        qb = [[sb(f"qb{u}{h}", [P, S], F32R) for h in range(2)] for u in range(2)]
        ka = [[sb(f"ka{u}{h}", [P, S], F32R) for h in range(2)] for u in range(2)]
        kb = [[sb(f"kb{u}{h}", [P, S], F32R) for h in range(2)] for u in range(2)]
        ex = [sb(f"ex{k}", [P, S]) for k in range(NP)]
        total = [[sb(f"sum{u}{h}", [P, S]) for h in range(2)] for u in range(2)]
        osb, den = sb("osb", [P, S]), sb("den", [P, S])
        oT = [sb(f"oT{u}", [P, S]) for u in range(2)]
        cos, sin = sb("cos", [P, S]), sb("sin", [P, S])
        ones = sb("ones", [P, DH])
        mx = sb("mx", [P, MAXES])
        mneg = sb("mneg", [MAXES, P], F32R)
        fill_i, tok_i = sb("fill_i", [P, 2], I32), sb("tok_i", [P, 1], I32)
        pst = [ps(f"st{k}", [P, S]) for k in range(2)]
        ppv, pfr = ps("pv", [P, S]), ps("fr", [P, S])
        s_const, s_init, s_apart = sem("const"), sem("init"), sem("apart")
        s_ldw = [sem(f"ldw{u}") for u in range(2)]
        s_ldv = [sem(f"ldv{u}") for u in range(2)]
        s_fr, s_frd = sem("fr"), sem("frd")
        s_rot, s_hi, s_lo = sem("rot"), sem("hi"), sem("lo")
        s_mrow = sem("mrow")
        s_st, s_exp, s_pv, s_sum = sem("st"), sem("exp"), sem("pvd"), sem("sumd")
        s_osb, s_denf, s_dend, s_rec, s_ot = sem("osb"), sem("denf"), sem("dend"), sem("rec"), sem("ot")
        s_store = [sem(f"store{u}") for u in range(2)]
        s_idx, s_scat = sem("idx"), sem("scat")
        blk = ph.block()
        NREC = 8

        def run(e, prologue, body, tail):
            prologue()
            body(At(0, 0), True)
            with e.Fori(0, NPAIR // 2 - 1) as it:
                for off in (1, 2):
                    body(At(it, off), True)
            body(At(0, NPAIR - 1), False)
            tail(At(0, NPAIR))

        @blk.sync
        def _(e):
            def load_qk(j):
                e.dma_start(wqk[j.u][:, :, :], io["wqk"][j.n() % HP, :, :, :]).then_inc(s_ldw[j.u], 16)
                e.dma_start(c[j.u][:, :, :], scr["c"][j.n() // HP, :, :, :].rearrange("j p s -> p j s")).then_inc(s_ldw[j.u], 16)

            def load_v(j):
                e.dma_start(v[j.u][:, :, :], scr["v"][j.n() // HP, j.n() % HP, :, :, :]).then_inc(s_ldv[j.u], 16)

            def max_rows(j):
                e.wait_ge(s_frd, j.n(FRONT, FRONT))
                for h in range(2):
                    r = other[h].start
                    e.dma_start(qb[j.u][h][r:r + 1, :].bitcast(F32).rearrange("o (t q) -> o t q", q=P),
                                mneg[h * KT:(h + 1) * KT, :].bitcast(F32)).then_inc(s_mrow, 16)

            def store(i):
                e.wait_ge(s_ot, i.n(1, 1))
                e.dma_start(scr["o"][i.n(), :, :], oT[i.u][:, :]).then_inc(s_store[i.u], 16)

            def prologue():
                load_qk(At(0, 0))
                e.dma_start(cos[:, :], io["cos"]).then_inc(s_const, 16)
                e.dma_start(sin[:, :], io["sin"]).then_inc(s_const, 16)
                for s in s_store:
                    e.sem_inc(s, 16)
                load_qk(At(0, 1))
                load_v(At(0, 0))
                e.wait_ge(s_init, 2)
                max_rows(At(0, 0))

            def body(i, more):
                first = isinstance(i.base, int) and i.off == 0
                if more:
                    if not (isinstance(i.base, int) and i.off >= NPAIR - 2):
                        e.wait_ge(s_fr, i.n(FRONT, 4))
                        j = i.next(2)
                        jn = j.n() % NPAIR
                        e.dma_start(wqk[j.u][:, :, :], io["wqk"][jn % HP, :, :, :]).then_inc(s_ldw[j.u], 16)
                        e.dma_start(c[j.u][:, :, :], scr["c"][jn // HP, :, :, :].rearrange("j p s -> p j s")).then_inc(s_ldw[j.u], 16)
                    wait(e, s_pv, i.n(KT, 0))
                    load_v(i.next(1))
                if not first:
                    store(i.next(-1))
                if more:
                    max_rows(i.next(1))

            def tail(i):
                store(i.next(-1))
                for u in range(2):
                    e.wait_ge(s_ldw[u], 32 * (NPAIR // 2 + (u == 0)))
                    e.wait_ge(s_store[u], 16 * (NPAIR // 2 + 1))

            run(e, prologue, body, tail)

        @blk.gpsimd
        def _(e):
            def prologue():
                pass

            def body(i, more):
                def sums(kt):
                    for h in range(2):
                        wait_apart(e, s_exp, i.n(TILES, 2 * kt + h + 1), s_apart)
                        acc = total[i.u][h][:, :]
                        if kt == 1:
                            wait_apart(e, s_denf, i.n(1, -1), s_apart)
                            a0 = ex[h][:, :]
                        else:
                            wait_apart(e, s_sum, i.n(14, 2 * (kt - 2) + h + 1), s_apart)
                            a0 = acc
                        e.tensor_tensor(out=acc, in0=a0, in1=ex[(2 * kt + h) % NP][:, :], op=ALU.add).then_inc(s_sum, 1)

                for kt in range(1, KT):
                    sums(kt)
                    if kt == 2:
                        wait_apart(e, s_scat, i.n(32, 0), s_apart)
                        e.tensor_copy(fill_i[:, :], keep["fill"][:, i.n(), :])
                        e.tensor_copy(tok_i[:, :], keep["tok"][:, bass.ds(i.n(), 1)]).then_inc(s_idx, 1)
                        wait_apart(e, s_idx, i.n(1, 1), s_apart)
                        for k in range(2):
                            e.indirect_dma_start(out=scr["table"], out_offset=bass.IndirectOffsetOnAxis(ap=fill_i[:, k:k + 1], axis=0),
                                                 in_=tok_i[:, :], in_offset=None, bounds_check=NSLOT - 1, oob_is_err=False).then_inc(s_scat, 16)

            def tail(i):
                e.wait_ge(s_scat, 32 * NPAIR)

            run(e, prologue, body, tail)

        @blk.vector
        def _(e):
            def rope(j):
                for w in range(2):
                    wait(e, s_rot, j.n(2, w))
                    e.wait_ge(s_fr, j.n(FRONT, 2 * w + 1))
                    e.tensor_tensor(out=t1[:, :], in0=pfr[:, :], in1=cos[:, :], op=ALU.mult).then_inc(s_frd, 1)
                    e.wait_ge(s_fr, j.n(FRONT, 2 * w + 2))
                    e.tensor_tensor(out=t2[:, :], in0=pfr[:, :], in1=sin[:, :], op=ALU.mult).then_inc(s_frd, 1)
                    e.wait_ge(s_frd, j.n(FRONT, 2 * w + 2))
                    wait(e, s_hi, j.n(8, 4 * w - 4))
                    e.tensor_tensor(out=rot[w][:, :], in0=t1[:, :], in1=t2[:, :], op=ALU.add).then_inc(s_rot, 1)

            def low(j):
                for w, (hi, dst) in enumerate(((qa, qb), (ka, ka))):
                    for h in range(2):
                        e.wait_ge(s_hi, j.n(8, 4 * w + 2 * h + 2))
                        r = rows[h]
                        to = r if w == 0 else other[h]
                        e.tensor_tensor(out=dst[j.u][h][to, :], in0=rot[w][r, :], in1=hi[j.u][h][r, :].bitcast(F32), op=ALU.subtract).then_inc(s_lo, 1)

            def maximum(j, m):
                e.wait_ge(s_fr, j.n(FRONT, 5 + m))
                e.reduce_max(mx[:, m:m + 1], pfr[:, :], AX.X).then_inc(s_frd, 1)

            def recip(i, piece):
                if piece == 0:
                    e.wait_ge(s_dend, i.n(1, 1))
                n = S // NREC
                cols = slice(piece * n, (piece + 1) * n)
                e.reciprocal(den[:, cols], den[:, cols]).then_inc(s_rec, 1)

            def normalise(i):
                e.wait_ge(s_rec, i.n(NREC, NREC))
                e.wait_ge(s_osb, i.n(1, 1))
                e.wait_ge(s_store[i.u], i.same(16, 16))
                e.tensor_tensor(out=oT[i.u][:, :], in0=osb[:, :], in1=den[:, :], op=ALU.mult).then_inc(s_ot, 1)

            def front(j, i=None):
                rope(j)
                low(j)
                for m in range(MAXES):
                    maximum(j, m)
                    if i is not None and m % 2 == 0:
                        recip(i, m // 2)
                        if m // 2 == NREC - 1:
                            normalise(i)

            def back_only(i):
                for piece in range(NREC):
                    recip(i, piece)
                normalise(i)

            def prologue():
                for u in range(2):
                    for h in range(2):
                        e.memset(qb[u][h][other[h], :].bitcast(F32), 0.0)
                        last = e.memset(kb[u][h][other[h], :].bitcast(F32), 0.0)
                e.memset(ones[:, :], 1.0)
                last.then_inc(s_init, 1)
                e.wait_ge(s_init, 1)
                for u in range(2):
                    for h in range(2):
                        r = other[h].start
                        last = e.memset(kb[u][h][r:r + 1, :].bitcast(F32), 1.0)
                last.then_inc(s_init, 1)
                e.wait_ge(s_const, 32)
                front(At(0, 0))

            def body(i, more):
                prev = None if isinstance(i.base, int) and i.off == 0 else i.next(-1)
                if more:
                    front(i.next(1), prev)
                else:
                    back_only(prev)

            run(e, prologue, body, lambda i: back_only(i.next(-1)))

        @blk.scalar
        def _(e):
            def exps(i, s):
                kt, h = s // 2, s % 2
                e.wait_ge(s_st, i.n(TILES, s + 1))
                wait(e, s_pv, i.n(KT, kt - NP // 2 + 1))
                back = kt - NP // 2
                wait(e, s_sum, i.n(14, 2 * max(back - 1, 0) + h + 1) if back >= 0 else i.n(14, 2 * (back + KT - 1) + h + 1 - 14))
                e.activation(ex[s % NP][:, :], pst[s % 2][:, :], ACT.Exp, scale=SCALE).then_inc(s_exp, 1)

            def high(j, w):
                e.wait_ge(s_rot, j.n(2, w + 1))
                if w == 0:
                    wait(e, s_st, j.n(TILES, -TILES))
                for h in range(2):
                    r = rows[h]
                    for dst, to in (((qa, r), (qa, other[h])), ((ka, r), (kb, r)))[w]:
                        e.activation(dst[j.u][h][to, :], rot[w][r, :], ACT.Copy).then_inc(s_hi, 1)

            def out_copy(i):
                e.wait_ge(s_pv, i.n(KT, KT))
                wait(e, s_ot, i.n())
                e.activation(osb[:, :], ppv[:, :], ACT.Copy).then_inc(s_osb, 1)

            def den_copy(i):
                e.wait_ge(s_denf, i.n(1, 1))
                wait(e, s_ot, i.n())
                e.activation(den[:, :], pfr[:, :], ACT.Copy).then_inc(s_dend, 1)

            def negate(j):
                e.wait_ge(s_fr, j.n(FRONT, FRONT))
                wait(e, s_mrow, j.n(32, 0))
                e.activation(mneg[:, :], pfr[0:MAXES, 0:P], ACT.Copy, scale=-1.0).then_inc(s_frd, 1)

            def prologue():
                high(At(0, 0), 0)
                high(At(0, 0), 1)
                negate(At(0, 0))

            def body(i, more):
                prev = None if isinstance(i.base, int) and i.off == 0 else i.next(-1)
                for s in range(TILES):
                    exps(i, s)
                    if s == 1 and prev is not None:
                        out_copy(prev)
                    if s == 2 and more:
                        high(i.next(1), 0)
                    if s == 4 and more:
                        high(i.next(1), 1)
                    if s == 5 and prev is not None:
                        den_copy(prev)
                if more:
                    negate(i.next(1))

            def tail(i):
                out_copy(i.next(-1))
                den_copy(i.next(-1))

            run(e, prologue, body, tail)

        @blk.tensor
        def _(e):
            def scores(i, s):
                kt, h = s // 2, s % 2
                if s < 2:
                    e.wait_ge(s_mrow, i.n(32, 32))
                wait(e, s_exp, i.n(TILES, s - 1))
                keys = slice(kt * P, (kt + 1) * P)
                for ww, (kk, qq) in enumerate(((ka, qa), (kb, qb))):
                    for n in range(NH2):
                        cols = slice(n * HALF, (n + 1) * HALF)
                        mm = e.matmul(pst[s % 2][:, cols], kk[i.u][h][:, keys], qq[i.u][h][:, cols], start=(ww == 0), stop=(ww == 1))
                mm.then_inc(s_st, 1)

            def values(i, kt):
                if kt == 0:
                    e.wait_ge(s_ldv[i.u], i.same(16, 16))
                    wait(e, s_osb, i.n())
                e.wait_ge(s_exp, i.n(TILES, 2 * kt + 2))
                for n in range(NH2):
                    cols = slice(n * HALF, (n + 1) * HALF)
                    for h in range(2):
                        mm = e.matmul(ppv[rows[h], cols], v[i.u][:, kt, rows[h]], ex[(2 * kt + h) % NP][:, cols],
                                      start=(kt == 0), stop=(kt == KT - 1))
                mm.then_inc(s_pv, 1)

            def denominators(i):
                e.wait_ge(s_sum, i.n(14, 14))
                for n in range(NH2):
                    cols = slice(n * HALF, (n + 1) * HALF)
                    for h in range(2):
                        mm = e.matmul(pfr[rows[h], cols], ones[:, :], total[i.u][h][:, cols], start=True, stop=True)
                mm.then_inc(s_denf, 1)

            def project(j, k):
                if k == 0:
                    e.wait_ge(s_ldw[j.u], j.same(32, 32))
                wait(e, s_frd, j.n(FRONT, k))
                for n in range(NH2):
                    cols = slice(n * HALF, (n + 1) * HALF)
                    mm = e.matmul(pfr[:, cols], wqk[j.u][:, k, :], c[j.u][:, k // 2, cols], start=True, stop=True)
                mm.then_inc(s_fr, 1)

            def max_scores(j, m, den_of):
                h, qt = m // KT, m % KT
                if m == 0:
                    e.wait_ge(s_hi, j.n(8, 8))
                    e.wait_ge(s_lo, j.n(4, 4))
                    if den_of is not None:
                        e.wait_ge(s_dend, den_of.n(1, 1))
                e.wait_ge(s_frd, j.n(FRONT, 4 + m))
                for n in range(NH2):
                    cols = slice(n * HALF, (n + 1) * HALF)
                    mm = e.matmul(pfr[:, cols], qa[j.u][h][:, qt * P:(qt + 1) * P], ka[j.u][h][:, cols], start=True, stop=True)
                mm.then_inc(s_fr, 1)

            def turn_maxima(j):
                e.wait_ge(s_frd, j.n(FRONT, FRONT - 1))
                e.transpose(pfr[0:MAXES, 0:P], mx[:, :], keep["ident"][:, :]).then_inc(s_fr, 1)

            def prologue():
                for k in range(4):
                    project(At(0, 0), k)
                for m in range(MAXES):
                    max_scores(At(0, 0), m, None)
                turn_maxima(At(0, 0))

            PLAN = [0, 0, 0, 0, 0, 1, 1, 2, 1, 2, 1, 2, 1, 2, 2, 1]
            assert sum(PLAN) == MAXES

            def body(i, more):
                prev = None if isinstance(i.base, int) and i.off == 0 else i.next(-1)
                nxt = i.next(1)
                m = 0
                for s in range(TILES):
                    scores(i, s)
                    if s == 1 and prev is not None:
                        values(prev, KT - 1)
                    if s % 2 == 1 and s > 1:
                        values(i, s // 2 - 1)
                    if more and s < 4:
                        project(nxt, s)
                    if s == 4 and prev is not None:
                        e.wait_ge(s_frd, nxt.n(FRONT, 4 if more else 0))
                        denominators(prev)
                    if more:
                        for _ in range(PLAN[s]):
                            max_scores(nxt, m, prev)
                            m += 1
                if more:
                    turn_maxima(nxt)

            def tail(i):
                values(i.next(-1), KT - 1)
                e.wait_ge(s_dend, i.n(1, -1))
                denominators(i.next(-1))

            run(e, prologue, body, tail)


def experts_phase(nc, io, scr, keep):
    with ExitStack() as ctx:
        ph = Phase(nc, ctx, "ex")
        sb, ps, sem = ph.sb, ph.ps, ph.sem
        STEPS = NE // 2 * PARTS
        w1 = [sb(f"w1{q}", [P, KD, FF]) for q in range(2)]
        w2 = [sb(f"w2{q}", [P, NF, D]) for q in range(2)]
        slots = sb("slots", [SLOT_P, NE, SLOT_T], I32)
        idx = [sb(f"idx{q}", [SLOT_P, PART_T], I32) for q in range(2)]
        xg = [sb(f"xg{q}", [SLOT_P, PART_T, D]) for q in range(2)]
        xT = [sb(f"xT{q}", [P, KD, PW]) for q in range(2)]
        hT = [sb(f"hT{q}", [P, NF, PW]) for q in range(2)]
        out = [sb(f"out{q}", [SLOT_P, PART_T, D]) for q in range(2)]
        ptr = ps("tr", [P, KD, HALF])
        ph_ = [ps(f"h{k}", [P, HALF]) for k in range(2)]
        po = ps("o", [P, PART_T, HALF])
        s_w = [sem(f"w{q}") for q in range(2)]
        s_g = [sem(f"g{q}") for q in range(2)]
        s_os = [sem(f"os{q}") for q in range(2)]
        s_apart = sem("apart")
        s_slots, s_idx, s_tr, s_xT, s_h, s_silu, s_o, s_oe = (sem(n) for n in ("slots", "idx", "tr", "xT", "h", "silu", "o", "oe"))
        blk = ph.block()

        @blk.sync
        def _(e):
            e.dma_start(slots[:, :, :], scr["table"].rearrange("(e p t) o -> p e (t o)", e=NE, p=SLOT_P)).then_inc(s_slots, 16)
            for q in range(2):
                e.dma_start(w1[q][:, :, :], io["w1"][q, :, :].rearrange("(k p) f -> p k f", p=P)).then_inc(s_w[q], 16)
                e.dma_start(w2[q][:, :, :], io["w2"][q, :, :].rearrange("(k p) d -> p k d", p=P)).then_inc(s_w[q], 16)
            with e.Fori(1, NE // 2) as pr:
                for q in range(2):
                    e.wait_ge(s_o, pr * (2 * PARTS) + (q - 1))
                    e.dma_start(w1[q][:, :, :], io["w1"][pr * 2 + q, :, :].rearrange("(k p) f -> p k f", p=P)).then_inc(s_w[q], 16)
                    e.dma_start(w2[q][:, :, :], io["w2"][pr * 2 + q, :, :].rearrange("(k p) d -> p k d", p=P)).then_inc(s_w[q], 16)

        @blk.gpsimd
        def _(e):
            e.wait_ge(s_slots, 16)

            def gather(n, q, first):
                a = At(n, q)
                if not first:
                    wait_apart(e, s_tr, a.n(1, -1), s_apart)
                col = (n // PARTS) * (2 * SLOT_T) + (n % PARTS) * PART_T + q * SLOT_T
                e.tensor_copy(idx[q][:, :], slots[:, :, :].rearrange("p e t -> p (e t)")[:, bass.ds(col, PART_T)]).then_inc(s_idx, 1)
                wait_apart(e, s_idx, a.n(1, 1), s_apart)
                for c in range(PART_T):
                    e.indirect_dma_start(out=xg[q][:, c, :], out_offset=None, in_=scr["xn"].rearrange("b s d -> (b s) d"),
                                         in_offset=bass.IndirectOffsetOnAxis(ap=idx[q][:, c:c + 1], axis=0)).then_inc(s_g[q], 16)

            for q in range(2):
                gather(0, q, True)
            with e.Fori(1, STEPS) as n:
                for q in range(2):
                    gather(n, q, False)

        @blk.vector
        def _(e):
            def turned(a):
                e.wait_ge(s_tr, a.n(1, 1))
                e.tensor_copy(xT[a.u][:, :, :], ptr[:, :, 0:PW]).then_inc(s_xT, 1)

            def outputs(a):
                e.wait_ge(s_os[a.u], a.same(16, 16))
                e.wait_ge(s_o, a.n(1, 1))
                e.tensor_copy(out[a.u][:, :, :], po[0:SLOT_P, :, 0:D]).then_inc(s_oe, 1)

            turned(At(0, 0))
            with e.Fori(0, STEPS - 1) as n:
                for q in range(2):
                    turned(At(n, q + 1))
                    outputs(At(n, q))
            turned(At(STEPS - 1, 1))
            outputs(At(STEPS - 1, 0))
            outputs(At(STEPS - 1, 1))

        @blk.scalar
        def _(e):
            for q in range(2):
                e.sem_inc(s_os[q], 16)

            def silus(a):
                for f in range(NF):
                    e.wait_ge(s_h, a.n(NF, f + 1))
                    e.activation(hT[a.u][:, f, :], ph_[f % 2][:, 0:PW], ACT.Silu).then_inc(s_silu, 1)

            def store(n, q):
                a = At(n, q)
                e.wait_ge(s_oe, a.n(1, 1))
                dst = scr["eo"].rearrange("(e p g c) d -> e g p (c d)", e=NE, p=SLOT_P, g=PARTS)
                e.dma_start(dst[(n // PARTS) * 2 + q, n % PARTS, :, :], out[q][:, :, :].rearrange("p c d -> p (c d)")).then_inc(s_os[q], 16)

            silus(At(0, 0))
            with e.Fori(0, STEPS - 1) as n:
                silus(At(n, 1))
                store(n, 0)
                silus(At(n, 2))
                store(n, 1)
            silus(At(STEPS - 1, 1))
            store(STEPS - 1, 0)
            store(STEPS - 1, 1)
            for q in range(2):
                e.wait_ge(s_os[q], 16 * (STEPS + 1))

        @blk.tensor
        def _(e):
            def turn(a, first=False):
                e.wait_ge(s_g[a.u], a.same(48, 48))
                if not first:
                    e.wait_ge(s_xT, a.n())
                for c in range(PART_T):
                    for k in range(KD):
                        mm = e.transpose(ptr[:, k, c * SLOT_P:(c + 1) * SLOT_P], xg[a.u][:, c, k * P:(k + 1) * P], keep["ident"][0:SLOT_P, 0:SLOT_P])
                mm.then_inc(s_tr, 1)

            def hidden(n, q):
                a = At(n, q)
                e.wait_ge(s_w[q], (n // PARTS) * 32 + 32)
                e.wait_ge(s_xT, a.n(1, 1))
                for f in range(NF):
                    wait(e, s_silu, a.n(NF, f - 1))
                    for k in range(KD):
                        mm = e.matmul(ph_[f % 2][:, 0:PW], w1[q][:, k, f * P:(f + 1) * P], xT[q][:, k, :], start=(k == 0), stop=(k == KD - 1))
                    mm.then_inc(s_h, 1)

            def down(n, q, first=False):
                a = At(n, q)
                if not first:
                    e.wait_ge(s_oe, a.n())
                for c in range(PART_T):
                    for f in range(NF):
                        if c == 0:
                            e.wait_ge(s_silu, a.n(NF, f + 1))
                        mm = e.matmul(po[0:SLOT_P, c, 0:D], hT[q][:, f, c * SLOT_P:(c + 1) * SLOT_P], w2[q][:, f, :], start=(f == 0), stop=(f == NF - 1))
                mm.then_inc(s_o, 1)

            turn(At(0, 0), True)
            hidden(0, 0)
            turn(At(0, 1))
            down(0, 0, True)
            hidden(0, 1)
            turn(At(0, 2))
            down(0, 1)
            with e.Fori(1, STEPS - 1) as n:
                hidden(n, 0)
                turn(At(n, 1))
                down(n, 0)
                hidden(n, 1)
                turn(At(n, 2))
                down(n, 1)
            hidden(STEPS - 1, 0)
            turn(At(STEPS - 1, 1))
            down(STEPS - 1, 0)
            hidden(STEPS - 1, 1)
            down(STEPS - 1, 1)


def combine_phase(nc, io, scr, keep):
    with ExitStack() as ctx:
        ph = Phase(nc, ctx, "cb")
        sb, ps, sem = ph.sb, ph.ps, ph.sem
        oT = [sb(f"oT{u}", [P, HP, S]) for u in range(2)]
        x = [sb(f"x{u}", [P, TB, D]) for u in range(2)]
        xn = [sb(f"xn{u}", [P, TB, D]) for u in range(2)]
        res = [sb(f"res{u}", [P, TB, D]) for u in range(2)]
        wo = sb("wo", [P, HP, D])
        NG = 4
        idx = [sb(f"idx{k}", [P, 2], I32) for k in range(NG)]
        eo = [[sb(f"eo{k}{j}", [P, D]) for j in range(2)] for k in range(NG)]
        att = [sb(f"att{k}", [P, D]) for k in range(2)]
        mix = [sb(f"mix{k}", [P, D]) for k in range(2)]
        gate = [sb(f"gate{k}", [P, D]) for k in range(2)]
        g2 = sb("g2", [P, TB, 2])
        pj = [ps(f"pj{k}", [P, HALF]) for k in range(2)]
        s_wo, s_pj, s_att, s_mix, s_silu, s_res, s_idx, s_g2 = (sem(n) for n in ("wo", "pj", "att", "mix", "silu", "res", "idx", "g2"))
        s_apart = sem("apart")
        s_ld = [sem(f"ld{u}") for u in range(2)]
        s_g = [sem(f"rows{k}") for k in range(NG)]
        s_st = [sem(f"st{u}") for u in range(2)]
        blk = ph.block()

        @blk.sync
        def _(e):
            e.dma_start(wo[:, :, :], io["woT"].rearrange("(r p) d -> p r d", p=P)).then_inc(s_wo, 16)

            def load(a):
                e.dma_start(oT[a.u][:, :, :], scr["o"].rearrange("(b r) p s -> b p r s", r=HP)[a.n(), :, :, :]).then_inc(s_ld[a.u], 16)
                e.dma_start(xn[a.u][:, :, :], scr["xn"][a.n(), :, :].rearrange("(t p) d -> p t d", p=P)).then_inc(s_ld[a.u], 16)
                e.dma_start(x[a.u][:, :, :], io["x"][a.n(), :, :].rearrange("(t p) d -> p t d", p=P)).then_inc(s_ld[a.u], 16)

            def store(a):
                e.wait_ge(s_res, a.n(TB, TB + 2))
                e.dma_start(io["out"][a.n(), :, :].rearrange("(t p) d -> p t d", p=P), res[a.u][:, :, :]).then_inc(s_st[a.u], 16)

            for u in range(2):
                e.sem_inc(s_st[u], 16)
                load(At(0, u))
            with e.Fori(0, NBATCH // 2 - 1) as it:
                for u in range(2):
                    store(At(it, u))
                    load(At(it, u + 2))
            for u in range(2):
                store(At(0, NBATCH - 2 + u))
            for u in range(2):
                e.wait_ge(s_st[u], 16 * (NBATCH // 2 + 1))

        @blk.gpsimd
        def _(e):
            def gather(b, t, first):
                k = t % NG
                if not first:
                    wait_apart(e, s_mix, b * (2 * TB) + 2 * (t - NG + 1), s_apart)
                e.tensor_copy(idx[k][:, :], keep["read"][:, b * TB + t, :]).then_inc(s_idx, 1)
                wait_apart(e, s_idx, b * TB + (t + 1), s_apart)
                for j in range(2):
                    e.indirect_dma_start(out=eo[k][j][:, :], out_offset=None, in_=scr["eo"],
                                         in_offset=bass.IndirectOffsetOnAxis(ap=idx[k][:, j:j + 1], axis=0)).then_inc(s_g[k], 16)

            e.wait_ge(s_wo, 16)
            for t in range(TB):
                gather(0, t, t < NG)
            with e.Fori(1, NBATCH) as b:
                for t in range(TB):
                    gather(b, t, False)

        @blk.vector
        def _(e):
            def tile(a, t):
                u, k = a.u, t % 2
                e.wait_ge(s_res, a.n(TB, t + 1))
                e.wait_ge(s_pj, a.n(TB, t + 1))
                e.tensor_tensor(out=att[k][:, :], in0=pj[k][:, 0:D], in1=xn[u][:, t, :], op=ALU.add).then_inc(s_att, 1)
                e.wait_ge(s_g[t % NG], a.n(2 * 32, 32 + 32 * (t // NG)))
                e.scalar_tensor_tensor(out=mix[k][:, :], in0=eo[t % NG][0][:, :], scalar=g2[:, t, 0:1], in1=xn[u][:, t, :], op0=ALU.mult, op1=ALU.add).then_inc(s_mix, 1)
                e.wait_ge(s_mix, a.n(2 * TB, 2 * t + 1))
                e.scalar_tensor_tensor(out=mix[k][:, :], in0=eo[t % NG][1][:, :], scalar=g2[:, t, 1:2], in1=mix[k][:, :], op0=ALU.mult, op1=ALU.add).then_inc(s_mix, 1)

            def finish(a, t):
                u, k = a.u, t % 2
                e.wait_ge(s_silu, a.n(TB, t + 1))
                e.wait_ge(s_att, a.n(TB, t + 1))
                e.tensor_tensor(out=att[k][:, :], in0=att[k][:, :], in1=gate[k][:, :], op=ALU.mult).then_inc(s_g2, 1)
                e.wait_ge(s_g2, a.n(TB + 1, t + 2))
                e.tensor_tensor(out=res[u][:, t, :], in0=att[k][:, :], in1=x[u][:, t, :], op=ALU.add).then_inc(s_res, 1)

            def batch(a):
                e.wait_ge(s_ld[a.u], a.same(48, 48))
                e.wait_ge(s_st[a.u], a.same(16, 16))
                e.tensor_copy(g2[:, :, :], keep["gate"][:, bass.ds(a.n(TB), TB), :]).then_inc(s_g2, 1)
                e.wait_ge(s_g2, a.n(TB + 1, 1))
                for t in range(TB):
                    tile(a, t)
                    if t:
                        finish(a, t - 1)
                finish(a, TB - 1)

            e.sem_inc(s_res, 2)
            with e.Fori(0, NBATCH // 2) as it:
                for u in range(2):
                    batch(At(it, u))

        @blk.scalar
        def _(e):
            with e.Fori(0, NBATCH) as b:
                for t in range(TB):
                    e.wait_ge(s_mix, b * (2 * TB) + 2 * (t + 1))
                    e.activation(gate[t % 2][:, :], mix[t % 2][:, :], ACT.Silu).then_inc(s_silu, 1)

        @blk.tensor
        def _(e):
            e.wait_ge(s_wo, 16)

            def tile(a, t, first):
                if t == 0:
                    e.wait_ge(s_ld[a.u], a.same(48, 48))
                if not first:
                    e.wait_ge(s_att, a.n(TB, t - 1))
                for r in range(HP):
                    mm = e.matmul(pj[t % 2][:, 0:D], oT[a.u][:, r, t * P:(t + 1) * P], wo[:, r, :], start=(r == 0), stop=(r == HP - 1))
                mm.then_inc(s_pj, 1)

            for u in range(2):
                for t in range(TB):
                    tile(At(0, u), t, u == 0 and t < 2)
            with e.Fori(1, NBATCH // 2) as it:
                for u in range(2):
                    for t in range(TB):
                        tile(At(it, u), t, False)


def build(nc, io):
    with ExitStack() as ctx:
        def scratch(name, shape, dt=F32):
            return nc.dram_tensor(f"scr_{name}", shape, dt, kind="Internal").ap()

        scr = {
            "xn": scratch("xn", [NBATCH, S, D]),
            "c": scratch("c", [NBATCH, 2, DL, S]),
            "v": scratch("v", [NBATCH, HP, P, KT, P]),
            "o": scratch("o", [NPAIR, P, S]),
            "table": scratch("table", [NSLOT, 1], I32),
            "eo": scratch("eo", [NSLOT, D]),
        }

        def sb(name, shape, dt=F32):
            return ctx.enter_context(nc.sbuf_tensor(f"keep_{name}", shape, dt))

        keep = {
            "ident": sb("ident", [P, P]),
            "logits": sb("logits", [P, NT * NE]),
            "tok": sb("tok", [P, NT], I32),
            "gate": sb("gate", [P, NT, 2]),
            "fill": sb("fill", [P, NT, 2], I32),
            "read": sb("read", [P, NT, 2], I32),
        }
        project_phase(nc, io, scr, keep)
        route_phase(nc, io, scr, keep)
        attend_phase(nc, io, scr, keep)
        experts_phase(nc, io, scr, keep)
        combine_phase(nc, io, scr, keep)


def shape_constants():
    inv_freq = 1.0 / 10000.0 ** (np.arange(0, DH, 2, dtype=np.float32) / DH)
    freqs = np.outer(np.arange(S, dtype=np.float32), inv_freq).astype(np.float32)
    cos = np.concatenate([np.cos(freqs), np.cos(freqs)], -1)[:, ::2].astype(np.float32)
    sin = np.concatenate([np.sin(freqs), np.sin(freqs)], -1)[:, ::2].astype(np.float32)
    dim = np.arange(P) % DH
    e = np.tile(np.arange(NE, dtype=np.float32), NT)
    return {
        "cos": np.ascontiguousarray(cos.T[dim // 2]),
        "sin": np.ascontiguousarray(sin.T[dim // 2] * np.where(dim % 2 == 0, -1.0, 1.0).astype(np.float32)[:, None]),
        "ident": np.eye(P, dtype=np.float32),
        "tri": np.triu(np.ones((P, P), np.float32), 1),
        "rev": np.broadcast_to(NE - e, (P, NT * NE)).copy(),
        "ebase": np.broadcast_to(e * CAPP, (P, NT * NE)).copy(),
        "newe": np.broadcast_to((np.arange(NT * NE) % NT != 0).astype(np.float32), (P, NT * NE)).copy(),
        "tok": (np.arange(NT)[None, :] * P + np.arange(P)[:, None]).astype(np.int32),
    }


def kernel(**inputs):
    import concourse.bacc as bacc
    from concourse.bass_utils import run_bass_kernel_spmd

    a = {k: np.asarray(v) for k, v in inputs.items()}
    swap = np.arange(P) ^ 1

    def pairs(w):
        return w.reshape(HP, P, DL).transpose(0, 2, 1)

    wq, wk = pairs(a["L0_attn_w_up_q"]), pairs(a["L0_attn_w_up_k"])
    arrays = {
        "x": a["L0_attn_x"],
        "wdqT": a["L0_attn_w_down_q"].T,
        "wdkvT": a["L0_attn_w_down_kv"].T,
        "wqk": np.stack([wq, wq[:, :, swap], wk, wk[:, :, swap]], axis=2),
        "wvT": a["L0_attn_w_up_v"].T,
        "woT": a["L0_attn_w_out"].T,
        "lnp": np.stack([a["L0_attn_ln_scale"].reshape(KD, P).T, a["L0_attn_ln_bias"].reshape(KD, P).T], axis=2),
        "rwT": a["L0_ffn_router_w"].T,
        "w1": a["L0_ffn_w1"],
        "w2": a["L0_ffn_w2"],
        **shape_constants(),
    }
    arrays = {k: np.ascontiguousarray(v) for k, v in arrays.items()}
    nc = bacc.Bacc("TRN2", target_bir_lowering=False, num_devices=1)
    io = {k: nc.dram_tensor(f"in_{k}", v.shape, mybir.dt.from_np(v.dtype), kind="ExternalInput").ap() for k, v in arrays.items()}
    io["out"] = nc.dram_tensor("out_0", [NBATCH, S, D], F32, kind="ExternalOutput").ap()
    build(nc, io)
    r = run_bass_kernel_spmd(nc, [{f"in_{k}": v for k, v in arrays.items()}], core_ids=[0])
    return r.results[0]["out_0"]
```

```python
from contextlib import ExitStack

import numpy as np
import concourse.bass as bass
from concourse import mybir

F32, F32R, I32 = mybir.dt.float32, mybir.dt.float32r, mybir.dt.int32
ALU, ACT, AX = mybir.AluOpType, mybir.ActivationFunctionType, mybir.AxisListType

P = 128
NBATCH, S, D = 8, 1024, 256
H, DH, DL = 16, 64, 128
NE, FF = 8, 1024
NTOK = NBATCH * S
NT = NTOK // P
TB = S // P
KD = D // P
HALF = 512
NH2 = S // HALF
HP = H // 2
NPAIR = NBATCH * HP
KT = S // P
CAP = int(1.25 * NTOK * 2 / NE) + 1
SLOT_P = 122
SLOT_T = 21
CAPP = SLOT_P * SLOT_T
PART_T = 3
PARTS = SLOT_T // PART_T
PW = PART_T * SLOT_P
NF = FF // P
NSLOT = NE * CAPP
EPS = 1e-5
FAR = float(1 << 20)
SCALE = 1.0 / 8.0


class At:

    def __init__(self, base, off):
        self.base, self.off, self.u = base, off, off % 2

    def n(self, k=1, add=0):
        return self.base * (2 * k) + (self.off * k + add)

    def same(self, k, add=0):
        return self.base * k + ((self.off // 2) * k + add)

    def next(self, d):
        return At(self.base, self.off + d)


def wait(eng, sem, value):
    if not (isinstance(value, int) and value <= 0):
        eng.wait_ge(sem, value)


def wait_apart(eng, sem, value, own):
    wait(eng, sem, value)
    eng.sem_inc(own, 1)


class Phase:

    def __init__(self, nc, ctx, tag):
        self.nc, self.ctx, self.tag = nc, ctx, tag

    def sb(self, name, shape, dt=F32):
        return self.ctx.enter_context(self.nc.sbuf_tensor(f"{self.tag}_{name}", shape, dt))

    def ps(self, name, shape):
        return self.ctx.enter_context(self.nc.psum_tensor(f"{self.tag}_{name}", shape, F32))

    def sem(self, name):
        return self.ctx.enter_context(self.nc.semaphore(f"{self.tag}_{name}"))

    def block(self):
        return self.ctx.enter_context(self.nc.Block())


def project_phase(nc, io, scr, keep):
    with ExitStack() as ctx:
        ph = Phase(nc, ctx, "pj")
        sb, ps, sem = ph.sb, ph.ps, ph.sem
        xin = [sb(f"xin{u}", [P, TB, D]) for u in range(2)]
        xn = [sb(f"xn{u}", [P, TB, D]) for u in range(2)]
        h = sb("h", [P, TB, D])
        stats = sb("stats", [P, TB, 6])
        mv = sb("mv", [P, TB, 2])
        rstd, veps, minus_half = (sb(n, [P, TB]) for n in ("rstd", "veps", "minus_half"))
        xnT = sb("xnT", [P, KD, S])
        hT = sb("hT", [P, KD, S])
        csb = [sb(f"c{u}", [P, 2, S]) for u in range(2)]
        vsb = [sb(f"v{k}", [P, H * DH]) for k in range(4)]
        wd = sb("wd", [P, 2, KD, DL])
        wv = sb("wv", [DL, H * DH])
        rw = sb("rw", [P, KD, NE])
        lnp = sb("lnp", [P, KD, 2])
        pa = [ps(f"pa{k}", [P, S]) for k in range(2)]
        lg = ps("lg", [P, TB, NE])
        s_const, s_ln, s_pa, s_lgf, s_lgd = (sem(n) for n in ("const", "ln", "pa", "lgf", "lgd"))
        s_eps, s_apart, s_apart_v = sem("eps"), sem("apart"), sem("apart_v")
        s_x = [sem(f"x{u}") for u in range(2)]
        s_xs = [sem(f"xs{u}") for u in range(2)]
        s_cs = [sem(f"cs{u}") for u in range(2)]
        s_vs = [sem(f"vs{k}") for k in range(4)]
        s_act, s_dve = sem("act"), sem("dve")
        blk = ph.block()
        NCONST = 16 * 6
        ITEMS = 6 + TB

        @blk.sync
        def _(e):
            e.dma_start(keep["ident"][:, :], io["ident"]).then_inc(s_const, 16)
            e.dma_start(rw[:, :, :], io["rwT"].rearrange("(k p) e -> p k e", p=P)).then_inc(s_const, 16)
            e.dma_start(wd[:, 0, :, :], io["wdqT"].rearrange("(k p) m -> p k m", p=P)).then_inc(s_const, 16)
            e.dma_start(wd[:, 1, :, :], io["wdkvT"].rearrange("(k p) m -> p k m", p=P)).then_inc(s_const, 16)
            e.dma_start(wv[:, :], io["wvT"]).then_inc(s_const, 16)
            e.dma_start(lnp[:, :, :], io["lnp"]).then_inc(s_const, 16)
            for s in s_xs:
                e.sem_inc(s, 16)
            for s in s_cs:
                e.sem_inc(s, 32)
            for s in s_vs:
                e.sem_inc(s, 16)
            with e.Fori(0, NBATCH // 2) as it:
                for u in range(2):
                    a = At(it, u)
                    e.wait_ge(s_ln, a.n(8, 4))
                    e.dma_start(scr["xn"][a.n(), :, :].rearrange("(t p) d -> p t d", p=P), xn[u][:, :, :]).then_inc(s_xs[u], 16)
                    e.wait_ge(s_act, a.n(7, 4))
                    e.dma_start(scr["c"][a.n(), 0, :, :], csb[u][:, 0, :]).then_inc(s_cs[u], 16)
                    e.wait_ge(s_dve, a.n(7, 4))
                    e.dma_start(scr["c"][a.n(), 1, :, :], csb[u][:, 1, :]).then_inc(s_cs[u], 16)
                    for t in range(TB):
                        e.wait_ge((s_act, s_dve)[t % 2], a.n(7, 5 + t // 2))
                        e.dma_start(scr["v"][a.n(), :, :, t, :].rearrange("r p m -> p r m"),
                                    vsb[t % 4][:, :].rearrange("p (r m) -> p r m", r=HP)).then_inc(s_vs[t % 4], 16)
            for s in s_xs:
                e.wait_ge(s, 16 * (NBATCH // 2 + 1))
            for s in s_cs:
                e.wait_ge(s, 32 * (NBATCH // 2 + 1))
            for s in s_vs:
                e.wait_ge(s, 16 * (2 * NBATCH + 1))

        @blk.gpsimd
        def _(e):
            def load(a):
                e.dma_start(xin[a.u][:, :, :], io["x"][a.n(), :, :].rearrange("(t p) d -> p t d", p=P)).then_inc(s_x[a.u], 16)

            def deviations(a):
                for k in (0, 4):
                    wait_apart(e, s_ln, a.n(8, k + 2), s_apart)
                    e.tensor_scalar(veps[:, :], mv[:, :, 1], EPS, None, ALU.add).then_inc(s_eps, 1)
                    wait_apart(e, s_eps, a.n(2, k // 4 + 2), s_apart)
                    e.tensor_tensor(out=rstd[:, :], in0=veps[:, :], in1=minus_half[:, :], op=ALU.pow).then_inc(s_ln, 1)

            e.memset(minus_half[:, :], -0.5).then_inc(s_eps, 1)
            for u in range(2):
                load(At(0, u))
            for u in range(2):
                deviations(At(0, u))
            with e.Fori(1, NBATCH // 2) as it:
                for u in range(2):
                    a = At(it, u)
                    wait_apart(e, s_ln, a.n(8, -12), s_apart)
                    load(a)
                    deviations(a)

        @blk.vector
        def _(e):
            def norm_stats(src):
                for t in range(TB):
                    last = e.bn_stats(stats[:, t, :], src[:, t, :])
                last.then_inc(s_ln, 1)

            def norm_apply(a, k, src, dst):
                wait_apart(e, s_ln, a.n(8, k + 1), s_apart_v)
                for t in range(TB):
                    last = e.bn_aggr(mv[:, t, :], stats[:, t, :])
                last.then_inc(s_ln, 1)
                e.wait_ge(s_ln, a.n(8, k + 3))
                for t in range(TB):
                    last = e.tensor_scalar(dst[:, t, :], src[:, t, :], mv[:, t, 0:1], rstd[:, t:t + 1], ALU.subtract, ALU.mult)
                last.then_inc(s_ln, 1)

            def norms(a):
                u = a.u
                e.wait_ge(s_x[u], a.same(16, 16))
                norm_stats(xin[u])
                yield
                e.wait_ge(s_xs[u], a.same(16, 16))
                norm_apply(a, 0, xin[u], xn[u])
                yield
                e.wait_ge(s_ln, a.n(8, 4))
                norm_stats(xn[u])
                yield
                norm_apply(a, 4, xn[u], h)
                yield

            def evacuate(a, following):
                u = a.u
                e.wait_ge(s_pa, a.n(ITEMS, 2))
                e.tensor_copy(xnT[:, 1, :], pa[1][:, :]).then_inc(s_dve, 1)
                e.wait_ge(s_pa, a.n(ITEMS, 4))
                e.tensor_scalar(hT[:, 1, :], pa[1][:, :], lnp[:, 1, 0:1], lnp[:, 1, 1:2], ALU.mult, ALU.add).then_inc(s_dve, 1)
                e.wait_ge(s_lgf, a.n(1, 1))
                e.tensor_copy(keep["logits"][:, bass.ds(a.n(TB * NE), TB * NE)], lg[:, :, :].rearrange("p t e -> p (t e)")).then_inc(s_lgd, 1)
                e.wait_ge(s_pa, a.n(ITEMS, 6))
                e.wait_ge(s_cs[u], a.same(32, 32))
                e.tensor_copy(csb[u][:, 1, :], pa[1][:, :]).then_inc(s_dve, 1)
                for t in range(1, TB, 2):
                    if following:
                        next(following)
                    e.wait_ge(s_pa, a.n(ITEMS, 7 + t))
                    e.wait_ge(s_vs[t % 4], a.n(32, 16 + 16 * (t // 4)))
                    e.tensor_copy(vsb[t % 4][:, :], pa[1][:, :]).then_inc(s_dve, 1)

            e.sem_inc(s_dve, 1)
            e.sem_inc(s_lgd, 1)
            e.wait_ge(s_const, NCONST)
            for _ in norms(At(0, 0)):
                pass
            with e.Fori(0, NBATCH // 2 - 1) as it:
                for u in range(2):
                    evacuate(At(it, u), norms(At(it, u + 1)))
            evacuate(At(0, NBATCH - 2), norms(At(0, NBATCH - 1)))
            evacuate(At(0, NBATCH - 1), None)

        @blk.scalar
        def _(e):
            e.sem_inc(s_act, 1)
            e.wait_ge(s_const, NCONST)
            with e.Fori(0, NBATCH // 2) as it:
                for u in range(2):
                    a = At(it, u)
                    e.wait_ge(s_pa, a.n(ITEMS, 1))
                    e.activation(xnT[:, 0, :], pa[0][:, :], ACT.Copy).then_inc(s_act, 1)
                    e.wait_ge(s_pa, a.n(ITEMS, 3))
                    e.activation(hT[:, 0, :], pa[0][:, :], ACT.Identity, scale=lnp[:, 0, 0:1], bias=lnp[:, 0, 1:2]).then_inc(s_act, 1)
                    e.wait_ge(s_pa, a.n(ITEMS, 5))
                    e.wait_ge(s_cs[u], a.same(32, 32))
                    e.activation(csb[u][:, 0, :], pa[0][:, :], ACT.Copy).then_inc(s_act, 1)
                    for t in range(0, TB, 2):
                        e.wait_ge(s_pa, a.n(ITEMS, 7 + t))
                        e.wait_ge(s_vs[t % 4], a.n(32, 16 + 16 * (t // 4)))
                        e.activation(vsb[t % 4][:, :], pa[0][:, :], ACT.Copy).then_inc(s_act, 1)

        @blk.tensor
        def _(e):
            e.wait_ge(s_const, NCONST)
            with e.Fori(0, NBATCH // 2) as it:
                for u in range(2):
                    a = At(it, u)

                    def fill(k):
                        e.wait_ge((s_act, s_dve)[k % 2], a.n(7, 1 + k // 2))
                        return pa[k % 2]

                    for src, k0, ready in ((xn[u], 0, 4), (h, 2, 8)):
                        e.wait_ge(s_ln, a.n(8, ready))
                        for k in range(KD):
                            out = fill(k0 + k)
                            for t in range(TB):
                                mm = e.transpose(out[:, t * P:(t + 1) * P], src[:, t, k * P:(k + 1) * P], keep["ident"][:, :])
                            mm.then_inc(s_pa, 1)
                    e.wait_ge(s_act, a.n(7, 2))
                    e.wait_ge(s_dve, a.n(7, 2))
                    e.wait_ge(s_lgd, a.n(1, 1))
                    for t in range(TB):
                        for k in range(KD):
                            mm = e.matmul(lg[:, t, :], xnT[:, k, t * P:(t + 1) * P], rw[:, k, :], start=(k == 0), stop=(k == KD - 1))
                    mm.then_inc(s_lgf, 1)
                    e.wait_ge(s_act, a.n(7, 3))
                    e.wait_ge(s_dve, a.n(7, 3))
                    for j in range(2):
                        out = fill(4 + j)
                        for k in range(KD):
                            for n in range(NH2):
                                cols = slice(n * HALF, (n + 1) * HALF)
                                mm = e.matmul(out[:, cols], wd[:, j, k, :], hT[:, k, cols], start=(k == 0), stop=(k == KD - 1))
                        mm.then_inc(s_pa, 1)
                    e.wait_ge(s_dve, a.n(7, 4))
                    for t in range(TB):
                        out = fill(6 + t)
                        for n in range(NH2):
                            cols = slice(n * HALF, (n + 1) * HALF)
                            mm = e.matmul(out[:, cols], csb[u][:, 1, t * P:(t + 1) * P], wv[:, cols], start=True, stop=True)
                        mm.then_inc(s_pa, 1)


def route_phase(nc, io, scr, keep):
    with ExitStack() as ctx:
        ph = Phase(nc, ctx, "rt")
        sb, ps, sem = ph.sb, ph.ps, ph.sem
        C = NT * NE
        lg3 = keep["logits"][:, :].rearrange("p (t e) -> p t e", e=NE)
        rev, ebase, newe = sb("rev", [P, C]), sb("ebase", [P, C]), sb("newe", [P, C])
        tri, ones = sb("tri", [P, P]), sb("ones", [P, P])
        rev3, ebase3 = (x[:, :].rearrange("p (t e) -> p t e", e=NE) for x in (rev, ebase))

        def cube(name):
            return sb(name, [P, C])[:, :].rearrange("p (t e) -> p t e", e=NE)

        w, pick, second, both, rank, tmp = (cube(n) for n in ("w", "pick", "second", "both", "rank", "tmp"))
        oh = [cube("oh0"), cube("oh1")]
        tot, cum = sb("tot", [P, NE, NT]), sb("cum", [P, NE, NT])
        m = [sb(f"m{k}", [P, NT]) for k in range(2)]
        idx = sb("idx", [P, NT])
        dif, p2, den = (sb(n, [P, NT]) for n in ("dif", "p2", "den"))
        rk, pos, over, kept = (sb(n, [P, NT]) for n in ("rk", "pos", "over", "kept"))
        zero = sb("zero", [SLOT_P, NSLOT // SLOT_P], I32)
        pp, pt = ps("prefix", [P, C]), ps("total", [P, C])
        s_const, s_v, s_oh, s_mm, s_dif, s_exp, s_zero = (sem(n) for n in ("const", "v", "oh", "mm", "dif", "exp", "zero"))
        blk = ph.block()

        @blk.sync
        def _(e):
            e.dma_start(rev[:, :], io["rev"]).then_inc(s_const, 16)
            e.dma_start(ebase[:, :], io["ebase"]).then_inc(s_const, 16)
            e.dma_start(newe[:, :], io["newe"]).then_inc(s_const, 16)
            e.dma_start(tri[:, :], io["tri"]).then_inc(s_const, 16)
            e.dma_start(keep["tok"][:, :], io["tok"]).then_inc(s_const, 16)
            e.wait_ge(s_zero, 1)
            e.dma_start(scr["table"].rearrange("(p n) o -> p (n o)", p=SLOT_P), zero[:, :]).then_inc(s_const, 16)
            e.wait_ge(s_const, 96)

        @blk.gpsimd
        def _(e):
            e.memset(zero[:, :], 0).then_inc(s_zero, 1)

        @blk.scalar
        def _(e):
            e.wait_ge(s_dif, 1)
            e.activation(p2[:, :], dif[:, :], ACT.Exp).then_inc(s_exp, 1)

        @blk.tensor
        def _(e):
            e.wait_ge(s_const, 96)
            e.wait_ge(s_oh, 1)
            e.matmul(pp[:, :], tri[:, :], both.rearrange("p t e -> p (t e)"), start=True, stop=True)
            e.matmul(pt[:, :], ones[:, :], both.rearrange("p t e -> p (t e)"), start=True, stop=True).then_inc(s_mm, 1)

        @blk.vector
        def _(e):
            done = [0]

            def then(ins):
                done[0] += 1
                ins.then_inc(s_v, 1)
                e.wait_ge(s_v, done[0])

            def bc(x):
                return x[:, :].unsqueeze(2).broadcast_to((P, NT, NE))

            e.memset(ones[:, :], 1.0)
            e.wait_ge(s_const, 96)
            src = lg3
            for k in range(2):
                then(e.tensor_reduce(out=m[k][:, :], in_=src, axis=AX.X, op=ALU.max))
                then(e.tensor_tensor(out=pick, in0=src, in1=bc(m[k]), op=ALU.is_ge))
                then(e.tensor_tensor(out=w, in0=pick, in1=rev3, op=ALU.mult))
                then(e.tensor_reduce(out=idx[:, :], in_=w, axis=AX.X, op=ALU.max))
                then(e.tensor_tensor(out=oh[k], in0=rev3, in1=bc(idx), op=ALU.is_equal))
                if k == 0:
                    then(e.scalar_tensor_tensor(out=second, in0=oh[0], scalar=-3e38, in1=lg3, op0=ALU.mult, op1=ALU.add))
                    src = second
            e.tensor_tensor(out=both, in0=oh[0], in1=oh[1], op=ALU.add).then_inc(s_oh, 1)
            e.tensor_tensor(out=dif[:, :], in0=m[1][:, :], in1=m[0][:, :], op=ALU.subtract).then_inc(s_dif, 1)
            e.wait_ge(s_exp, 1)
            then(e.tensor_scalar(den[:, :], p2[:, :], 1.0, None, ALU.add))
            then(e.reciprocal(keep["gate"][:, :, 0], den[:, :]))
            then(e.tensor_tensor(out=keep["gate"][:, :, 1], in0=p2[:, :], in1=keep["gate"][:, :, 0], op=ALU.mult))
            e.wait_ge(s_mm, 1)
            then(e.tensor_copy(tot[:, :, :], pt[:, :].rearrange("p (t e) -> p e t", e=NE)))
            then(e.tensor_tensor_scan(cum[:, :, :].rearrange("p e t -> p (e t)"), newe[:, :], tot[:, :, :].rearrange("p e t -> p (e t)"), 0.0, ALU.mult, ALU.add))
            then(e.tensor_tensor(out=cum[:, :, :], in0=cum[:, :, :], in1=tot[:, :, :], op=ALU.subtract))
            then(e.tensor_tensor(out=rank, in0=pp[:, :].rearrange("p (t e) -> p t e", e=NE), in1=cum[:, :, :].rearrange("p e t -> p t e"), op=ALU.add))
            for k in range(2):
                then(e.tensor_tensor(out=tmp, in0=oh[k], in1=rank, op=ALU.mult))
                then(e.tensor_reduce(out=rk[:, :], in_=tmp, axis=AX.X, op=ALU.add))
                then(e.tensor_tensor(out=tmp, in0=oh[k], in1=ebase3, op=ALU.mult))
                then(e.tensor_reduce(out=pos[:, :], in_=tmp, axis=AX.X, op=ALU.add))
                then(e.tensor_scalar(over[:, :], rk[:, :], float(CAP), FAR, ALU.is_ge, ALU.mult))
                then(e.tensor_tensor(out=over[:, :], in0=over[:, :], in1=rk[:, :], op=ALU.add))
                then(e.tensor_tensor(out=keep["fill"][:, :, k], in0=over[:, :], in1=pos[:, :], op=ALU.add))
                then(e.tensor_scalar(kept[:, :], rk[:, :], float(CAP), None, ALU.is_lt))
                then(e.tensor_tensor(out=keep["gate"][:, :, k], in0=keep["gate"][:, :, k], in1=kept[:, :], op=ALU.mult))
                then(e.tensor_scalar(rk[:, :], rk[:, :], float(CAP - 1), None, ALU.min))
                then(e.tensor_tensor(out=keep["read"][:, :, k], in0=rk[:, :], in1=pos[:, :], op=ALU.add))


def attend_phase(nc, io, scr, keep):
    with ExitStack() as ctx:
        ph = Phase(nc, ctx, "at")
        sb, ps, sem = ph.sb, ph.ps, ph.sem
        NP = 8
        TILES = 2 * KT
        NPROJ, NMAX = 2 * NH2, 2 * KT * NH2
        NSUM = 2 * (KT - 1)
        LO, HI = slice(0, DH), slice(DH, P)
        rows = [LO, HI]
        other = [HI, LO]
        bank = [slice(n * HALF, (n + 1) * HALF) for n in range(NH2)]
        wqk = [sb(f"wqk{u}", [DL, 2, P]) for u in range(2)]
        c = [sb(f"c{u}", [DL, 2, S]) for u in range(2)]
        v = [sb(f"v{u}", [P, KT, P]) for u in range(2)]
        raw = [sb("rawq", [P, S]), sb("rawk", [P, S])]
        swp = [sb("swpq", [P, S]), sb("swpk", [P, S])]
        rot = [sb("rotq", [P, S]), sb("rotk", [P, S])]
        qa = [[sb(f"qa{u}{h}", [P, S], F32R) for h in range(2)] for u in range(2)]
        qb = [[sb(f"qb{u}{h}", [P, S], F32R) for h in range(2)] for u in range(2)]
        ka = [[sb(f"ka{u}{h}", [P, S], F32R) for h in range(2)] for u in range(2)]
        kb = [[sb(f"kb{u}{h}", [P, S], F32R) for h in range(2)] for u in range(2)]
        ex = [sb(f"ex{k}", [P, S]) for k in range(NP)]
        total = [[sb(f"sum{u}{h}", [P, S]) for h in range(2)] for u in range(2)]
        osb, den, rec = sb("osb", [P, S]), sb("den", [P, S]), sb("rec", [P, S])
        denc, recc = sb("denc", [P, 2, S // P]), sb("recc", [P, 2, S // P])
        oT = [sb(f"oT{u}", [P, S]) for u in range(2)]
        cos, sin = sb("cos", [P, S]), sb("sin", [P, S])
        ones = sb("ones", [P, DH])
        mx = sb("mx", [P, NMAX])
        mq = [sb(f"mq{h}", [P, KT]) for h in range(2)]
        mneg = [sb(f"mneg{h}", [KT, P], F32R) for h in range(2)]
        fill_i, tok_i = sb("fill_i", [P, 2], I32), sb("tok_i", [P, 1], I32)
        pst = [ps(f"st{k}", [P, S]) for k in range(2)]
        ppv = ps("pv", [P, S])
        pfr = [ps(f"fr{k}", [P, HALF]) for k in range(2)]
        s_const, s_init, s_apart, s_apart_s = (sem(n) for n in ("const", "init", "apart", "apart_s"))
        s_ldw = [sem(f"ldw{u}") for u in range(2)]
        s_ldv = [sem(f"ldv{u}") for u in range(2)]
        s_pf, s_pe, s_mf, s_me, s_tf, s_te, s_df, s_de = (sem(n) for n in ("pf", "pe", "mf", "me", "tf", "te", "df", "de"))
        s_sw, s_prod, s_rot, s_hi, s_high, s_lo, s_mq, s_mrow = (sem(n) for n in ("sw", "prod", "rot", "hi", "high", "lo", "mq", "mrow"))
        s_st, s_exp, s_pv, s_sum = sem("st"), sem("exp"), sem("pvd"), sem("sumd")
        s_osb, s_denc, s_recc, s_recd, s_rec, s_ot = (sem(n) for n in ("osb", "denc", "recc", "recd", "rec", "ot"))
        s_store = [sem(f"store{u}") for u in range(2)]
        s_idx, s_scat = sem("idx"), sem("scat")
        blk = ph.block()

        def run(e, prologue, body, tail):
            prologue()
            body(At(0, 0), None, 4)
            with e.Fori(0, NPAIR // 2 - 3) as it:
                for off in (1, 2):
                    i = At(it, off)
                    body(i, i.next(-1), 4)
            for n in range(NPAIR - 5, NPAIR):
                i = At(0, n)
                body(i, i.next(-1), NPAIR - 1 - n)
            tail(At(0, NPAIR - 1))

        @blk.sync
        def _(e):
            def load_qk(j):
                e.dma_start(wqk[j.u][:, :, :], io["wqk"][j.n() % HP, :, :, :]).then_inc(s_ldw[j.u], 16)
                e.dma_start(c[j.u][:, :, :], scr["c"][j.n() // HP, :, :, :].rearrange("j p s -> p j s")).then_inc(s_ldw[j.u], 16)

            def load_v(j):
                e.dma_start(v[j.u][:, :, :], scr["v"][j.n() // HP, j.n() % HP, :, :, :]).then_inc(s_ldv[j.u], 16)

            def swap_rows(j):
                wait_apart(e, s_rot, j.n(2, 0), s_apart_s)
                for w in range(2):
                    e.wait_ge(s_pe, j.n(NPROJ, NH2 * (w + 1)))
                    for o in range(2):
                        e.dma_start(swp[w][o:P:2, :], raw[w][1 - o:P:2, :]).then_inc(s_sw, 16)

            def max_rows(j):
                for h in range(2):
                    r = other[h].start
                    e.wait_ge(s_te, j.n(2, h + 1))
                    e.dma_start(qb[j.u][h][r:r + 1, :].bitcast(F32).rearrange("o (t q) -> o t q", q=P),
                                mneg[h][:, :].bitcast(F32)).then_inc(s_mrow, 16)

            def spread(i):
                e.wait_ge(s_de, i.n(2, 2))
                for h in range(2):
                    r = rows[h].start
                    e.dma_start(denc[:, h, :], den[r:r + 1, :].rearrange("o (p k) -> o p k", p=P)).then_inc(s_denc, 16)

            def broadcast(i):
                e.wait_ge(s_recc, i.n(1, 1))
                e.dma_start(scr["rec"][i.n(), :, :].rearrange("h (p k) -> p h k", p=P), recc[:, :, :]).then_inc(s_recd, 16)
                e.wait_ge(s_recd, i.n(16, 16))
                for h in range(2):
                    e.dma_start(rec[rows[h], :], scr["rec"][i.n(), h, :].unsqueeze(0).broadcast_to((DH, S))).then_inc(s_rec, 16)

            def store(i):
                e.wait_ge(s_ot, i.n(1, 1))
                e.dma_start(scr["o"][i.n(), :, :], oT[i.u][:, :]).then_inc(s_store[i.u], 16)

            def prologue():
                load_qk(At(0, 0))
                e.dma_start(cos[:, :], io["cos"]).then_inc(s_const, 16)
                e.dma_start(sin[:, :], io["sin"]).then_inc(s_const, 16)
                for s in s_store:
                    e.sem_inc(s, 16)
                load_qk(At(0, 1))
                load_v(At(0, 0))
                e.wait_ge(s_init, 2)
                e.wait_ge(s_pf, NPROJ)
                load_qk(At(0, 2))
                swap_rows(At(0, 0))
                e.wait_ge(s_pf, 2 * NPROJ)
                load_qk(At(0, 3))
                swap_rows(At(0, 1))
                max_rows(At(0, 0))
                swap_rows(At(0, 2))

            def body(i, prev, ahead):
                if ahead >= 4:
                    e.wait_ge(s_pf, i.n(NPROJ, 3 * NPROJ))
                    load_qk(i.next(4))
                if prev:
                    e.wait_ge(s_pv, i.n(KT, 0))
                if ahead:
                    load_v(i.next(1))
                if prev and ahead >= 2:
                    swap_rows(i.next(2))
                if prev:
                    spread(prev)
                    broadcast(prev)
                if ahead:
                    max_rows(i.next(1))
                if prev:
                    store(prev)

            def tail(i):
                spread(i)
                broadcast(i)
                store(i)
                for u in range(2):
                    e.wait_ge(s_store[u], 16 * (NPAIR // 2 + 1))

            run(e, prologue, body, tail)

        @blk.gpsimd
        def _(e):
            def body(i, *_):
                def sums(kt):
                    for h in range(2):
                        wait_apart(e, s_exp, i.n(TILES, 2 * kt + h + 1), s_apart)
                        acc = total[i.u][h][:, :]
                        if kt == 1:
                            wait_apart(e, s_df, i.n(2, -2), s_apart)
                            a0 = ex[h][:, :]
                        else:
                            wait_apart(e, s_sum, i.n(NSUM, 2 * (kt - 2) + h + 1), s_apart)
                            a0 = acc
                        e.tensor_tensor(out=acc, in0=a0, in1=ex[(2 * kt + h) % NP][:, :], op=ALU.add).then_inc(s_sum, 1)

                for kt in range(1, KT):
                    sums(kt)
                    if kt == 2:
                        wait_apart(e, s_scat, i.n(32, 0), s_apart)
                        e.tensor_copy(fill_i[:, :], keep["fill"][:, i.n(), :])
                        e.tensor_copy(tok_i[:, :], keep["tok"][:, bass.ds(i.n(), 1)]).then_inc(s_idx, 1)
                        wait_apart(e, s_idx, i.n(1, 1), s_apart)
                        for k in range(2):
                            e.indirect_dma_start(out=scr["table"], out_offset=bass.IndirectOffsetOnAxis(ap=fill_i[:, k:k + 1], axis=0),
                                                 in_=tok_i[:, :], in_offset=None, bounds_check=NSLOT - 1, oob_is_err=False).then_inc(s_scat, 16)

            run(e, lambda: None, body, lambda i: e.wait_ge(s_scat, 32 * NPAIR))

        @blk.vector
        def _(e):
            def rope(j):
                e.wait_ge(s_sw, j.n(64, 64))
                wait(e, s_hi, j.n(4, 0))
                wait(e, s_lo, j.n(4, 0))
                for w in range(2):
                    e.tensor_tensor(out=rot[w][:, :], in0=raw[w][:, :], in1=cos[:, :], op=ALU.mult).then_inc(s_prod, 1)
                for w in range(2):
                    e.tensor_tensor(out=swp[w][:, :], in0=swp[w][:, :], in1=sin[:, :], op=ALU.mult).then_inc(s_prod, 1)
                e.wait_ge(s_prod, j.n(4, 4))
                for w in (1, 0):
                    e.tensor_tensor(out=rot[w][:, :], in0=rot[w][:, :], in1=swp[w][:, :], op=ALU.add).then_inc(s_rot, 1)

            def split(j):
                e.wait_ge(s_rot, j.n(2, 2))
                wait(e, s_st, j.n(TILES, -TILES))
                for h in range(2):
                    for to, x in ((ka, 1), (qa, 0)):
                        e.tensor_copy(to[j.u][h][rows[h], :], rot[x][rows[h], :]).then_inc(s_high, 1)
                for h in range(2):
                    e.wait_ge(s_high, j.n(4, 2 * h + 1))
                    e.tensor_tensor(out=ka[j.u][h][other[h], :], in0=rot[1][rows[h], :], in1=ka[j.u][h][rows[h], :].bitcast(F32), op=ALU.subtract).then_inc(s_lo, 1)
                for h in range(2):
                    e.wait_ge(s_high, j.n(4, 2 * h + 2))
                    e.tensor_tensor(out=qb[j.u][h][rows[h], :], in0=rot[0][rows[h], :], in1=qa[j.u][h][rows[h], :].bitcast(F32), op=ALU.subtract).then_inc(s_lo, 1)

            def maxima(j, first, count):
                for m in range(first, first + count):
                    e.wait_ge(s_mf, j.n(NMAX, m + 1))
                    e.reduce_max(mx[:, m:m + 1], pfr[m % 2][:, :], AX.X).then_inc(s_me, 1)

            def join(j, h):
                e.wait_ge(s_me, j.n(NMAX, NMAX // 2 * (h + 1)))
                wait(e, s_tf, j.n(2, h - 1))
                m = mx[:, :].rearrange("p (h q n) -> p h n q", h=2, n=NH2)
                e.tensor_tensor(out=mq[h][:, :], in0=m[:, h, 0, :], in1=m[:, h, 1, :], op=ALU.max).then_inc(s_mq, 1)

            def recip(i):
                e.wait_ge(s_denc, i.n(32, 32))
                wait(e, s_recd, i.n(16, 0))
                e.reciprocal(recc[:, :, :], denc[:, :, :]).then_inc(s_recc, 1)

            def normalise(i):
                e.wait_ge(s_rec, i.n(32, 32))
                e.wait_ge(s_osb, i.n(1, 1))
                e.wait_ge(s_store[i.u], i.same(16, 16))
                e.tensor_tensor(out=oT[i.u][:, :], in0=osb[:, :], in1=rec[:, :], op=ALU.mult).then_inc(s_ot, 1)

            def front(j, prev):
                split(j)
                maxima(j, 0, NMAX // 2)
                join(j, 0)
                maxima(j, NMAX // 2, 8)
                if prev:
                    recip(prev)
                maxima(j, NMAX // 2 + 8, NMAX // 2 - 8)
                join(j, 1)

            def prologue():
                for u in range(2):
                    for h in range(2):
                        e.memset(qb[u][h][other[h], :].bitcast(F32), 0.0)
                        last = e.memset(kb[u][h][other[h], :].bitcast(F32), 0.0)
                e.memset(ones[:, :], 1.0)
                last.then_inc(s_init, 1)
                e.wait_ge(s_init, 1)
                for u in range(2):
                    for h in range(2):
                        r = other[h].start
                        last = e.memset(kb[u][h][r:r + 1, :].bitcast(F32), 1.0)
                last.then_inc(s_init, 1)
                e.wait_ge(s_const, 32)
                rope(At(0, 0))
                front(At(0, 0), None)
                rope(At(0, 1))

            def body(i, prev, ahead):
                if ahead:
                    front(i.next(1), prev)
                else:
                    recip(prev)
                if ahead >= 2:
                    rope(i.next(2))
                if prev:
                    normalise(prev)

            def tail(i):
                recip(i)
                normalise(i)

            run(e, prologue, body, tail)

        @blk.scalar
        def _(e):
            def exps(i, s):
                kt, h = s // 2, s % 2
                back = kt - NP // 2
                e.wait_ge(s_st, i.n(TILES, s + 1))
                wait(e, s_pv, i.n(KT, back + 1))
                wait(e, s_sum, i.n(NSUM, 2 * max(back - 1, 0) + h + 1 if back >= 0 else 2 * (back + KT - 1) + h + 1 - NSUM))
                e.activation(ex[s % NP][:, :], pst[s % 2][:, :], ACT.Exp, scale=SCALE).then_inc(s_exp, 1)

            def proj_copy(j, w):
                wait(e, s_prod, j.n(4, w - 3))
                for n in range(NH2):
                    e.wait_ge(s_pf, j.n(NPROJ, NH2 * w + n + 1))
                    e.activation(raw[w][:, bank[n]], pfr[n][:, :], ACT.Copy).then_inc(s_pe, 1)

            def query_high(j, h):
                e.wait_ge(s_rot, j.n(2, 2))
                if h == 0:
                    wait(e, s_st, j.n(TILES, -TILES))
                e.activation(qa[j.u][h][other[h], :], rot[0][rows[h], :], ACT.Copy).then_inc(s_hi, 1)

            def key_high(j, h):
                e.wait_ge(s_rot, j.n(2, 1))
                e.activation(kb[j.u][h][rows[h], :], rot[1][rows[h], :], ACT.Copy).then_inc(s_hi, 1)

            def out_copy(i):
                e.wait_ge(s_pv, i.n(KT, KT))
                wait(e, s_ot, i.n())
                e.activation(osb[:, :], ppv[:, :], ACT.Copy).then_inc(s_osb, 1)

            def den_copy(i):
                for n in range(NH2):
                    e.wait_ge(s_df, i.n(2, n + 1))
                    wait(e, s_denc, i.n(32, 0))
                    e.activation(den[:, bank[n]], pfr[n][:, :], ACT.Copy).then_inc(s_de, 1)

            def negate(j):
                for h in range(2):
                    e.wait_ge(s_tf, j.n(2, h + 1))
                    wait(e, s_mrow, j.n(32, 0))
                    e.activation(mneg[h][:, :], pfr[h][0:KT, 0:P], ACT.Copy, scale=-1.0).then_inc(s_te, 1)

            def prologue():
                for n in range(2):
                    for w in range(2):
                        proj_copy(At(0, n), w)
                for h in range(2):
                    query_high(At(0, 0), h)
                for h in range(2):
                    key_high(At(0, 0), h)
                negate(At(0, 0))
                for w in range(2):
                    proj_copy(At(0, 2), w)

            def body(i, prev, ahead):
                nxt, more = i.next(1), ahead >= 1
                for s in range(TILES):
                    exps(i, s)
                    if s == 0 and more:
                        query_high(nxt, 0)
                    if s == 1 and prev:
                        if ahead >= 2:
                            proj_copy(i.next(2), 1)
                        out_copy(prev)
                    if s == 3 and prev:
                        den_copy(prev)
                    if s == 4 and more:
                        query_high(nxt, 1)
                    if s in (6, 8) and more:
                        key_high(nxt, s // 8)
                    if s == 13 and more:
                        negate(nxt)
                if ahead >= 3:
                    proj_copy(i.next(3), 0)

            def tail(i):
                out_copy(i)
                den_copy(i)

            run(e, prologue, body, tail)

        @blk.tensor
        def _(e):
            def scores(i, s):
                kt, h = s // 2, s % 2
                if s < 2:
                    e.wait_ge(s_mrow, i.n(32, 32))
                    e.wait_ge(s_hi, i.n(4, 4))
                    e.wait_ge(s_lo, i.n(4, 4))
                wait(e, s_exp, i.n(TILES, s - 1))
                keys = slice(kt * P, (kt + 1) * P)
                for ww, (kk, qq) in enumerate(((ka, qa), (kb, qb))):
                    for n in range(NH2):
                        mm = e.matmul(pst[s % 2][:, bank[n]], kk[i.u][h][:, keys], qq[i.u][h][:, bank[n]], start=(ww == 0), stop=(ww == 1))
                    if ww == 1:
                        mm.then_inc(s_st, 1)
                    yield

            def values(i, kt):
                if kt == 0:
                    e.wait_ge(s_ldv[i.u], i.same(16, 16))
                    wait(e, s_osb, i.n())
                e.wait_ge(s_exp, i.n(TILES, 2 * kt + 2))
                for n in range(NH2):
                    for h in range(2):
                        mm = e.matmul(ppv[rows[h], bank[n]], v[i.u][:, kt, rows[h]], ex[(2 * kt + h) % NP][:, bank[n]],
                                      start=(kt == 0), stop=(kt == KT - 1))
                    if n == NH2 - 1:
                        mm.then_inc(s_pv, 1)
                    yield

            def denominators(i, emptied):
                e.wait_ge(s_sum, i.n(NSUM, NSUM))
                e.wait_ge(*emptied)
                for n in range(NH2):
                    for h in range(2):
                        mm = e.matmul(pfr[n][rows[h], :], ones[:, :], total[i.u][h][:, bank[n]], start=True, stop=True)
                    mm.then_inc(s_df, 1)
                    yield

            def project(j, w, emptied=None):
                if w == 0:
                    e.wait_ge(s_ldw[j.u], j.same(32, 32))
                    wait(e, *emptied)
                for n in range(NH2):
                    if w:
                        e.wait_ge(s_pe, j.n(NPROJ, n + 1))
                    e.matmul(pfr[n][:, :], wqk[j.u][:, w, :], c[j.u][:, w, bank[n]], start=True, stop=True).then_inc(s_pf, 1)
                    yield

            def max_scores(j, m, emptied):
                h, qt, n = m // (KT * NH2), m // NH2 % KT, m % NH2
                if m % (KT * NH2) == 0:
                    e.wait_ge(s_hi, j.n(4, h + 1))
                    e.wait_ge(s_lo, j.n(4, h + 1))
                if emptied:
                    e.wait_ge(*emptied)
                else:
                    e.wait_ge(s_me, j.n(NMAX, m - 1))
                e.matmul(pfr[m % 2][:, :], qa[j.u][h][:, qt * P:(qt + 1) * P], ka[j.u][h][:, bank[n]], start=True, stop=True).then_inc(s_mf, 1)

            def turn_maxima(j, h):
                e.wait_ge(s_mq, j.n(2, 2))
                e.transpose(pfr[h][0:KT, 0:P], mq[h][:, :], keep["ident"][:, :]).then_inc(s_tf, 1)

            def front(i, prev, ahead):
                j = i.next(1)
                if prev and ahead >= 2:
                    yield from project(i.next(2), 1)
                    last = (s_pe, i.n(NPROJ, 3 * NPROJ))
                else:
                    yield from (None,) * NH2
                    last = (s_te, i.n(2, 2))
                if prev:
                    yield from denominators(prev, last)
                    last = (s_de, i.n(2, 0))
                else:
                    yield from (None,) * NH2
                    last = (s_pe, 3 * NPROJ)
                if ahead:
                    for m in range(NMAX):
                        max_scores(j, m, last if m < 2 else None)
                        yield
                    for h in range(2):
                        turn_maxima(j, h)
                        yield
                if ahead >= 3:
                    yield from project(i.next(3), 0, (s_te, j.n(2, 2)))

            def drain(g):
                for _ in g:
                    pass

            def prologue():
                for n in range(2):
                    drain(project(At(0, n), 0, (s_pe, n * NPROJ)))
                    drain(project(At(0, n), 1))
                for m in range(NMAX):
                    max_scores(At(0, 0), m, (s_pe, 2 * NPROJ) if m < 2 else None)
                for h in range(2):
                    turn_maxima(At(0, 0), h)
                drain(project(At(0, 2), 0, (s_te, 2)))
                drain(project(At(0, 2), 1))

            PLAN = [(0, 0, 1, 1), (1, 1, 1, 1), (2, 2, 2, 2), (2, 2, 2, 2),
                    (2, 2, 2, 2), (2, 2, 1, 1), (0, 0, 1, 1), (0, 0, 1, 1)]
            assert sum(map(sum, PLAN)) == NMAX + 2 + NH2 + NPROJ

            def body(i, prev, ahead):
                work = front(i, prev, ahead)
                for kt in range(KT):
                    plan = list(PLAN[kt]) if ahead else [0, 0, 0, 4 * (kt == 2)]

                    def some():
                        for _ in range(plan.pop(0)):
                            next(work, None)

                    for h in range(2):
                        drain(scores(i, 2 * kt + h))
                        some()
                    if kt or prev:
                        for _ in values(*((i, kt - 1) if kt else (prev, KT - 1))):
                            some()
                    else:
                        some()
                        some()
                drain(work)

            def tail(i):
                drain(values(i, KT - 1))
                drain(denominators(i, (s_de, i.n(2, 0))))

            run(e, prologue, body, tail)


def experts_phase(nc, io, scr, keep):
    with ExitStack() as ctx:
        ph = Phase(nc, ctx, "ex")
        sb, ps, sem = ph.sb, ph.ps, ph.sem
        STEPS = NE // 2 * PARTS
        HL = 2
        PASSES = ((0, 0), (0, 1), (1, 0))
        raw = [sb(f"raw{q}", [P, KD * FF + NF * D]) for q in range(2)]
        w1 = [sb(f"w1{q}", [P, HL, KD, FF], F32R) for q in range(2)]
        w2 = [sb(f"w2{q}", [P, HL, NF, D], F32R) for q in range(2)]
        slots = sb("slots", [SLOT_P, NE, SLOT_T], I32)
        idx = [sb(f"idx{q}", [SLOT_P, PART_T], I32) for q in range(2)]
        xg = [sb(f"xg{q}", [SLOT_P, PART_T, D]) for q in range(2)]
        xT = [sb(f"xT{q}", [P, HL, KD, PW], F32R) for q in range(2)]
        hs = sb("hs", [P, NF, PW])
        hT = [sb(f"hT{q}", [P, HL, NF, PW], F32R) for q in range(2)]
        out = [sb(f"out{q}", [SLOT_P, PART_T, D]) for q in range(2)]
        ptr = ps("tr", [P, KD, HALF])
        phid = [ps(f"h{k}", [P, HALF]) for k in range(2)]
        po = ps("o", [P, PART_T, HALF])
        s_w = [sem(f"w{q}") for q in range(2)]
        s_g = [sem(f"g{q}") for q in range(2)]
        s_os = [sem(f"os{q}") for q in range(2)]
        s_split = [sem(f"split{q}") for q in range(2)]
        s_apart = sem("apart")
        s_slots, s_idx, s_tr, s_xh, s_xT, s_h, s_silu, s_hh, s_hT, s_o, s_oe = (
            sem(n) for n in ("slots", "idx", "tr", "xh", "xT", "h", "silu", "hh", "hT", "o", "oe"))
        blk = ph.block()

        @blk.sync
        def _(e):
            e.dma_start(slots[:, :, :], scr["table"].rearrange("(e p t) o -> p e (t o)", e=NE, p=SLOT_P)).then_inc(s_slots, 16)

            def load(expert, q):
                e.dma_start(raw[q][:, 0:KD * FF].rearrange("p (k f) -> p k f", k=KD), io["w1"][expert, :, :].rearrange("(k p) f -> p k f", p=P)).then_inc(s_w[q], 16)
                e.dma_start(raw[q][:, KD * FF:].rearrange("p (k d) -> p k d", k=NF), io["w2"][expert, :, :].rearrange("(k p) d -> p k d", p=P)).then_inc(s_w[q], 16)

            for q in range(2):
                load(q, q)
            with e.Fori(1, NE // 2) as pr:
                for q in range(2):
                    e.wait_ge(s_split[q], pr * 4)
                    load(pr * 2 + q, q)

        @blk.gpsimd
        def _(e):
            e.wait_ge(s_slots, 16)

            def gather(n, q, first):
                a = At(n, q)
                if not first:
                    wait_apart(e, s_tr, a.n(1, -1), s_apart)
                col = (n // PARTS) * (2 * SLOT_T) + (n % PARTS) * PART_T + q * SLOT_T
                e.tensor_copy(idx[q][:, :], slots[:, :, :].rearrange("p e t -> p (e t)")[:, bass.ds(col, PART_T)]).then_inc(s_idx, 1)
                wait_apart(e, s_idx, a.n(1, 1), s_apart)
                for c in range(PART_T):
                    e.indirect_dma_start(out=xg[q][:, c, :], out_offset=None, in_=scr["xn"].rearrange("b s d -> (b s) d"),
                                         in_offset=bass.IndirectOffsetOnAxis(ap=idx[q][:, c:c + 1], axis=0)).then_inc(s_g[q], 16)

            for q in range(2):
                gather(0, q, True)
            with e.Fori(1, STEPS) as n:
                for q in range(2):
                    gather(n, q, False)

        @blk.vector
        def _(e):
            def split_weights(pr, q):
                e.wait_ge(s_w[q], pr * 32 + 32)
                wait(e, s_o, pr * (2 * PARTS) + (q - 1) if not isinstance(pr, int) or pr else 0)
                n1 = KD * FF
                flat = ((w1[q][:, :, :, :].rearrange("p s k f -> p s (k f)"), raw[q][:, 0:n1]),
                        (w2[q][:, :, :, :].rearrange("p s k d -> p s (k d)"), raw[q][:, n1:]))
                for halves, src in flat:
                    e.tensor_copy(halves[:, 0, :], src).then_inc(s_split[q], 1)
                e.wait_ge(s_split[q], pr * 4 + 2)
                for halves, src in flat:
                    e.tensor_tensor(out=halves[:, 1, :], in0=src, in1=halves[:, 0, :].bitcast(F32), op=ALU.subtract).then_inc(s_split[q], 1)

            def turned(a):
                e.wait_ge(s_tr, a.n(1, 1))
                wait(e, s_h, a.n(NF, -NF))
                e.tensor_copy(xT[a.u][:, 0, :, :], ptr[:, :, 0:PW]).then_inc(s_xh, 1)
                e.wait_ge(s_xh, a.n(1, 1))
                e.tensor_tensor(out=xT[a.u][:, 1, :, :], in0=ptr[:, :, 0:PW], in1=xT[a.u][:, 0, :, :].bitcast(F32), op=ALU.subtract).then_inc(s_xT, 1)

            def hidden(a):
                q = a.u
                for f in range(0, NF, 2):
                    e.wait_ge(s_silu, a.n(NF, f + 2))
                    if f == 0:
                        wait(e, s_o, a.n(1, -1))
                    e.tensor_copy(hT[q][:, 0, f:f + 2, :], hs[:, f:f + 2, :]).then_inc(s_hh, 1)
                    e.wait_ge(s_hh, a.n(NF // 2, f // 2 + 1))
                    e.tensor_tensor(out=hT[q][:, 1, f:f + 2, :], in0=hs[:, f:f + 2, :], in1=hT[q][:, 0, f:f + 2, :].bitcast(F32), op=ALU.subtract).then_inc(s_hT, 1)

            def outputs(a):
                e.wait_ge(s_os[a.u], a.same(16, 16))
                e.wait_ge(s_o, a.n(1, 1))
                e.tensor_copy(out[a.u][:, :, :], po[0:SLOT_P, :, 0:D]).then_inc(s_oe, 1)

            turned(At(0, 0))
            split_weights(0, 0)
            split_weights(0, 1)

            def parts(n, last_of_pair):
                hidden(At(n, 0))
                turned(At(n, 1))
                outputs(At(n, 0))
                hidden(At(n, 1))
                if not last_of_pair:
                    turned(At(n, 2))
                    outputs(At(n, 1))

            parts(0, False)
            with e.Fori(1, PARTS - 1) as n:
                parts(n, False)

            def seam(pr):
                n = pr * PARTS + (PARTS - 1)
                hidden(At(n, 0))
                turned(At(n, 1))
                outputs(At(n, 0))
                split_weights(pr + 1, 0)
                hidden(At(n, 1))
                turned(At(n, 2))
                outputs(At(n, 1))
                split_weights(pr + 1, 1)

            with e.Fori(0, NE // 2 - 1) as pr:
                seam(pr)
                with e.Fori(0, PARTS - 1) as g:
                    parts(pr * PARTS + g + PARTS, False)
            parts(STEPS - 1, True)
            outputs(At(STEPS - 1, 1))

        @blk.scalar
        def _(e):
            for q in range(2):
                e.sem_inc(s_os[q], 16)

            def silus(a):
                for f in range(NF):
                    e.wait_ge(s_h, a.n(NF, f + 1))
                    wait(e, s_hT, a.n(NF // 2, f // 2 + 1 - NF // 2))
                    e.activation(hs[:, f, :], phid[f % 2][:, 0:PW], ACT.Silu).then_inc(s_silu, 1)

            def store(n, q):
                a = At(n, q)
                e.wait_ge(s_oe, a.n(1, 1))
                dst = scr["eo"].rearrange("(e p g c) d -> e g p (c d)", e=NE, p=SLOT_P, g=PARTS)
                e.dma_start(dst[(n // PARTS) * 2 + q, n % PARTS, :, :], out[q][:, :, :].rearrange("p c d -> p (c d)")).then_inc(s_os[q], 16)

            silus(At(0, 0))
            silus(At(0, 1))
            with e.Fori(1, STEPS) as n:
                silus(At(n, 0))
                store(n - 1, 0)
                silus(At(n, 1))
                store(n - 1, 1)
            store(STEPS - 1, 0)
            store(STEPS - 1, 1)
            for q in range(2):
                e.wait_ge(s_os[q], 16 * (STEPS + 1))

        @blk.tensor
        def _(e):
            def turn(a, first=False):
                e.wait_ge(s_g[a.u], a.same(48, 48))
                if not first:
                    e.wait_ge(s_xT, a.n())
                for c in range(PART_T):
                    for k in range(KD):
                        mm = e.transpose(ptr[:, k, c * SLOT_P:(c + 1) * SLOT_P], xg[a.u][:, c, k * P:(k + 1) * P], keep["ident"][0:SLOT_P, 0:SLOT_P])
                mm.then_inc(s_tr, 1)

            def hidden(n, q):
                a = At(n, q)
                e.wait_ge(s_split[q], (n // PARTS) * 4 + 4)
                e.wait_ge(s_xT, a.n(1, 1))
                for f in range(NF):
                    wait(e, s_silu, a.n(NF, f - 1))
                    for ws, xs in PASSES:
                        for k in range(KD):
                            mm = e.matmul(phid[f % 2][:, 0:PW], w1[q][:, ws, k, f * P:(f + 1) * P], xT[q][:, xs, k, :],
                                          start=(ws + xs + k == 0), stop=(ws == 1 and k == KD - 1))
                    mm.then_inc(s_h, 1)

            def down(n, q, first=False):
                a = At(n, q)
                if not first:
                    e.wait_ge(s_oe, a.n())
                for c in range(PART_T):
                    for f in range(NF):
                        if c == 0 and f % 2 == 0:
                            e.wait_ge(s_hT, a.n(NF // 2, f // 2 + 1))
                        for hh, ws in PASSES:
                            mm = e.matmul(po[0:SLOT_P, c, 0:D], hT[q][:, hh, f, c * SLOT_P:(c + 1) * SLOT_P], w2[q][:, ws, f, :],
                                          start=(hh + ws + f == 0), stop=(hh == 1 and f == NF - 1))
                mm.then_inc(s_o, 1)

            turn(At(0, 0), True)
            hidden(0, 0)
            turn(At(0, 1))
            down(0, 0, True)
            hidden(0, 1)
            turn(At(0, 2))
            down(0, 1)
            with e.Fori(1, STEPS - 1) as n:
                hidden(n, 0)
                turn(At(n, 1))
                down(n, 0)
                hidden(n, 1)
                turn(At(n, 2))
                down(n, 1)
            hidden(STEPS - 1, 0)
            turn(At(STEPS - 1, 1))
            down(STEPS - 1, 0)
            hidden(STEPS - 1, 1)
            down(STEPS - 1, 1)


def combine_phase(nc, io, scr, keep):
    with ExitStack() as ctx:
        ph = Phase(nc, ctx, "cb")
        sb, ps, sem = ph.sb, ph.ps, ph.sem
        oT = [sb(f"oT{u}", [P, HP, S]) for u in range(2)]
        x = [sb(f"x{u}", [P, TB, D]) for u in range(2)]
        xn = [sb(f"xn{u}", [P, TB, D]) for u in range(2)]
        res = [sb(f"res{u}", [P, TB, D]) for u in range(2)]
        wo = sb("wo", [P, HP, D])
        NG = 4
        idx = [sb(f"idx{k}", [P, 2], I32) for k in range(NG)]
        eo = [[sb(f"eo{k}{j}", [P, D]) for j in range(2)] for k in range(NG)]
        att = [sb(f"att{k}", [P, D]) for k in range(2)]
        mix = [sb(f"mix{k}", [P, D]) for k in range(2)]
        gate = [sb(f"gate{k}", [P, D]) for k in range(2)]
        g2 = sb("g2", [P, TB, 2])
        pj = [ps(f"pj{k}", [P, HALF]) for k in range(2)]
        s_wo, s_pj, s_att, s_mix, s_silu, s_res, s_idx, s_g2 = (sem(n) for n in ("wo", "pj", "att", "mix", "silu", "res", "idx", "g2"))
        s_apart = sem("apart")
        s_ld = [sem(f"ld{u}") for u in range(2)]
        s_g = [sem(f"rows{k}") for k in range(NG)]
        s_st = [sem(f"st{u}") for u in range(2)]
        blk = ph.block()

        @blk.sync
        def _(e):
            e.dma_start(wo[:, :, :], io["woT"].rearrange("(r p) d -> p r d", p=P)).then_inc(s_wo, 16)

            def load(a):
                e.dma_start(oT[a.u][:, :, :], scr["o"].rearrange("(b r) p s -> b p r s", r=HP)[a.n(), :, :, :]).then_inc(s_ld[a.u], 16)
                e.dma_start(xn[a.u][:, :, :], scr["xn"][a.n(), :, :].rearrange("(t p) d -> p t d", p=P)).then_inc(s_ld[a.u], 16)
                e.dma_start(x[a.u][:, :, :], io["x"][a.n(), :, :].rearrange("(t p) d -> p t d", p=P)).then_inc(s_ld[a.u], 16)

            def store(a):
                e.wait_ge(s_res, a.n(TB, TB + 2))
                e.dma_start(io["out"][a.n(), :, :].rearrange("(t p) d -> p t d", p=P), res[a.u][:, :, :]).then_inc(s_st[a.u], 16)

            for u in range(2):
                e.sem_inc(s_st[u], 16)
                load(At(0, u))
            with e.Fori(0, NBATCH // 2 - 1) as it:
                for u in range(2):
                    store(At(it, u))
                    load(At(it, u + 2))
            for u in range(2):
                store(At(0, NBATCH - 2 + u))
            for u in range(2):
                e.wait_ge(s_st[u], 16 * (NBATCH // 2 + 1))

        @blk.gpsimd
        def _(e):
            def gather(b, t, first):
                k = t % NG
                if not first:
                    wait_apart(e, s_mix, b * (2 * TB) + 2 * (t - NG + 1), s_apart)
                e.tensor_copy(idx[k][:, :], keep["read"][:, b * TB + t, :]).then_inc(s_idx, 1)
                wait_apart(e, s_idx, b * TB + (t + 1), s_apart)
                for j in range(2):
                    e.indirect_dma_start(out=eo[k][j][:, :], out_offset=None, in_=scr["eo"],
                                         in_offset=bass.IndirectOffsetOnAxis(ap=idx[k][:, j:j + 1], axis=0)).then_inc(s_g[k], 16)

            e.wait_ge(s_wo, 16)
            for t in range(TB):
                gather(0, t, t < NG)
            with e.Fori(1, NBATCH) as b:
                for t in range(TB):
                    gather(b, t, False)

        @blk.vector
        def _(e):
            def tile(a, t):
                u, k = a.u, t % 2
                e.wait_ge(s_res, a.n(TB, t + 1))
                e.wait_ge(s_pj, a.n(TB, t + 1))
                e.tensor_tensor(out=att[k][:, :], in0=pj[k][:, 0:D], in1=xn[u][:, t, :], op=ALU.add).then_inc(s_att, 1)
                e.wait_ge(s_g[t % NG], a.n(2 * 32, 32 + 32 * (t // NG)))
                e.scalar_tensor_tensor(out=mix[k][:, :], in0=eo[t % NG][0][:, :], scalar=g2[:, t, 0:1], in1=xn[u][:, t, :], op0=ALU.mult, op1=ALU.add).then_inc(s_mix, 1)
                e.wait_ge(s_mix, a.n(2 * TB, 2 * t + 1))
                e.scalar_tensor_tensor(out=mix[k][:, :], in0=eo[t % NG][1][:, :], scalar=g2[:, t, 1:2], in1=mix[k][:, :], op0=ALU.mult, op1=ALU.add).then_inc(s_mix, 1)

            def finish(a, t):
                u, k = a.u, t % 2
                e.wait_ge(s_silu, a.n(TB, t + 1))
                e.wait_ge(s_att, a.n(TB, t + 1))
                e.tensor_tensor(out=att[k][:, :], in0=att[k][:, :], in1=gate[k][:, :], op=ALU.mult).then_inc(s_g2, 1)
                e.wait_ge(s_g2, a.n(TB + 1, t + 2))
                e.tensor_tensor(out=res[u][:, t, :], in0=att[k][:, :], in1=x[u][:, t, :], op=ALU.add).then_inc(s_res, 1)

            def batch(a):
                e.wait_ge(s_ld[a.u], a.same(48, 48))
                e.wait_ge(s_st[a.u], a.same(16, 16))
                e.tensor_copy(g2[:, :, :], keep["gate"][:, bass.ds(a.n(TB), TB), :]).then_inc(s_g2, 1)
                e.wait_ge(s_g2, a.n(TB + 1, 1))
                for t in range(TB):
                    tile(a, t)
                    if t:
                        finish(a, t - 1)
                finish(a, TB - 1)

            e.sem_inc(s_res, 2)
            with e.Fori(0, NBATCH // 2) as it:
                for u in range(2):
                    batch(At(it, u))

        @blk.scalar
        def _(e):
            with e.Fori(0, NBATCH) as b:
                for t in range(TB):
                    e.wait_ge(s_mix, b * (2 * TB) + 2 * (t + 1))
                    e.activation(gate[t % 2][:, :], mix[t % 2][:, :], ACT.Silu).then_inc(s_silu, 1)

        @blk.tensor
        def _(e):
            e.wait_ge(s_wo, 16)

            def tile(a, t, first):
                if t == 0:
                    e.wait_ge(s_ld[a.u], a.same(48, 48))
                if not first:
                    e.wait_ge(s_att, a.n(TB, t - 1))
                for r in range(HP):
                    mm = e.matmul(pj[t % 2][:, 0:D], oT[a.u][:, r, t * P:(t + 1) * P], wo[:, r, :], start=(r == 0), stop=(r == HP - 1))
                mm.then_inc(s_pj, 1)

            for u in range(2):
                for t in range(TB):
                    tile(At(0, u), t, u == 0 and t < 2)
            with e.Fori(1, NBATCH // 2) as it:
                for u in range(2):
                    for t in range(TB):
                        tile(At(it, u), t, False)


def build(nc, io):
    with ExitStack() as ctx:
        def scratch(name, shape, dt=F32):
            return nc.dram_tensor(f"scr_{name}", shape, dt, kind="Internal").ap()

        scr = {
            "xn": scratch("xn", [NBATCH, S, D]),
            "c": scratch("c", [NBATCH, 2, DL, S]),
            "v": scratch("v", [NBATCH, HP, P, KT, P]),
            "o": scratch("o", [NPAIR, P, S]),
            "rec": scratch("rec", [NPAIR, 2, S]),
            "table": scratch("table", [NSLOT, 1], I32),
            "eo": scratch("eo", [NSLOT, D]),
        }

        def sb(name, shape, dt=F32):
            return ctx.enter_context(nc.sbuf_tensor(f"keep_{name}", shape, dt))

        keep = {
            "ident": sb("ident", [P, P]),
            "logits": sb("logits", [P, NT * NE]),
            "tok": sb("tok", [P, NT], I32),
            "gate": sb("gate", [P, NT, 2]),
            "fill": sb("fill", [P, NT, 2], I32),
            "read": sb("read", [P, NT, 2], I32),
        }
        project_phase(nc, io, scr, keep)
        route_phase(nc, io, scr, keep)
        attend_phase(nc, io, scr, keep)
        experts_phase(nc, io, scr, keep)
        combine_phase(nc, io, scr, keep)


def shape_constants():
    inv_freq = 1.0 / 10000.0 ** (np.arange(0, DH, 2, dtype=np.float32) / DH)
    freqs = np.outer(np.arange(S, dtype=np.float32), inv_freq).astype(np.float32)
    cos = np.concatenate([np.cos(freqs), np.cos(freqs)], -1)[:, ::2].astype(np.float32)
    sin = np.concatenate([np.sin(freqs), np.sin(freqs)], -1)[:, ::2].astype(np.float32)
    dim = np.arange(P) % DH
    e = np.tile(np.arange(NE, dtype=np.float32), NT)
    return {
        "cos": np.ascontiguousarray(cos.T[dim // 2]),
        "sin": np.ascontiguousarray(sin.T[dim // 2] * np.where(dim % 2 == 0, -1.0, 1.0).astype(np.float32)[:, None]),
        "ident": np.eye(P, dtype=np.float32),
        "tri": np.triu(np.ones((P, P), np.float32), 1),
        "rev": np.broadcast_to(NE - e, (P, NT * NE)).copy(),
        "ebase": np.broadcast_to(e * CAPP, (P, NT * NE)).copy(),
        "newe": np.broadcast_to((np.arange(NT * NE) % NT != 0).astype(np.float32), (P, NT * NE)).copy(),
        "tok": (np.arange(NT)[None, :] * P + np.arange(P)[:, None]).astype(np.int32),
    }


def kernel(**inputs):
    import concourse.bacc as bacc
    from concourse.bass_utils import run_bass_kernel_spmd

    a = {k: np.asarray(v) for k, v in inputs.items()}

    def pairs(w):
        return w.reshape(HP, P, DL).transpose(0, 2, 1)

    wq, wk = pairs(a["L0_attn_w_up_q"]), pairs(a["L0_attn_w_up_k"])
    arrays = {
        "x": a["L0_attn_x"],
        "wdqT": a["L0_attn_w_down_q"].T,
        "wdkvT": a["L0_attn_w_down_kv"].T,
        "wqk": np.stack([wq, wk], axis=2),
        "wvT": a["L0_attn_w_up_v"].T,
        "woT": a["L0_attn_w_out"].T,
        "lnp": np.stack([a["L0_attn_ln_scale"].reshape(KD, P).T, a["L0_attn_ln_bias"].reshape(KD, P).T], axis=2),
        "rwT": a["L0_ffn_router_w"].T,
        "w1": a["L0_ffn_w1"],
        "w2": a["L0_ffn_w2"],
        **shape_constants(),
    }
    arrays = {k: np.ascontiguousarray(v) for k, v in arrays.items()}
    nc = bacc.Bacc("TRN2", target_bir_lowering=False, num_devices=1)
    io = {k: nc.dram_tensor(f"in_{k}", v.shape, mybir.dt.from_np(v.dtype), kind="ExternalInput").ap() for k, v in arrays.items()}
    io["out"] = nc.dram_tensor("out_0", [NBATCH, S, D], F32, kind="ExternalOutput").ap()
    build(nc, io)
    r = run_bass_kernel_spmd(nc, [{f"in_{k}": v for k, v in arrays.items()}], core_ids=[0])
    return r.results[0]["out_0"]
```

```python
from contextlib import ExitStack

import numpy as np
import concourse.bass as bass
from concourse import mybir

F32, F32R, I32 = mybir.dt.float32, mybir.dt.float32r, mybir.dt.int32
ALU, ACT, AX = mybir.AluOpType, mybir.ActivationFunctionType, mybir.AxisListType

P = 128
NBATCH, S, D = 8, 1024, 256
H, DH, DL = 16, 64, 128
NE, FF = 8, 1024
NTOK = NBATCH * S
NT = NTOK // P
TB = S // P
KD = D // P
HALF = 512
NH2 = S // HALF
HP = H // 2
NPAIR = NBATCH * HP
KT = S // P
CAP = int(1.25 * NTOK * 2 / NE) + 1
SLOT_P = 122
SLOT_T = 21
CAPP = SLOT_P * SLOT_T
PART_T = 3
PARTS = SLOT_T // PART_T
PW = PART_T * SLOT_P
NF = FF // P
NSLOT = NE * CAPP
EPS = 1e-5
FAR = float(1 << 20)
SCALE = 1.0 / 8.0


class At:

    def __init__(self, base, off):
        self.base, self.off, self.u = base, off, off % 2

    def n(self, k=1, add=0):
        return self.base * (2 * k) + (self.off * k + add)

    def same(self, k, add=0):
        return self.base * k + ((self.off // 2) * k + add)

    def next(self, d):
        return At(self.base, self.off + d)


def wait(eng, sem, value):
    if not (isinstance(value, int) and value <= 0):
        eng.wait_ge(sem, value)


def wait_apart(eng, sem, value, own):
    wait(eng, sem, value)
    eng.sem_inc(own, 1)


class Phase:

    def __init__(self, nc, ctx, tag):
        self.nc, self.ctx, self.tag = nc, ctx, tag

    def sb(self, name, shape, dt=F32):
        return self.ctx.enter_context(self.nc.sbuf_tensor(f"{self.tag}_{name}", shape, dt))

    def ps(self, name, shape):
        return self.ctx.enter_context(self.nc.psum_tensor(f"{self.tag}_{name}", shape, F32))

    def sem(self, name):
        return self.ctx.enter_context(self.nc.semaphore(f"{self.tag}_{name}"))

    def block(self):
        return self.ctx.enter_context(self.nc.Block())


def project_phase(nc, io, scr, keep):
    with ExitStack() as ctx:
        ph = Phase(nc, ctx, "pj")
        sb, ps, sem = ph.sb, ph.ps, ph.sem
        xin = [sb(f"xin{u}", [P, TB, D]) for u in range(2)]
        xn = [sb(f"xn{u}", [P, TB, D]) for u in range(2)]
        h = sb("h", [P, TB, D])
        stats = sb("stats", [P, TB, 6])
        mv = sb("mv", [P, TB, 2])
        rstd, veps, minus_half = (sb(n, [P, TB]) for n in ("rstd", "veps", "minus_half"))
        xnT = sb("xnT", [P, KD, S])
        hT = sb("hT", [P, KD, S])
        csb = [sb(f"c{u}", [P, 2, S]) for u in range(2)]
        vsb = [sb(f"v{k}", [P, H * DH]) for k in range(4)]
        wd = sb("wd", [P, 2, KD, DL])
        ckv = [sb(f"ckv{w}", [P, S], F32R) for w in range(2)]
        wvraw = sb("wvraw", [DL, H * DH])
        wv = [sb(f"wv{w}", [DL, H * DH], F32R) for w in range(2)]
        rw = sb("rw", [P, KD, NE])
        lnp = sb("lnp", [P, KD, 2])
        pa = [ps(f"pa{k}", [P, S]) for k in range(2)]
        lg = ps("lg", [P, TB, NE])
        s_const, s_ln, s_pa, s_lgf, s_lgd = (sem(n) for n in ("const", "ln", "pa", "lgf", "lgd"))
        s_eps, s_apart, s_apart_v = sem("eps"), sem("apart"), sem("apart_v")
        s_x = [sem(f"x{u}") for u in range(2)]
        s_xs = [sem(f"xs{u}") for u in range(2)]
        s_cs = [sem(f"cs{u}") for u in range(2)]
        s_vs = [sem(f"vs{k}") for k in range(4)]
        s_act = sem("act")
        s_wh, s_wl, s_ch, s_cl = (sem(n) for n in ("wh", "wl", "ch", "cl"))
        blk = ph.block()
        NCONST = 16 * 6
        XNT, HT, CKV, CQ, V = 0, 2, 4, 5, 6
        ITEMS = V + TB
        PASSES = ((0, 0), (0, 1), (1, 0))

        def emptied(a, k):
            return a.n(ITEMS, k + 3)

        @blk.sync
        def _(e):
            e.dma_start(keep["ident"][:, :], io["ident"]).then_inc(s_const, 16)
            e.dma_start(rw[:, :, :], io["rwT"].rearrange("(k p) e -> p k e", p=P)).then_inc(s_const, 16)
            e.dma_start(wd[:, 0, :, :], io["wdqT"].rearrange("(k p) m -> p k m", p=P)).then_inc(s_const, 16)
            e.dma_start(wd[:, 1, :, :], io["wdkvT"].rearrange("(k p) m -> p k m", p=P)).then_inc(s_const, 16)
            e.dma_start(wvraw[:, :], io["wvT"]).then_inc(s_const, 16)
            e.dma_start(lnp[:, :, :], io["lnp"]).then_inc(s_const, 16)
            for s in s_xs:
                e.sem_inc(s, 16)
            for s in s_cs:
                e.sem_inc(s, 32)
            for s in s_vs:
                e.sem_inc(s, 16)
            with e.Fori(0, NBATCH // 2) as it:
                for u in range(2):
                    a = At(it, u)
                    e.wait_ge(s_ln, a.n(8, 4))
                    e.dma_start(scr["xn"][a.n(), :, :].rearrange("(t p) d -> p t d", p=P), xn[u][:, :, :]).then_inc(s_xs[u], 16)
                    for j, k in ((1, CKV), (0, CQ)):
                        e.wait_ge(s_act, emptied(a, k))
                        e.dma_start(scr["c"][a.n(), j, :, :], csb[u][:, j, :]).then_inc(s_cs[u], 16)
                    for t in range(TB):
                        e.wait_ge(s_act, emptied(a, V + t))
                        e.dma_start(scr["v"][a.n(), :, :, t, :].rearrange("r p m -> p r m"),
                                    vsb[t % 4][:, :].rearrange("p (r m) -> p r m", r=HP)).then_inc(s_vs[t % 4], 16)
            for s in s_xs:
                e.wait_ge(s, 16 * (NBATCH // 2 + 1))
            for s in s_cs:
                e.wait_ge(s, 32 * (NBATCH // 2 + 1))
            for s in s_vs:
                e.wait_ge(s, 16 * (2 * NBATCH + 1))

        @blk.gpsimd
        def _(e):
            def load(a):
                e.dma_start(xin[a.u][:, :, :], io["x"][a.n(), :, :].rearrange("(t p) d -> p t d", p=P)).then_inc(s_x[a.u], 16)

            def deviations(a, k):
                wait_apart(e, s_ln, a.n(8, k + 2), s_apart)
                e.tensor_scalar(veps[:, :], mv[:, :, 1], EPS, None, ALU.add).then_inc(s_eps, 1)
                wait_apart(e, s_eps, a.n(2, k // 4 + 2), s_apart)
                e.tensor_tensor(out=rstd[:, :], in0=veps[:, :], in1=minus_half[:, :], op=ALU.pow).then_inc(s_ln, 1)

            def batch(a, more):
                deviations(a, 0)
                if more:
                    wait_apart(e, s_ln, a.n(8, -4), s_apart)
                    load(a.next(1))
                deviations(a, 4)

            e.memset(minus_half[:, :], -0.5).then_inc(s_eps, 1)
            for u in range(2):
                load(At(0, u))
            batch(At(0, 0), False)
            with e.Fori(0, NBATCH // 2 - 1) as it:
                for off in (1, 2):
                    batch(At(it, off), True)
            batch(At(0, NBATCH - 1), False)

        @blk.vector
        def _(e):
            def norm_stats(src):
                for t in range(TB):
                    last = e.bn_stats(stats[:, t, :], src[:, t, :])
                last.then_inc(s_ln, 1)

            def norm_apply(a, k, src, dst):
                wait_apart(e, s_ln, a.n(8, k + 1), s_apart_v)
                for t in range(TB):
                    last = e.bn_aggr(mv[:, t, :], stats[:, t, :])
                last.then_inc(s_ln, 1)
                e.wait_ge(s_ln, a.n(8, k + 3))
                for t in range(TB):
                    last = e.tensor_scalar(dst[:, t, :], src[:, t, :], mv[:, t, 0:1], rstd[:, t:t + 1], ALU.subtract, ALU.mult)
                last.then_inc(s_ln, 1)

            def norms(a):
                u = a.u
                e.wait_ge(s_x[u], a.same(16, 16))
                norm_stats(xin[u])
                yield
                e.wait_ge(s_xs[u], a.same(16, 16))
                norm_apply(a, 0, xin[u], xn[u])
                yield
                e.wait_ge(s_ln, a.n(8, 4))
                norm_stats(xn[u])
                yield
                norm_apply(a, 4, xn[u], h)
                yield

            def batch(a, following):
                for _ in range(3):
                    if following:
                        next(following)
                e.wait_ge(s_lgf, a.n(1, 1))
                e.tensor_copy(keep["logits"][:, bass.ds(a.n(TB * NE), TB * NE)], lg[:, :, :].rearrange("p t e -> p (t e)")).then_inc(s_lgd, 1)
                e.wait_ge(s_act, emptied(a, CKV))
                e.tensor_copy(ckv[0][:, :], csb[a.u][:, 1, :]).then_inc(s_ch, 1)
                e.wait_ge(s_ch, a.n(1, 1))
                e.tensor_tensor(out=ckv[1][:, :], in0=csb[a.u][:, 1, :], in1=ckv[0][:, :].bitcast(F32), op=ALU.subtract).then_inc(s_cl, 1)
                if following:
                    next(following)

            e.sem_inc(s_lgd, 1)
            e.wait_ge(s_const, NCONST)
            for _ in norms(At(0, 0)):
                pass
            e.wait_ge(s_wh, 1)
            e.tensor_tensor(out=wv[1][:, :], in0=wvraw[:, :], in1=wv[0][:, :].bitcast(F32), op=ALU.subtract).then_inc(s_wl, 1)
            with e.Fori(0, NBATCH // 2 - 1) as it:
                for u in range(2):
                    batch(At(it, u), norms(At(it, u + 1)))
            batch(At(0, NBATCH - 2), norms(At(0, NBATCH - 1)))
            batch(At(0, NBATCH - 1), None)

        @blk.scalar
        def _(e):
            e.sem_inc(s_act, 2)
            e.wait_ge(s_const, NCONST)
            e.activation(wv[0][:, :], wvraw[:, :], ACT.Identity).then_inc(s_wh, 1)
            with e.Fori(0, NBATCH // 2) as it:
                for u in range(2):
                    a = At(it, u)

                    def empty(k, dst, **affine):
                        e.wait_ge(s_pa, a.n(ITEMS, k + 1))
                        e.activation(dst, pa[k % 2][:, :], ACT.Identity, **affine).then_inc(s_act, 1)

                    for k in range(KD):
                        empty(XNT + k, xnT[:, k, :])
                    for k in range(KD):
                        empty(HT + k, hT[:, k, :], scale=lnp[:, k, 0:1], bias=lnp[:, k, 1:2])
                    e.wait_ge(s_cs[u], a.same(32, 32))
                    empty(CKV, csb[u][:, 1, :])
                    empty(CQ, csb[u][:, 0, :])
                    for t in range(TB):
                        e.wait_ge(s_vs[t % 4], a.n(32, 16 + 16 * (t // 4)))
                        empty(V + t, vsb[t % 4][:, :])

        @blk.tensor
        def _(e):
            e.wait_ge(s_const, NCONST)
            with e.Fori(0, NBATCH // 2) as it:
                for u in range(2):
                    a = At(it, u)

                    def fill(k):
                        e.wait_ge(s_act, a.n(ITEMS, k + 1))
                        return pa[k % 2]

                    for src, k0, ready in ((xn[u], XNT, 4), (h, HT, 8)):
                        e.wait_ge(s_ln, a.n(8, ready))
                        for k in range(KD):
                            out = fill(k0 + k)
                            for t in range(TB):
                                mm = e.transpose(out[:, t * P:(t + 1) * P], src[:, t, k * P:(k + 1) * P], keep["ident"][:, :])
                            mm.then_inc(s_pa, 1)
                    e.wait_ge(s_act, emptied(a, XNT + 1))
                    e.wait_ge(s_lgd, a.n(1, 1))
                    for t in range(TB):
                        for k in range(KD):
                            mm = e.matmul(lg[:, t, :], xnT[:, k, t * P:(t + 1) * P], rw[:, k, :], start=(k == 0), stop=(k == KD - 1))
                    mm.then_inc(s_lgf, 1)
                    e.wait_ge(s_act, emptied(a, HT + 1))
                    for j, item in ((1, CKV), (0, CQ)):
                        out = fill(item)
                        for k in range(KD):
                            for n in range(NH2):
                                cols = slice(n * HALF, (n + 1) * HALF)
                                mm = e.matmul(out[:, cols], wd[:, j, k, :], hT[:, k, cols], start=(k == 0), stop=(k == KD - 1))
                        mm.then_inc(s_pa, 1)
                    e.wait_ge(s_wl, 1)
                    e.wait_ge(s_cl, a.n(1, 1))
                    for t in range(TB):
                        out = fill(V + t)
                        for cs, ws in PASSES:
                            for n in range(NH2):
                                cols = slice(n * HALF, (n + 1) * HALF)
                                mm = e.matmul(out[:, cols], ckv[cs][:, t * P:(t + 1) * P], wv[ws][:, cols],
                                              start=(cs + ws == 0), stop=(cs == 1))
                        mm.then_inc(s_pa, 1)


def route_phase(nc, io, scr, keep):
    with ExitStack() as ctx:
        ph = Phase(nc, ctx, "rt")
        sb, ps, sem = ph.sb, ph.ps, ph.sem
        C = NT * NE
        lg3 = keep["logits"][:, :].rearrange("p (t e) -> p t e", e=NE)
        rev, ebase, newe = sb("rev", [P, C]), sb("ebase", [P, C]), sb("newe", [P, C])
        tri, ones = sb("tri", [P, P]), sb("ones", [P, P])
        rev3, ebase3 = (x[:, :].rearrange("p (t e) -> p t e", e=NE) for x in (rev, ebase))

        def cube(name):
            return sb(name, [P, C])[:, :].rearrange("p (t e) -> p t e", e=NE)

        w, pick, second, both, rank, tmp = (cube(n) for n in ("w", "pick", "second", "both", "rank", "tmp"))
        oh = [cube("oh0"), cube("oh1")]
        tot, cum = sb("tot", [P, NE, NT]), sb("cum", [P, NE, NT])
        m = [sb(f"m{k}", [P, NT]) for k in range(2)]
        idx = sb("idx", [P, NT])
        dif, p2, den = (sb(n, [P, NT]) for n in ("dif", "p2", "den"))
        rk, pos, over, kept = (sb(n, [P, NT]) for n in ("rk", "pos", "over", "kept"))
        zero = sb("zero", [SLOT_P, NSLOT // SLOT_P], I32)
        pp, pt = ps("prefix", [P, C]), ps("total", [P, C])
        s_const, s_v, s_oh, s_mm, s_dif, s_exp, s_zero = (sem(n) for n in ("const", "v", "oh", "mm", "dif", "exp", "zero"))
        blk = ph.block()

        @blk.sync
        def _(e):
            e.dma_start(rev[:, :], io["rev"]).then_inc(s_const, 16)
            e.dma_start(ebase[:, :], io["ebase"]).then_inc(s_const, 16)
            e.dma_start(newe[:, :], io["newe"]).then_inc(s_const, 16)
            e.dma_start(tri[:, :], io["tri"]).then_inc(s_const, 16)
            e.dma_start(keep["tok"][:, :], io["tok"]).then_inc(s_const, 16)
            e.wait_ge(s_zero, 1)
            e.dma_start(scr["table"].rearrange("(p n) o -> p (n o)", p=SLOT_P), zero[:, :]).then_inc(s_const, 16)
            e.wait_ge(s_const, 96)

        @blk.gpsimd
        def _(e):
            e.memset(zero[:, :], 0).then_inc(s_zero, 1)

        @blk.scalar
        def _(e):
            e.wait_ge(s_dif, 1)
            e.activation(p2[:, :], dif[:, :], ACT.Exp).then_inc(s_exp, 1)

        @blk.tensor
        def _(e):
            e.wait_ge(s_const, 96)
            e.wait_ge(s_oh, 1)
            e.matmul(pp[:, :], tri[:, :], both.rearrange("p t e -> p (t e)"), start=True, stop=True)
            e.matmul(pt[:, :], ones[:, :], both.rearrange("p t e -> p (t e)"), start=True, stop=True).then_inc(s_mm, 1)

        @blk.vector
        def _(e):
            done = [0]

            def then(ins):
                done[0] += 1
                ins.then_inc(s_v, 1)
                e.wait_ge(s_v, done[0])

            def bc(x):
                return x[:, :].unsqueeze(2).broadcast_to((P, NT, NE))

            e.memset(ones[:, :], 1.0)
            e.wait_ge(s_const, 96)
            src = lg3
            for k in range(2):
                then(e.tensor_reduce(out=m[k][:, :], in_=src, axis=AX.X, op=ALU.max))
                then(e.tensor_tensor(out=pick, in0=src, in1=bc(m[k]), op=ALU.is_ge))
                then(e.tensor_tensor(out=w, in0=pick, in1=rev3, op=ALU.mult))
                then(e.tensor_reduce(out=idx[:, :], in_=w, axis=AX.X, op=ALU.max))
                then(e.tensor_tensor(out=oh[k], in0=rev3, in1=bc(idx), op=ALU.is_equal))
                if k == 0:
                    then(e.scalar_tensor_tensor(out=second, in0=oh[0], scalar=-3e38, in1=lg3, op0=ALU.mult, op1=ALU.add))
                    src = second
            e.tensor_tensor(out=both, in0=oh[0], in1=oh[1], op=ALU.add).then_inc(s_oh, 1)
            e.tensor_tensor(out=dif[:, :], in0=m[1][:, :], in1=m[0][:, :], op=ALU.subtract).then_inc(s_dif, 1)
            e.wait_ge(s_exp, 1)
            then(e.tensor_scalar(den[:, :], p2[:, :], 1.0, None, ALU.add))
            then(e.reciprocal(keep["gate"][:, :, 0], den[:, :]))
            then(e.tensor_tensor(out=keep["gate"][:, :, 1], in0=p2[:, :], in1=keep["gate"][:, :, 0], op=ALU.mult))
            e.wait_ge(s_mm, 1)
            then(e.tensor_copy(tot[:, :, :], pt[:, :].rearrange("p (t e) -> p e t", e=NE)))
            then(e.tensor_tensor_scan(cum[:, :, :].rearrange("p e t -> p (e t)"), newe[:, :], tot[:, :, :].rearrange("p e t -> p (e t)"), 0.0, ALU.mult, ALU.add))
            then(e.tensor_tensor(out=cum[:, :, :], in0=cum[:, :, :], in1=tot[:, :, :], op=ALU.subtract))
            then(e.tensor_tensor(out=rank, in0=pp[:, :].rearrange("p (t e) -> p t e", e=NE), in1=cum[:, :, :].rearrange("p e t -> p t e"), op=ALU.add))
            for k in range(2):
                then(e.tensor_tensor(out=tmp, in0=oh[k], in1=rank, op=ALU.mult))
                then(e.tensor_reduce(out=rk[:, :], in_=tmp, axis=AX.X, op=ALU.add))
                then(e.tensor_tensor(out=tmp, in0=oh[k], in1=ebase3, op=ALU.mult))
                then(e.tensor_reduce(out=pos[:, :], in_=tmp, axis=AX.X, op=ALU.add))
                then(e.tensor_scalar(over[:, :], rk[:, :], float(CAP), FAR, ALU.is_ge, ALU.mult))
                then(e.tensor_tensor(out=over[:, :], in0=over[:, :], in1=rk[:, :], op=ALU.add))
                then(e.tensor_tensor(out=keep["fill"][:, :, k], in0=over[:, :], in1=pos[:, :], op=ALU.add))
                then(e.tensor_scalar(kept[:, :], rk[:, :], float(CAP), None, ALU.is_lt))
                then(e.tensor_tensor(out=keep["gate"][:, :, k], in0=keep["gate"][:, :, k], in1=kept[:, :], op=ALU.mult))
                then(e.tensor_scalar(rk[:, :], rk[:, :], float(CAP - 1), None, ALU.min))
                then(e.tensor_tensor(out=keep["read"][:, :, k], in0=rk[:, :], in1=pos[:, :], op=ALU.add))


def attend_phase(nc, io, scr, keep):
    with ExitStack() as ctx:
        ph = Phase(nc, ctx, "at")
        sb, ps, sem = ph.sb, ph.ps, ph.sem
        NP = 8
        TILES = 2 * KT
        NPROJ, NMAX = 2 * NH2, 2 * KT * NH2
        NSUM = 2 * (KT - 1)
        LO, HI = slice(0, DH), slice(DH, P)
        rows = [LO, HI]
        other = [HI, LO]
        bank = [slice(n * HALF, (n + 1) * HALF) for n in range(NH2)]
        wqk = [sb(f"wqk{u}", [DL, 2, P]) for u in range(2)]
        c = [sb(f"c{u}", [DL, 2, S]) for u in range(2)]
        v = [sb(f"v{u}", [P, KT, P]) for u in range(2)]
        raw = [sb("rawq", [P, S]), sb("rawk", [P, S])]
        swp = [sb("swpq", [P, S]), sb("swpk", [P, S])]
        rot = [sb("rotq", [P, S]), sb("rotk", [P, S])]
        qa = [[sb(f"qa{u}{h}", [P, S], F32R) for h in range(2)] for u in range(2)]
        qb = [[sb(f"qb{u}{h}", [P, S], F32R) for h in range(2)] for u in range(2)]
        ka = [[sb(f"ka{u}{h}", [P, S], F32R) for h in range(2)] for u in range(2)]
        kb = [[sb(f"kb{u}{h}", [P, S], F32R) for h in range(2)] for u in range(2)]
        ex = [sb(f"ex{k}", [P, S]) for k in range(NP)]
        total = [[sb(f"sum{u}{h}", [P, S]) for h in range(2)] for u in range(2)]
        osb, den, rec = sb("osb", [P, S]), sb("den", [P, S]), sb("rec", [P, S])
        denc, recc = sb("denc", [P, 2, S // P]), sb("recc", [P, 2, S // P])
        oT = [sb(f"oT{u}", [P, S]) for u in range(2)]
        cos, sin = sb("cos", [P, S]), sb("sin", [P, S])
        ones = sb("ones", [P, DH])
        mx = sb("mx", [P, NMAX])
        mq = [sb(f"mq{h}", [P, KT]) for h in range(2)]
        mneg = [sb(f"mneg{h}", [KT, P], F32R) for h in range(2)]
        fill_i, tok_i = sb("fill_i", [P, 2], I32), sb("tok_i", [P, 1], I32)
        pst = [ps(f"st{k}", [P, S]) for k in range(2)]
        ppv = ps("pv", [P, S])
        pfr = [ps(f"fr{k}", [P, HALF]) for k in range(2)]
        s_const, s_init, s_apart, s_apart_s = (sem(n) for n in ("const", "init", "apart", "apart_s"))
        s_ldw = [sem(f"ldw{u}") for u in range(2)]
        s_ldv = [sem(f"ldv{u}") for u in range(2)]
        s_pf, s_pe, s_mf, s_me, s_tf, s_te, s_df, s_de = (sem(n) for n in ("pf", "pe", "mf", "me", "tf", "te", "df", "de"))
        s_sw, s_prod, s_rot, s_hi, s_high, s_lo, s_mq, s_mrow = (sem(n) for n in ("sw", "prod", "rot", "hi", "high", "lo", "mq", "mrow"))
        s_st, s_exp, s_pv, s_sum = sem("st"), sem("exp"), sem("pvd"), sem("sumd")
        s_osb, s_denc, s_recc, s_recd, s_rec, s_ot = (sem(n) for n in ("osb", "denc", "recc", "recd", "rec", "ot"))
        s_store = [sem(f"store{u}") for u in range(2)]
        s_idx, s_scat = sem("idx"), sem("scat")
        blk = ph.block()

        def run(e, prologue, body, tail):
            prologue()
            body(At(0, 0), None, 4)
            with e.Fori(0, NPAIR // 2 - 3) as it:
                for off in (1, 2):
                    i = At(it, off)
                    body(i, i.next(-1), 4)
            for n in range(NPAIR - 5, NPAIR):
                i = At(0, n)
                body(i, i.next(-1), NPAIR - 1 - n)
            tail(At(0, NPAIR - 1))

        @blk.sync
        def _(e):
            def load_qk(j):
                e.dma_start(wqk[j.u][:, :, :], io["wqk"][j.n() % HP, :, :, :]).then_inc(s_ldw[j.u], 16)
                e.dma_start(c[j.u][:, :, :], scr["c"][j.n() // HP, :, :, :].rearrange("j p s -> p j s")).then_inc(s_ldw[j.u], 16)

            def load_v(j):
                e.dma_start(v[j.u][:, :, :], scr["v"][j.n() // HP, j.n() % HP, :, :, :]).then_inc(s_ldv[j.u], 16)

            def swap_rows(j):
                wait_apart(e, s_rot, j.n(2, 0), s_apart_s)
                for w in range(2):
                    e.wait_ge(s_pe, j.n(NPROJ, NH2 * (w + 1)))
                    for o in range(2):
                        e.dma_start(swp[w][o:P:2, :], raw[w][1 - o:P:2, :]).then_inc(s_sw, 16)

            def max_rows(j):
                for h in range(2):
                    r = other[h].start
                    e.wait_ge(s_te, j.n(2, h + 1))
                    e.dma_start(qb[j.u][h][r:r + 1, :].bitcast(F32).rearrange("o (t q) -> o t q", q=P),
                                mneg[h][:, :].bitcast(F32)).then_inc(s_mrow, 16)

            def spread(i):
                e.wait_ge(s_de, i.n(2, 2))
                for h in range(2):
                    r = rows[h].start
                    e.dma_start(denc[:, h, :], den[r:r + 1, :].rearrange("o (p k) -> o p k", p=P)).then_inc(s_denc, 16)

            def broadcast(i):
                e.wait_ge(s_recc, i.n(1, 1))
                e.dma_start(scr["rec"][i.n(), :, :].rearrange("h (p k) -> p h k", p=P), recc[:, :, :]).then_inc(s_recd, 16)
                e.wait_ge(s_recd, i.n(16, 16))
                for h in range(2):
                    e.dma_start(rec[rows[h], :], scr["rec"][i.n(), h, :].unsqueeze(0).broadcast_to((DH, S))).then_inc(s_rec, 16)

            def store(i):
                e.wait_ge(s_ot, i.n(1, 1))
                e.dma_start(scr["o"][i.n(), :, :], oT[i.u][:, :]).then_inc(s_store[i.u], 16)

            def prologue():
                load_qk(At(0, 0))
                e.dma_start(cos[:, :], io["cos"]).then_inc(s_const, 16)
                e.dma_start(sin[:, :], io["sin"]).then_inc(s_const, 16)
                for s in s_store:
                    e.sem_inc(s, 16)
                load_qk(At(0, 1))
                load_v(At(0, 0))
                e.wait_ge(s_init, 2)
                e.wait_ge(s_pf, NPROJ)
                load_qk(At(0, 2))
                swap_rows(At(0, 0))
                e.wait_ge(s_pf, 2 * NPROJ)
                load_qk(At(0, 3))
                swap_rows(At(0, 1))
                max_rows(At(0, 0))
                swap_rows(At(0, 2))

            def body(i, prev, ahead):
                if ahead >= 4:
                    e.wait_ge(s_pf, i.n(NPROJ, 3 * NPROJ))
                    load_qk(i.next(4))
                if prev:
                    e.wait_ge(s_pv, i.n(KT, 0))
                if ahead:
                    load_v(i.next(1))
                if prev and ahead >= 2:
                    swap_rows(i.next(2))
                if prev:
                    spread(prev)
                    broadcast(prev)
                if ahead:
                    max_rows(i.next(1))
                if prev:
                    store(prev)

            def tail(i):
                spread(i)
                broadcast(i)
                store(i)
                for u in range(2):
                    e.wait_ge(s_store[u], 16 * (NPAIR // 2 + 1))

            run(e, prologue, body, tail)

        @blk.gpsimd
        def _(e):
            def body(i, *_):
                def sums(kt):
                    for h in range(2):
                        wait_apart(e, s_exp, i.n(TILES, 2 * kt + h + 1), s_apart)
                        acc = total[i.u][h][:, :]
                        if kt == 1:
                            wait_apart(e, s_df, i.n(2, -2), s_apart)
                            a0 = ex[h][:, :]
                        else:
                            wait_apart(e, s_sum, i.n(NSUM, 2 * (kt - 2) + h + 1), s_apart)
                            a0 = acc
                        e.tensor_tensor(out=acc, in0=a0, in1=ex[(2 * kt + h) % NP][:, :], op=ALU.add).then_inc(s_sum, 1)

                for kt in range(1, KT):
                    sums(kt)
                    if kt == 2:
                        wait_apart(e, s_scat, i.n(32, 0), s_apart)
                        e.tensor_copy(fill_i[:, :], keep["fill"][:, i.n(), :])
                        e.tensor_copy(tok_i[:, :], keep["tok"][:, bass.ds(i.n(), 1)]).then_inc(s_idx, 1)
                        wait_apart(e, s_idx, i.n(1, 1), s_apart)
                        for k in range(2):
                            e.indirect_dma_start(out=scr["table"], out_offset=bass.IndirectOffsetOnAxis(ap=fill_i[:, k:k + 1], axis=0),
                                                 in_=tok_i[:, :], in_offset=None, bounds_check=NSLOT - 1, oob_is_err=False).then_inc(s_scat, 16)

            run(e, lambda: None, body, lambda i: e.wait_ge(s_scat, 32 * NPAIR))

        @blk.vector
        def _(e):
            def rope(j):
                e.wait_ge(s_sw, j.n(64, 64))
                wait(e, s_hi, j.n(4, 0))
                wait(e, s_lo, j.n(4, 0))
                for w in range(2):
                    e.tensor_tensor(out=rot[w][:, :], in0=raw[w][:, :], in1=cos[:, :], op=ALU.mult).then_inc(s_prod, 1)
                for w in range(2):
                    e.tensor_tensor(out=swp[w][:, :], in0=swp[w][:, :], in1=sin[:, :], op=ALU.mult).then_inc(s_prod, 1)
                e.wait_ge(s_prod, j.n(4, 4))
                for w in (1, 0):
                    e.tensor_tensor(out=rot[w][:, :], in0=rot[w][:, :], in1=swp[w][:, :], op=ALU.add).then_inc(s_rot, 1)

            def split(j):
                e.wait_ge(s_rot, j.n(2, 2))
                wait(e, s_st, j.n(TILES, -TILES))
                for h in range(2):
                    for to, x in ((ka, 1), (qa, 0)):
                        e.tensor_copy(to[j.u][h][rows[h], :], rot[x][rows[h], :]).then_inc(s_high, 1)
                for h in range(2):
                    e.wait_ge(s_high, j.n(4, 2 * h + 1))
                    e.tensor_tensor(out=ka[j.u][h][other[h], :], in0=rot[1][rows[h], :], in1=ka[j.u][h][rows[h], :].bitcast(F32), op=ALU.subtract).then_inc(s_lo, 1)
                for h in range(2):
                    e.wait_ge(s_high, j.n(4, 2 * h + 2))
                    e.tensor_tensor(out=qb[j.u][h][rows[h], :], in0=rot[0][rows[h], :], in1=qa[j.u][h][rows[h], :].bitcast(F32), op=ALU.subtract).then_inc(s_lo, 1)

            def maxima(j, first, count):
                for m in range(first, first + count):
                    e.wait_ge(s_mf, j.n(NMAX, m + 1))
                    e.reduce_max(mx[:, m:m + 1], pfr[m % 2][:, :], AX.X).then_inc(s_me, 1)

            def join(j, h):
                e.wait_ge(s_me, j.n(NMAX, NMAX // 2 * (h + 1)))
                wait(e, s_tf, j.n(2, h - 1))
                m = mx[:, :].rearrange("p (h q n) -> p h n q", h=2, n=NH2)
                e.tensor_tensor(out=mq[h][:, :], in0=m[:, h, 0, :], in1=m[:, h, 1, :], op=ALU.max).then_inc(s_mq, 1)

            def recip(i):
                e.wait_ge(s_denc, i.n(32, 32))
                wait(e, s_recd, i.n(16, 0))
                e.reciprocal(recc[:, :, :], denc[:, :, :]).then_inc(s_recc, 1)

            def normalise(i):
                e.wait_ge(s_rec, i.n(32, 32))
                e.wait_ge(s_osb, i.n(1, 1))
                e.wait_ge(s_store[i.u], i.same(16, 16))
                e.tensor_tensor(out=oT[i.u][:, :], in0=osb[:, :], in1=rec[:, :], op=ALU.mult).then_inc(s_ot, 1)

            def front(j, prev):
                split(j)
                maxima(j, 0, NMAX // 2)
                join(j, 0)
                maxima(j, NMAX // 2, 8)
                if prev:
                    recip(prev)
                maxima(j, NMAX // 2 + 8, NMAX // 2 - 8)
                join(j, 1)

            def prologue():
                for u in range(2):
                    for h in range(2):
                        e.memset(qb[u][h][other[h], :].bitcast(F32), 0.0)
                        last = e.memset(kb[u][h][other[h], :].bitcast(F32), 0.0)
                e.memset(ones[:, :], 1.0)
                last.then_inc(s_init, 1)
                e.wait_ge(s_init, 1)
                for u in range(2):
                    for h in range(2):
                        r = other[h].start
                        last = e.memset(kb[u][h][r:r + 1, :].bitcast(F32), 1.0)
                last.then_inc(s_init, 1)
                e.wait_ge(s_const, 32)
                rope(At(0, 0))
                front(At(0, 0), None)
                rope(At(0, 1))

            def body(i, prev, ahead):
                if ahead:
                    front(i.next(1), prev)
                else:
                    recip(prev)
                if ahead >= 2:
                    rope(i.next(2))
                if prev:
                    normalise(prev)

            def tail(i):
                recip(i)
                normalise(i)

            run(e, prologue, body, tail)

        @blk.scalar
        def _(e):
            def exps(i, s):
                kt, h = s // 2, s % 2
                back = kt - NP // 2
                e.wait_ge(s_st, i.n(TILES, s + 1))
                wait(e, s_pv, i.n(KT, back + 1))
                wait(e, s_sum, i.n(NSUM, 2 * max(back - 1, 0) + h + 1 if back >= 0 else 2 * (back + KT - 1) + h + 1 - NSUM))
                e.activation(ex[s % NP][:, :], pst[s % 2][:, :], ACT.Exp, scale=SCALE).then_inc(s_exp, 1)

            def proj_copy(j, w):
                wait(e, s_prod, j.n(4, w - 3))
                for n in range(NH2):
                    e.wait_ge(s_pf, j.n(NPROJ, NH2 * w + n + 1))
                    e.activation(raw[w][:, bank[n]], pfr[n][:, :], ACT.Copy).then_inc(s_pe, 1)

            def query_high(j, h):
                e.wait_ge(s_rot, j.n(2, 2))
                if h == 0:
                    wait(e, s_st, j.n(TILES, -TILES))
                e.activation(qa[j.u][h][other[h], :], rot[0][rows[h], :], ACT.Copy).then_inc(s_hi, 1)

            def key_high(j, h):
                e.wait_ge(s_rot, j.n(2, 1))
                e.activation(kb[j.u][h][rows[h], :], rot[1][rows[h], :], ACT.Copy).then_inc(s_hi, 1)

            def out_copy(i):
                e.wait_ge(s_pv, i.n(KT, KT))
                wait(e, s_ot, i.n())
                e.activation(osb[:, :], ppv[:, :], ACT.Copy).then_inc(s_osb, 1)

            def den_copy(i):
                for n in range(NH2):
                    e.wait_ge(s_df, i.n(2, n + 1))
                    wait(e, s_denc, i.n(32, 0))
                    e.activation(den[:, bank[n]], pfr[n][:, :], ACT.Copy).then_inc(s_de, 1)

            def negate(j):
                for h in range(2):
                    e.wait_ge(s_tf, j.n(2, h + 1))
                    wait(e, s_mrow, j.n(32, 0))
                    e.activation(mneg[h][:, :], pfr[h][0:KT, 0:P], ACT.Copy, scale=-1.0).then_inc(s_te, 1)

            def prologue():
                for n in range(2):
                    for w in range(2):
                        proj_copy(At(0, n), w)
                for h in range(2):
                    query_high(At(0, 0), h)
                for h in range(2):
                    key_high(At(0, 0), h)
                negate(At(0, 0))
                for w in range(2):
                    proj_copy(At(0, 2), w)

            def body(i, prev, ahead):
                nxt, more = i.next(1), ahead >= 1
                for s in range(TILES):
                    exps(i, s)
                    if s == 0 and more:
                        query_high(nxt, 0)
                    if s == 1 and prev:
                        if ahead >= 2:
                            proj_copy(i.next(2), 1)
                        out_copy(prev)
                    if s == 3 and prev:
                        den_copy(prev)
                    if s == 4 and more:
                        query_high(nxt, 1)
                    if s in (6, 8) and more:
                        key_high(nxt, s // 8)
                    if s == 13 and more:
                        negate(nxt)
                if ahead >= 3:
                    proj_copy(i.next(3), 0)

            def tail(i):
                out_copy(i)
                den_copy(i)

            run(e, prologue, body, tail)

        @blk.tensor
        def _(e):
            def scores(i, s):
                kt, h = s // 2, s % 2
                if s < 2:
                    e.wait_ge(s_mrow, i.n(32, 32))
                    e.wait_ge(s_hi, i.n(4, 4))
                    e.wait_ge(s_lo, i.n(4, 4))
                wait(e, s_exp, i.n(TILES, s - 1))
                keys = slice(kt * P, (kt + 1) * P)
                for ww, (kk, qq) in enumerate(((ka, qa), (kb, qb))):
                    for n in range(NH2):
                        mm = e.matmul(pst[s % 2][:, bank[n]], kk[i.u][h][:, keys], qq[i.u][h][:, bank[n]], start=(ww == 0), stop=(ww == 1))
                    if ww == 1:
                        mm.then_inc(s_st, 1)
                    yield

            def values(i, kt):
                if kt == 0:
                    e.wait_ge(s_ldv[i.u], i.same(16, 16))
                    wait(e, s_osb, i.n())
                e.wait_ge(s_exp, i.n(TILES, 2 * kt + 2))
                for n in range(NH2):
                    for h in range(2):
                        mm = e.matmul(ppv[rows[h], bank[n]], v[i.u][:, kt, rows[h]], ex[(2 * kt + h) % NP][:, bank[n]],
                                      start=(kt == 0), stop=(kt == KT - 1))
                    if n == NH2 - 1:
                        mm.then_inc(s_pv, 1)
                    yield

            def after(sem, value):
                return lambda n: wait(e, sem, value + (n - 1))

            def denominators(i, emptied):
                e.wait_ge(s_sum, i.n(NSUM, NSUM))
                for n in range(NH2):
                    emptied(n)
                    for h in range(2):
                        mm = e.matmul(pfr[n][rows[h], :], ones[:, :], total[i.u][h][:, bank[n]], start=True, stop=True)
                    mm.then_inc(s_df, 1)
                    yield

            def project(j, w, emptied=None):
                if w == 0:
                    e.wait_ge(s_ldw[j.u], j.same(32, 32))
                for n in range(NH2):
                    if w:
                        e.wait_ge(s_pe, j.n(NPROJ, n + 1))
                    else:
                        emptied(n)
                    e.matmul(pfr[n][:, :], wqk[j.u][:, w, :], c[j.u][:, w, bank[n]], start=True, stop=True).then_inc(s_pf, 1)
                    yield

            def max_scores(j, m, emptied=None):
                h, qt, n = m // (KT * NH2), m // NH2 % KT, m % NH2
                if m % (KT * NH2) == 0:
                    e.wait_ge(s_hi, j.n(4, h + 1))
                    e.wait_ge(s_lo, j.n(4, h + 1))
                if m < 2:
                    emptied(m)
                else:
                    e.wait_ge(s_me, j.n(NMAX, m - 1))
                e.matmul(pfr[m % 2][:, :], qa[j.u][h][:, qt * P:(qt + 1) * P], ka[j.u][h][:, bank[n]], start=True, stop=True).then_inc(s_mf, 1)

            def turn_maxima(j, h):
                e.wait_ge(s_mq, j.n(2, 2))
                e.transpose(pfr[h][0:KT, 0:P], mq[h][:, :], keep["ident"][:, :]).then_inc(s_tf, 1)

            def front(i, prev, ahead):
                j = i.next(1)
                if prev and ahead >= 2:
                    yield from project(i.next(2), 1)
                    last = after(s_pe, i.n(NPROJ, 3 * NPROJ))
                else:
                    yield from (None,) * NH2
                    last = after(s_te, i.n(2, 2))
                if prev:
                    yield from denominators(prev, last)
                    last = after(s_de, i.n(2, 0))
                else:
                    yield from (None,) * NH2
                    last = after(s_pe, 3 * NPROJ)
                if ahead:
                    for m in range(NMAX):
                        max_scores(j, m, last)
                        yield
                    for h in range(2):
                        turn_maxima(j, h)
                        yield
                if ahead >= 3:
                    yield from project(i.next(3), 0, after(s_te, j.n(2, 2)))

            def drain(g):
                for _ in g:
                    pass

            def prologue():
                for n in range(2):
                    drain(project(At(0, n), 0, after(s_pe, n * NPROJ)))
                    drain(project(At(0, n), 1))
                for m in range(NMAX):
                    max_scores(At(0, 0), m, after(s_pe, 2 * NPROJ))
                for h in range(2):
                    turn_maxima(At(0, 0), h)
                drain(project(At(0, 2), 0, after(s_te, 2)))
                drain(project(At(0, 2), 1))

            PLAN = [(0, 0, 0, 0, 1, 1), (0, 1, 0, 1, 1, 1), (0, 1, 1, 1, 2, 2), (0, 1, 1, 1, 2, 2),
                    (0, 1, 1, 1, 2, 2), (0, 1, 1, 1, 2, 2), (1, 1, 0, 0, 1, 1), (0, 0, 0, 0, 1, 1)]
            assert sum(map(sum, PLAN)) == NMAX + 2 + NH2 + NPROJ

            def body(i, prev, ahead):
                work = front(i, prev, ahead)
                for kt in range(KT):
                    plan = list(PLAN[kt])

                    def some():
                        for _ in range(plan.pop(0)):
                            next(work, None)

                    for h in range(2):
                        for _ in scores(i, 2 * kt + h):
                            some()
                    if kt or prev:
                        for _ in values(*((i, kt - 1) if kt else (prev, KT - 1))):
                            some()
                    else:
                        some()
                        some()
                drain(work)

            def tail(i):
                drain(values(i, KT - 1))
                drain(denominators(i, after(s_de, i.n(2, 0))))

            run(e, prologue, body, tail)


def experts_phase(nc, io, scr, keep):
    with ExitStack() as ctx:
        ph = Phase(nc, ctx, "ex")
        sb, ps, sem = ph.sb, ph.ps, ph.sem
        STEPS = NE // 2 * PARTS
        HL = 2
        PASSES = ((0, 0), (0, 1), (1, 0))
        raw = [sb(f"raw{q}", [P, KD * FF + NF * D]) for q in range(2)]
        w1 = [sb(f"w1{q}", [P, HL, KD, FF], F32R) for q in range(2)]
        w2 = [sb(f"w2{q}", [P, HL, NF, D], F32R) for q in range(2)]
        slots = sb("slots", [SLOT_P, NE, SLOT_T], I32)
        idx = [sb(f"idx{q}", [SLOT_P, PART_T], I32) for q in range(2)]
        xg = [sb(f"xg{q}", [SLOT_P, PART_T, D]) for q in range(2)]
        xT = [sb(f"xT{q}", [P, HL, KD, PW], F32R) for q in range(2)]
        hs = sb("hs", [P, NF, PW])
        hT = [sb(f"hT{q}", [P, HL, NF, PW], F32R) for q in range(2)]
        out = [sb(f"out{q}", [SLOT_P, PART_T, D]) for q in range(2)]
        ptr = ps("tr", [P, KD, HALF])
        phid = [ps(f"h{k}", [P, HALF]) for k in range(2)]
        po = ps("o", [P, PART_T, HALF])
        s_w = [sem(f"w{q}") for q in range(2)]
        s_g = [sem(f"g{q}") for q in range(2)]
        s_os = [sem(f"os{q}") for q in range(2)]
        s_split = [sem(f"split{q}") for q in range(2)]
        s_apart = sem("apart")
        s_slots, s_idx, s_tr, s_xh, s_xT, s_h, s_silu, s_hh, s_hT, s_o, s_oe = (
            sem(n) for n in ("slots", "idx", "tr", "xh", "xT", "h", "silu", "hh", "hT", "o", "oe"))
        blk = ph.block()

        @blk.sync
        def _(e):
            e.dma_start(slots[:, :, :], scr["table"].rearrange("(e p t) o -> p e (t o)", e=NE, p=SLOT_P)).then_inc(s_slots, 16)

            def load(expert, q):
                e.dma_start(raw[q][:, 0:KD * FF].rearrange("p (k f) -> p k f", k=KD), io["w1"][expert, :, :].rearrange("(k p) f -> p k f", p=P)).then_inc(s_w[q], 16)
                e.dma_start(raw[q][:, KD * FF:].rearrange("p (k d) -> p k d", k=NF), io["w2"][expert, :, :].rearrange("(k p) d -> p k d", p=P)).then_inc(s_w[q], 16)

            load(0, 0)
            e.wait_ge(s_g[0], 48)
            load(1, 1)
            with e.Fori(1, NE // 2) as pr:
                for q in range(2):
                    e.wait_ge(s_split[q], pr * 4)
                    load(pr * 2 + q, q)

        @blk.gpsimd
        def _(e):
            e.wait_ge(s_slots, 16)

            def gather(n, q, first):
                a = At(n, q)
                if not first:
                    wait_apart(e, s_tr, a.n(1, -1), s_apart)
                col = (n // PARTS) * (2 * SLOT_T) + (n % PARTS) * PART_T + q * SLOT_T
                e.tensor_copy(idx[q][:, :], slots[:, :, :].rearrange("p e t -> p (e t)")[:, bass.ds(col, PART_T)]).then_inc(s_idx, 1)
                wait_apart(e, s_idx, a.n(1, 1), s_apart)
                for c in range(PART_T):
                    e.indirect_dma_start(out=xg[q][:, c, :], out_offset=None, in_=scr["xn"].rearrange("b s d -> (b s) d"),
                                         in_offset=bass.IndirectOffsetOnAxis(ap=idx[q][:, c:c + 1], axis=0)).then_inc(s_g[q], 16)

            for q in range(2):
                gather(0, q, True)
            with e.Fori(1, STEPS) as n:
                for q in range(2):
                    gather(n, q, False)

        @blk.vector
        def _(e):
            def split_weights(pr, q):
                e.wait_ge(s_w[q], pr * 32 + 32)
                wait(e, s_o, pr * (2 * PARTS) + (q - 1) if not isinstance(pr, int) or pr else 0)
                n1 = KD * FF
                flat = ((w1[q][:, :, :, :].rearrange("p s k f -> p s (k f)"), raw[q][:, 0:n1]),
                        (w2[q][:, :, :, :].rearrange("p s k d -> p s (k d)"), raw[q][:, n1:]))
                for halves, src in flat:
                    e.tensor_copy(halves[:, 0, :], src).then_inc(s_split[q], 1)
                e.wait_ge(s_split[q], pr * 4 + 2)
                for halves, src in flat:
                    e.tensor_tensor(out=halves[:, 1, :], in0=src, in1=halves[:, 0, :].bitcast(F32), op=ALU.subtract).then_inc(s_split[q], 1)

            def turned(a):
                e.wait_ge(s_tr, a.n(1, 1))
                wait(e, s_h, a.n(NF, -NF))
                e.tensor_copy(xT[a.u][:, 0, :, :], ptr[:, :, 0:PW]).then_inc(s_xh, 1)
                e.wait_ge(s_xh, a.n(1, 1))
                e.tensor_tensor(out=xT[a.u][:, 1, :, :], in0=ptr[:, :, 0:PW], in1=xT[a.u][:, 0, :, :].bitcast(F32), op=ALU.subtract).then_inc(s_xT, 1)

            def hidden(a):
                q = a.u
                for f in range(0, NF, 2):
                    e.wait_ge(s_silu, a.n(NF, f + 2))
                    if f == 0:
                        wait(e, s_o, a.n(1, -1))
                    e.tensor_copy(hT[q][:, 0, f:f + 2, :], hs[:, f:f + 2, :]).then_inc(s_hh, 1)
                    e.wait_ge(s_hh, a.n(NF // 2, f // 2 + 1))
                    e.tensor_tensor(out=hT[q][:, 1, f:f + 2, :], in0=hs[:, f:f + 2, :], in1=hT[q][:, 0, f:f + 2, :].bitcast(F32), op=ALU.subtract).then_inc(s_hT, 1)

            def outputs(a):
                e.wait_ge(s_os[a.u], a.same(16, 16))
                e.wait_ge(s_o, a.n(1, 1))
                e.tensor_copy(out[a.u][:, :, :], po[0:SLOT_P, :, 0:D]).then_inc(s_oe, 1)

            split_weights(0, 0)
            turned(At(0, 0))
            split_weights(0, 1)

            def parts(n, last_of_pair):
                hidden(At(n, 0))
                turned(At(n, 1))
                outputs(At(n, 0))
                hidden(At(n, 1))
                if not last_of_pair:
                    turned(At(n, 2))
                    outputs(At(n, 1))

            parts(0, False)
            with e.Fori(1, PARTS - 1) as n:
                parts(n, False)

            def seam(pr):
                n = pr * PARTS + (PARTS - 1)
                hidden(At(n, 0))
                turned(At(n, 1))
                outputs(At(n, 0))
                split_weights(pr + 1, 0)
                hidden(At(n, 1))
                turned(At(n, 2))
                outputs(At(n, 1))
                split_weights(pr + 1, 1)

            with e.Fori(0, NE // 2 - 1) as pr:
                seam(pr)
                with e.Fori(0, PARTS - 1) as g:
                    parts(pr * PARTS + g + PARTS, False)
            parts(STEPS - 1, True)
            outputs(At(STEPS - 1, 1))

        @blk.scalar
        def _(e):
            for q in range(2):
                e.sem_inc(s_os[q], 16)

            def silus(a):
                for f in range(NF):
                    e.wait_ge(s_h, a.n(NF, f + 1))
                    wait(e, s_hT, a.n(NF // 2, f // 2 + 1 - NF // 2))
                    e.activation(hs[:, f, :], phid[f % 2][:, 0:PW], ACT.Silu).then_inc(s_silu, 1)

            def store(n, q):
                a = At(n, q)
                e.wait_ge(s_oe, a.n(1, 1))
                dst = scr["eo"].rearrange("(e p g c) d -> e g p (c d)", e=NE, p=SLOT_P, g=PARTS)
                e.dma_start(dst[(n // PARTS) * 2 + q, n % PARTS, :, :], out[q][:, :, :].rearrange("p c d -> p (c d)")).then_inc(s_os[q], 16)

            silus(At(0, 0))
            silus(At(0, 1))
            with e.Fori(1, STEPS) as n:
                silus(At(n, 0))
                store(n - 1, 0)
                silus(At(n, 1))
                store(n - 1, 1)
            store(STEPS - 1, 0)
            store(STEPS - 1, 1)
            for q in range(2):
                e.wait_ge(s_os[q], 16 * (STEPS + 1))

        @blk.tensor
        def _(e):
            def turn(a, first=False):
                e.wait_ge(s_g[a.u], a.same(48, 48))
                if not first:
                    e.wait_ge(s_xT, a.n())
                for c in range(PART_T):
                    for k in range(KD):
                        mm = e.transpose(ptr[:, k, c * SLOT_P:(c + 1) * SLOT_P], xg[a.u][:, c, k * P:(k + 1) * P], keep["ident"][0:SLOT_P, 0:SLOT_P])
                mm.then_inc(s_tr, 1)

            def hidden(n, q):
                a = At(n, q)
                e.wait_ge(s_split[q], (n // PARTS) * 4 + 4)
                e.wait_ge(s_xT, a.n(1, 1))
                for f in range(NF):
                    wait(e, s_silu, a.n(NF, f - 1))
                    for ws, xs in PASSES:
                        for k in range(KD):
                            mm = e.matmul(phid[f % 2][:, 0:PW], w1[q][:, ws, k, f * P:(f + 1) * P], xT[q][:, xs, k, :],
                                          start=(ws + xs + k == 0), stop=(ws == 1 and k == KD - 1))
                    mm.then_inc(s_h, 1)

            def down(n, q, first=False):
                a = At(n, q)
                if not first:
                    e.wait_ge(s_oe, a.n())
                for c in range(PART_T):
                    for f in range(NF):
                        if c == 0 and f % 2 == 0:
                            e.wait_ge(s_hT, a.n(NF // 2, f // 2 + 1))
                        for hh, ws in PASSES:
                            mm = e.matmul(po[0:SLOT_P, c, 0:D], hT[q][:, hh, f, c * SLOT_P:(c + 1) * SLOT_P], w2[q][:, ws, f, :],
                                          start=(hh + ws + f == 0), stop=(hh == 1 and f == NF - 1))
                mm.then_inc(s_o, 1)

            turn(At(0, 0), True)
            hidden(0, 0)
            turn(At(0, 1))
            down(0, 0, True)
            hidden(0, 1)
            turn(At(0, 2))
            down(0, 1)
            with e.Fori(1, STEPS - 1) as n:
                hidden(n, 0)
                turn(At(n, 1))
                down(n, 0)
                hidden(n, 1)
                turn(At(n, 2))
                down(n, 1)
            hidden(STEPS - 1, 0)
            turn(At(STEPS - 1, 1))
            down(STEPS - 1, 0)
            hidden(STEPS - 1, 1)
            down(STEPS - 1, 1)


def combine_phase(nc, io, scr, keep):
    with ExitStack() as ctx:
        ph = Phase(nc, ctx, "cb")
        sb, ps, sem = ph.sb, ph.ps, ph.sem
        CT = TB // 2
        LEAD = TB - 2
        PASSES = ((0, 0), (0, 1), (1, 0))
        raw = [sb(f"raw{k}", [P, HP, CT * P]) for k in range(2)]
        oT = [[sb(f"oT{k}{w}", [P, HP, CT * P], F32R) for w in range(2)] for k in range(2)]
        x = [sb(f"x{u}", [P, TB, D]) for u in range(2)]
        xn = [sb(f"xn{u}", [P, TB, D]) for u in range(2)]
        res = [sb(f"res{u}", [P, TB, D]) for u in range(2)]
        wraw = sb("wraw", [P, HP, D])
        wo = [sb(f"wo{w}", [P, HP, D], F32R) for w in range(2)]
        NG = TB
        idx = [sb(f"idx{k}", [P, 2], I32) for k in range(NG)]
        eo = [[sb(f"eo{k}{j}", [P, D]) for j in range(2)] for k in range(NG)]
        att = [sb(f"att{k}", [P, D]) for k in range(2)]
        mix = [sb(f"mix{k}", [P, D]) for k in range(2)]
        gate = [sb(f"gate{k}", [P, D]) for k in range(2)]
        g2 = sb("g2", [P, TB, 2])
        pj = [ps(f"pj{k}", [P, HALF]) for k in range(2)]
        s_wo, s_wh, s_wl, s_oh, s_ol = (sem(n) for n in ("wo", "wh", "wl", "oh", "ol"))
        s_pj, s_att, s_mix, s_silu, s_mul, s_res, s_idx, s_g2 = (sem(n) for n in ("pj", "att", "mix", "silu", "mul", "res", "idx", "g2"))
        s_apart = sem("apart")
        s_o = [sem(f"o{k}") for k in range(2)]
        s_ld = [sem(f"ld{u}") for u in range(2)]
        s_g = [sem(f"rows{k}") for k in range(NG)]
        s_st = [sem(f"st{u}") for u in range(2)]
        blk = ph.block()

        def piece(q):
            k, pairs, cols = q // CT, slice(q % 2 * (HP // 2), (q % 2 + 1) * (HP // 2)), slice(q % CT // 2 * 2 * P, (q % CT // 2 + 1) * 2 * P)
            return [tile[:, pairs, cols] for tile in (raw[k], *oT[k])]

        @blk.sync
        def _(e):
            def load_o(a, k):
                e.dma_start(raw[k][:, :, :], scr["o"].rearrange("(b r) p s -> b p r s", r=HP)[a.n(), :, :, k * CT * P:(k + 1) * CT * P]).then_inc(s_o[k], 16)

            def load_x(a):
                e.dma_start(xn[a.u][:, :, :], scr["xn"][a.n(), :, :].rearrange("(t p) d -> p t d", p=P)).then_inc(s_ld[a.u], 16)
                e.dma_start(x[a.u][:, :, :], io["x"][a.n(), :, :].rearrange("(t p) d -> p t d", p=P)).then_inc(s_ld[a.u], 16)

            def store(a):
                e.wait_ge(s_res, a.n(TB, TB + 2))
                e.dma_start(io["out"][a.n(), :, :].rearrange("(t p) d -> p t d", p=P), res[a.u][:, :, :]).then_inc(s_st[a.u], 16)

            def batch(a, more, after):
                if more:
                    e.wait_ge(s_ol, a.n(TB, 2 * CT))
                    load_o(a.next(1), 1)
                if after:
                    e.wait_ge(s_ol, a.n(TB, 3 * CT))
                    load_o(a.next(2), 0)
                store(a)
                if after:
                    load_x(a.next(2))

            e.dma_start(wraw[:, :, :], io["woT"].rearrange("(r p) d -> p r d", p=P)).then_inc(s_wo, 16)
            for u in range(2):
                e.sem_inc(s_st[u], 16)
                load_o(At(0, 0), u)
                if u == 0:
                    load_x(At(0, 0))
            e.wait_ge(s_g[0], 32)
            load_x(At(0, 1))
            e.wait_ge(s_ol, CT)
            load_o(At(0, 1), 0)
            with e.Fori(0, NBATCH // 2 - 1) as it:
                for u in range(2):
                    batch(At(it, u), True, True)
            batch(At(0, NBATCH - 2), True, False)
            batch(At(0, NBATCH - 1), False, False)
            for u in range(2):
                e.wait_ge(s_st[u], 16 * (NBATCH // 2 + 1))

        @blk.gpsimd
        def _(e):
            def gather(b, t, first):
                k = t % NG
                if not first:
                    wait_apart(e, s_mix, b * (2 * TB) + 2 * (t - NG + 1), s_apart)
                e.tensor_copy(idx[k][:, :], keep["read"][:, b * TB + t, :]).then_inc(s_idx, 1)
                wait_apart(e, s_idx, b * TB + (t + 1), s_apart)
                for j in range(2):
                    e.indirect_dma_start(out=eo[k][j][:, :], out_offset=None, in_=scr["eo"],
                                         in_offset=bass.IndirectOffsetOnAxis(ap=idx[k][:, j:j + 1], axis=0)).then_inc(s_g[k], 16)

            for t in range(TB):
                gather(0, t, t < NG)
            with e.Fori(1, NBATCH) as b:
                for t in range(TB):
                    gather(b, t, False)

        @blk.vector
        def _(e):
            def low(a, q):
                src, hi, lo = piece(q)
                e.wait_ge(s_oh, a.n(TB, q + 1))
                e.tensor_tensor(out=lo, in0=src, in1=hi.bitcast(F32), op=ALU.subtract).then_inc(s_ol, 1)

            def tile(a, t, back, ahead):
                u, k = a.u, t % 2
                e.wait_ge(s_res, a.n(TB, t + 1))
                e.wait_ge(s_pj, a.n(TB, t + 1))
                e.tensor_tensor(out=att[k][:, :], in0=pj[k][:, 0:D], in1=xn[u][:, t, :], op=ALU.add).then_inc(s_att, 1)
                e.wait_ge(s_g[t % NG], a.n(32, 32))
                e.scalar_tensor_tensor(out=mix[k][:, :], in0=eo[t % NG][0][:, :], scalar=g2[:, t, 0:1], in1=xn[u][:, t, :], op0=ALU.mult, op1=ALU.add).then_inc(s_mix, 1)
                if back:
                    gated(*back)
                e.wait_ge(s_mix, a.n(2 * TB, 2 * t + 1))
                e.scalar_tensor_tensor(out=mix[k][:, :], in0=eo[t % NG][1][:, :], scalar=g2[:, t, 1:2], in1=mix[k][:, :], op0=ALU.mult, op1=ALU.add).then_inc(s_mix, 1)
                if back:
                    residual(*back)
                if ahead:
                    low(*ahead)

            def gated(a, t):
                e.wait_ge(s_silu, a.n(TB, t + 1))
                e.wait_ge(s_att, a.n(TB, t + 1))
                e.tensor_tensor(out=att[t % 2][:, :], in0=att[t % 2][:, :], in1=gate[t % 2][:, :], op=ALU.mult).then_inc(s_mul, 1)

            def residual(a, t):
                e.wait_ge(s_mul, a.n(TB, t + 1))
                e.tensor_tensor(out=res[a.u][:, t, :], in0=att[t % 2][:, :], in1=x[a.u][:, t, :], op=ALU.add).then_inc(s_res, 1)

            def batch(a, back, more):
                e.wait_ge(s_ld[a.u], a.same(32, 32))
                e.wait_ge(s_st[a.u], a.same(16, 16))
                if back:
                    e.wait_ge(s_mix, a.n(2 * TB, 0))
                e.tensor_copy(g2[:, :, :], keep["gate"][:, bass.ds(a.n(TB), TB), :]).then_inc(s_g2, 1)
                e.wait_ge(s_g2, a.n(1, 1))
                for t in range(TB):
                    q = t + LEAD
                    tile(a, t, (a, t - 1) if t else back, (a, q) if q < TB else (a.next(1), q - TB) if more else None)

            e.sem_inc(s_res, 2)
            e.wait_ge(s_wh, 1)
            e.tensor_tensor(out=wo[1][:, :, :], in0=wraw[:, :, :], in1=wo[0][:, :, :].bitcast(F32), op=ALU.subtract).then_inc(s_wl, 1)
            for q in range(LEAD):
                low(At(0, 0), q)
            batch(At(0, 0), None, True)
            with e.Fori(0, NBATCH // 2 - 1) as it:
                for off in (1, 2):
                    batch(At(it, off), (At(it, off - 1), TB - 1), True)
            last = At(0, NBATCH - 1)
            batch(last, (last.next(-1), TB - 1), False)
            gated(last, TB - 1)
            residual(last, TB - 1)

        @blk.scalar
        def _(e):
            def high(a, q):
                if q % CT == 0:
                    e.wait_ge(s_o[q // CT], a.n(16, 16))
                if q % 2 == 0:
                    wait(e, s_pj, a.n(TB, q + 2 - TB))
                src, hi, _ = piece(q)
                e.activation(hi, src, ACT.Copy).then_inc(s_oh, 1)

            def batch(a, more):
                for t in range(TB):
                    q = t + LEAD
                    if q < TB:
                        high(a, q)
                    elif more:
                        high(a.next(1), q - TB)
                    e.wait_ge(s_mix, a.n(2 * TB, 2 * (t + 1)))
                    e.activation(gate[t % 2][:, :], mix[t % 2][:, :], ACT.Silu).then_inc(s_silu, 1)

            e.wait_ge(s_wo, 16)
            e.activation(wo[0][:, :, :], wraw[:, :, :], ACT.Copy).then_inc(s_wh, 1)
            for q in range(LEAD):
                high(At(0, 0), q)
            batch(At(0, 0), True)
            with e.Fori(0, NBATCH // 2 - 1) as it:
                for off in (1, 2):
                    batch(At(it, off), True)
            batch(At(0, NBATCH - 1), False)

        @blk.tensor
        def _(e):
            e.wait_ge(s_wl, 1)

            def tile(a, t, first):
                w, cols = t // CT, slice(t % CT * P, (t % CT + 1) * P)
                if t % 2 == 0:
                    e.wait_ge(s_ol, a.n(TB, t + 2))
                if not first:
                    e.wait_ge(s_att, a.n(TB, t - 1))
                for r in range(HP):
                    for os, ws in PASSES:
                        mm = e.matmul(pj[t % 2][:, 0:D], oT[w][os][:, r, cols], wo[ws][:, r, :],
                                      start=(os + ws + r == 0), stop=(os == 1 and r == HP - 1))
                mm.then_inc(s_pj, 1)

            for u in range(2):
                for t in range(TB):
                    tile(At(0, u), t, u == 0 and t < 2)
            with e.Fori(1, NBATCH // 2) as it:
                for u in range(2):
                    for t in range(TB):
                        tile(At(it, u), t, False)


def build(nc, io):
    with ExitStack() as ctx:
        def scratch(name, shape, dt=F32):
            return nc.dram_tensor(f"scr_{name}", shape, dt, kind="Internal").ap()

        scr = {
            "xn": scratch("xn", [NBATCH, S, D]),
            "c": scratch("c", [NBATCH, 2, DL, S]),
            "v": scratch("v", [NBATCH, HP, P, KT, P]),
            "o": scratch("o", [NPAIR, P, S]),
            "rec": scratch("rec", [NPAIR, 2, S]),
            "table": scratch("table", [NSLOT, 1], I32),
            "eo": scratch("eo", [NSLOT, D]),
        }

        def sb(name, shape, dt=F32):
            return ctx.enter_context(nc.sbuf_tensor(f"keep_{name}", shape, dt))

        keep = {
            "ident": sb("ident", [P, P]),
            "logits": sb("logits", [P, NT * NE]),
            "tok": sb("tok", [P, NT], I32),
            "gate": sb("gate", [P, NT, 2]),
            "fill": sb("fill", [P, NT, 2], I32),
            "read": sb("read", [P, NT, 2], I32),
        }
        project_phase(nc, io, scr, keep)
        route_phase(nc, io, scr, keep)
        attend_phase(nc, io, scr, keep)
        experts_phase(nc, io, scr, keep)
        combine_phase(nc, io, scr, keep)


def shape_constants():
    inv_freq = 1.0 / 10000.0 ** (np.arange(0, DH, 2, dtype=np.float32) / DH)
    freqs = np.outer(np.arange(S, dtype=np.float32), inv_freq).astype(np.float32)
    cos = np.concatenate([np.cos(freqs), np.cos(freqs)], -1)[:, ::2].astype(np.float32)
    sin = np.concatenate([np.sin(freqs), np.sin(freqs)], -1)[:, ::2].astype(np.float32)
    dim = np.arange(P) % DH
    e = np.tile(np.arange(NE, dtype=np.float32), NT)
    return {
        "cos": np.ascontiguousarray(cos.T[dim // 2]),
        "sin": np.ascontiguousarray(sin.T[dim // 2] * np.where(dim % 2 == 0, -1.0, 1.0).astype(np.float32)[:, None]),
        "ident": np.eye(P, dtype=np.float32),
        "tri": np.triu(np.ones((P, P), np.float32), 1),
        "rev": np.broadcast_to(NE - e, (P, NT * NE)).copy(),
        "ebase": np.broadcast_to(e * CAPP, (P, NT * NE)).copy(),
        "newe": np.broadcast_to((np.arange(NT * NE) % NT != 0).astype(np.float32), (P, NT * NE)).copy(),
        "tok": (np.arange(NT)[None, :] * P + np.arange(P)[:, None]).astype(np.int32),
    }


def kernel(**inputs):
    import concourse.bacc as bacc
    from concourse.bass_utils import run_bass_kernel_spmd

    a = {k: np.asarray(v) for k, v in inputs.items()}

    def pairs(w):
        return w.reshape(HP, P, DL).transpose(0, 2, 1)

    wq, wk = pairs(a["L0_attn_w_up_q"]), pairs(a["L0_attn_w_up_k"])
    arrays = {
        "x": a["L0_attn_x"],
        "wdqT": a["L0_attn_w_down_q"].T,
        "wdkvT": a["L0_attn_w_down_kv"].T,
        "wqk": np.stack([wq, wk], axis=2),
        "wvT": a["L0_attn_w_up_v"].T,
        "woT": a["L0_attn_w_out"].T,
        "lnp": np.stack([a["L0_attn_ln_scale"].reshape(KD, P).T, a["L0_attn_ln_bias"].reshape(KD, P).T], axis=2),
        "rwT": a["L0_ffn_router_w"].T,
        "w1": a["L0_ffn_w1"],
        "w2": a["L0_ffn_w2"],
        **shape_constants(),
    }
    arrays = {k: np.ascontiguousarray(v) for k, v in arrays.items()}
    nc = bacc.Bacc("TRN2", target_bir_lowering=False, num_devices=1)
    io = {k: nc.dram_tensor(f"in_{k}", v.shape, mybir.dt.from_np(v.dtype), kind="ExternalInput").ap() for k, v in arrays.items()}
    io["out"] = nc.dram_tensor("out_0", [NBATCH, S, D], F32, kind="ExternalOutput").ap()
    build(nc, io)
    r = run_bass_kernel_spmd(nc, [{f"in_{k}": v for k, v in arrays.items()}], core_ids=[0])
    return r.results[0]["out_0"]
```
